# Optimizing a Trainium2 kernel written in Bass

```python
import numpy as np
import jax
import jax.numpy as jnp

def _softmax(x, axis=-1):
    return jax.nn.softmax(x, axis=axis)

def _gelu(x):
    return jax.nn.gelu(x, approximate=True)

def _silu(x):
    return jax.nn.silu(x)

def _sigmoid(x):
    return jax.nn.sigmoid(x)

def _layernorm(x, axis=-1, eps=1e-05):
    m = jnp.mean(x, axis=axis, keepdims=True)
    v = jnp.var(x, axis=axis, keepdims=True)
    return (x - m) / jnp.sqrt(v + eps)

def _scatter_add(tgt, idx, src, axis=0):
    return tgt.at[idx].add(src)

def _segment_sum(src, seg, n):
    return jax.ops.segment_sum(src, seg, n)
kernel_name = 'mk_decoder_preln_d1_seqx_r4_05b178'

def setup_inputs(seed: int=0):
    np.random.seed(seed)
    _w = jnp.asarray

    def _rec_inputs():
        import jax
        import jax.numpy as jnp
        _rk = jax.random.key(seed)
        x = 0.000341 + 1 * jax.random.normal(jax.random.fold_in(_rk, 1), (8, 256, 512), jnp.float32)
        _lenS = 256 - jax.random.randint(jax.random.fold_in(_rk, 7), (8,), 0, max(1, 256 // 4) + 1, jnp.int32)
        _lenS2 = 256 - jax.random.randint(jax.random.fold_in(_rk, 8), (8,), 0, max(1, 256 // 4) + 1, jnp.int32)
        _ctx_2048P = jax.random.normal(jax.random.fold_in(_rk, 11), (8, 16, 512), jnp.float32)
        _ctx_2048c = jax.random.dirichlet(jax.random.fold_in(_rk, 511), 0.3 * jnp.ones((16,), jnp.float32), (8, 256))
        _ctx_2048t = jnp.einsum('bsk,bkd->bsd', _ctx_2048c, _ctx_2048P)
        _ctx_2048t = _ctx_2048t * jax.lax.rsqrt(jnp.mean(jnp.square(_ctx_2048t)) + 1e-12) * 0.953939
        ctx_2048 = -1.47943e-05 + 1.00017 * (_ctx_2048t + 0.3 * jax.random.normal(jax.random.fold_in(_rk, 611), (8, 256, 512), jnp.float32))
        return (x, ctx_2048)
    x, ctx_2048 = _rec_inputs()

    def _L0_attn_setup():
        import jax, jax.numpy as jnp
        import numpy as np
        EPS = 1e-05
        H = 16

        def rms(x, w=None):
            y = x * jax.lax.rsqrt(jnp.mean(jnp.square(x), axis=-1, keepdims=True) + EPS)
            return y * w if w is not None else y

        def rotate_every_two(x):
            x1 = x[..., ::2]
            x2 = x[..., 1::2]
            return jnp.stack([-x2, x1], axis=-1).reshape(x.shape)

        def theta_shift(x, sin, cos):
            return x * cos + rotate_every_two(x) * sin

        def retnet_rel_pos(S, Dh):
            angle = 1.0 / 10000.0 ** jnp.linspace(0.0, 1.0, Dh // 2)
            angle = jnp.repeat(angle, 2)
            idx = jnp.arange(S, dtype=jnp.float32)
            sin = jnp.sin(idx[:, None] * angle[None, :])
            cos = jnp.cos(idx[:, None] * angle[None, :])
            decay = jnp.log(1.0 - 2.0 ** (-5.0 - jnp.arange(H, dtype=jnp.float32)))
            i = jnp.arange(S)[:, None]
            j = jnp.arange(S)[None, :]
            expnt = jnp.where(i >= j, (i - j).astype(jnp.float32)[None, :, :] * decay[:, None, None], -jnp.inf)
            mask = jnp.exp(expnt)
            mask = jnp.nan_to_num(mask)
            mask = mask / jnp.sqrt(jnp.sum(mask, axis=-1, keepdims=True))
            return (sin, cos, mask)
        key = jax.random.key(seed)
        B, S, E, F = (4, 256, 512, 2048)
        ks = jax.random.split(key, 12)
        sE = 1.0 / np.sqrt(E)
        sF = 1.0 / np.sqrt(F)
        return {'x': jax.random.normal(ks[0], (B, S, E), jnp.float32), 'q_w': jax.random.normal(ks[1], (E, E), jnp.float32) * sE, 'k_w': jax.random.normal(ks[2], (E, E), jnp.float32) * sE, 'v_w': jax.random.normal(ks[3], (E, E), jnp.float32) * sE, 'g_w': jax.random.normal(ks[4], (E, E), jnp.float32) * sE, 'out_w': jax.random.normal(ks[5], (E, E), jnp.float32) * sE, 'fc1_w': jax.random.normal(ks[6], (E, F), jnp.float32) * sE, 'fc1_b': jnp.zeros((F,), jnp.float32), 'fc2_w': jax.random.normal(ks[7], (F, E), jnp.float32) * sF, 'fc2_b': jnp.zeros((E,), jnp.float32), 'retn_norm_w': jnp.ones((E,), jnp.float32), 'final_norm_w': jnp.ones((E,), jnp.float32)}
    _L0_attn_all = _L0_attn_setup()
    _L0_attn_in = {k: v for k, v in _L0_attn_all.items() if k in ('q_w', 'k_w', 'v_w', 'g_w', 'out_w', 'fc1_w', 'fc1_b', 'fc2_w', 'fc2_b', 'retn_norm_w', 'final_norm_w')}
    del _L0_attn_all

    def _L0_xattn_setup():
        import jax, jax.numpy as jnp
        import numpy as np

        def _wkv(time_decay, time_first, k, v):
            w = -jnp.exp(time_decay)
            u = time_first
            B, T, C = k.shape
            aa = jnp.zeros((B, C), dtype=k.dtype)
            bb = jnp.zeros((B, C), dtype=k.dtype)
            pp = jnp.full((B, C), -1e+38, dtype=k.dtype)

            def step(carry, kv_t):
                aa, bb, pp = carry
                kt, vt = kv_t
                ww = u + kt
                q = jnp.maximum(pp, ww)
                e1 = jnp.exp(pp - q)
                e2 = jnp.exp(ww - q)
                y_t = (e1 * aa + e2 * vt) / (e1 * bb + e2)
                ww2 = pp + w
                q2 = jnp.maximum(ww2, kt)
                e1b = jnp.exp(ww2 - q2)
                e2b = jnp.exp(kt - q2)
                new_carry = (e1b * aa + e2b * vt, e1b * bb + e2b, q2)
                return (new_carry, y_t)
            ks = jnp.transpose(k, (1, 0, 2))
            vs = jnp.transpose(v, (1, 0, 2))
            _, ys = jax.lax.scan(step, (aa, bb, pp), (ks, vs))
            return jnp.transpose(ys, (1, 0, 2))
        key = jax.random.key(seed)
        k1, k2, k3, k4 = jax.random.split(key, 4)
        B, T, C = (8, 256, 512)
        return {'batch_size': B, 'seq_len': T, 'embedding_dim': C, 'time_decay': jax.random.normal(k1, (C,), dtype=jnp.float32), 'time_first': jax.random.normal(k2, (C,), dtype=jnp.float32), 'k': jax.random.normal(k3, (B, T, C), dtype=jnp.float32), 'v': jax.random.normal(k4, (B, T, C), dtype=jnp.float32)}
    _L0_xattn_all = _L0_xattn_setup()
    _L0_xattn_in = {k: v for k, v in _L0_xattn_all.items() if k in ('time_decay', 'time_first')}
    del _L0_xattn_all

    def _L0_ffn_setup():
        import jax, jax.numpy as jnp
        import numpy as np
        from jax import lax
        TOP_K = 4
        ROUTED_SCALING = 1.0
        RENORMALIZE = True

        def _swiglu_ffn(x, wg, wu, wd):
            return jax.nn.silu(x @ wg.T) * (x @ wu.T) @ wd.T
        key = jax.random.key(seed)
        ks = jax.random.split(key, 9)
        H, I, E = (512, 256, 16)
        s = 0.02
        return {'hidden_states': jax.random.normal(ks[0], (2, 256, H), jnp.float32), 'gate_w': jax.random.normal(ks[1], (E, H), jnp.float32) * s, 'expert_bias': jax.random.normal(ks[2], (E,), jnp.float32) * s, 'w_gate': jax.random.normal(ks[3], (E, I, H), jnp.float32) * s, 'w_up': jax.random.normal(ks[4], (E, I, H), jnp.float32) * s, 'w_down': jax.random.normal(ks[5], (E, H, I), jnp.float32) * s, 'sw_gate': jax.random.normal(ks[6], (I, H), jnp.float32) * s, 'sw_up': jax.random.normal(ks[7], (I, H), jnp.float32) * s, 'sw_down': jax.random.normal(ks[8], (H, I), jnp.float32) * s}
    _L0_ffn_all = _L0_ffn_setup()
    _L0_ffn_in = {k: v for k, v in _L0_ffn_all.items() if k in ('gate_w', 'expert_bias', 'w_gate', 'w_up', 'w_down', 'sw_gate', 'sw_up', 'sw_down')}
    del _L0_ffn_all
    return {'x': x, 'ctx_2048': ctx_2048, 'L0_attn_q_w': _L0_attn_in['q_w'], 'L0_attn_k_w': _L0_attn_in['k_w'], 'L0_attn_v_w': _L0_attn_in['v_w'], 'L0_attn_g_w': _L0_attn_in['g_w'], 'L0_attn_out_w': _L0_attn_in['out_w'], 'L0_attn_fc1_w': _L0_attn_in['fc1_w'], 'L0_attn_fc1_b': _L0_attn_in['fc1_b'], 'L0_attn_fc2_w': _L0_attn_in['fc2_w'], 'L0_attn_fc2_b': _L0_attn_in['fc2_b'], 'L0_attn_retn_norm_w': _L0_attn_in['retn_norm_w'], 'L0_attn_final_norm_w': _L0_attn_in['final_norm_w'], 'L0_xattn_time_decay': _L0_xattn_in['time_decay'], 'L0_xattn_time_first': _L0_xattn_in['time_first'], 'L0_ffn_gate_w': _L0_ffn_in['gate_w'], 'L0_ffn_expert_bias': _L0_ffn_in['expert_bias'], 'L0_ffn_w_gate': _L0_ffn_in['w_gate'], 'L0_ffn_w_up': _L0_ffn_in['w_up'], 'L0_ffn_w_down': _L0_ffn_in['w_down'], 'L0_ffn_sw_gate': _L0_ffn_in['sw_gate'], 'L0_ffn_sw_up': _L0_ffn_in['sw_up'], 'L0_ffn_sw_down': _L0_ffn_in['sw_down']}

def reference(x, ctx_2048, L0_attn_q_w, L0_attn_k_w, L0_attn_v_w, L0_attn_g_w, L0_attn_out_w, L0_attn_fc1_w, L0_attn_fc1_b, L0_attn_fc2_w, L0_attn_fc2_b, L0_attn_retn_norm_w, L0_attn_final_norm_w, L0_xattn_time_decay, L0_xattn_time_first, L0_ffn_gate_w, L0_ffn_expert_bias, L0_ffn_w_gate, L0_ffn_w_up, L0_ffn_w_down, L0_ffn_sw_gate, L0_ffn_sw_up, L0_ffn_sw_down):
    import jax
    import jax.numpy as jnp

    def _L0_attn_ref(x, q_w, k_w, v_w, g_w, out_w, fc1_w, fc1_b, fc2_w, fc2_b, retn_norm_w, final_norm_w):
        import jax, jax.numpy as jnp
        import numpy as np
        EPS = 1e-05
        H = 16

        def rms(x, w=None):
            y = x * jax.lax.rsqrt(jnp.mean(jnp.square(x), axis=-1, keepdims=True) + EPS)
            return y * w if w is not None else y

        def rotate_every_two(x):
            x1 = x[..., ::2]
            x2 = x[..., 1::2]
            return jnp.stack([-x2, x1], axis=-1).reshape(x.shape)

        def theta_shift(x, sin, cos):
            return x * cos + rotate_every_two(x) * sin

        def retnet_rel_pos(S, Dh):
            angle = 1.0 / 10000.0 ** jnp.linspace(0.0, 1.0, Dh // 2)
            angle = jnp.repeat(angle, 2)
            idx = jnp.arange(S, dtype=jnp.float32)
            sin = jnp.sin(idx[:, None] * angle[None, :])
            cos = jnp.cos(idx[:, None] * angle[None, :])
            decay = jnp.log(1.0 - 2.0 ** (-5.0 - jnp.arange(H, dtype=jnp.float32)))
            i = jnp.arange(S)[:, None]
            j = jnp.arange(S)[None, :]
            expnt = jnp.where(i >= j, (i - j).astype(jnp.float32)[None, :, :] * decay[:, None, None], -jnp.inf)
            mask = jnp.exp(expnt)
            mask = jnp.nan_to_num(mask)
            mask = mask / jnp.sqrt(jnp.sum(mask, axis=-1, keepdims=True))
            return (sin, cos, mask)
        B, S, E = x.shape
        Dh = E // H
        scaling = Dh ** (-0.5)
        sin, cos, mask = retnet_rel_pos(S, Dh)
        residual = x
        h = rms(x, retn_norm_w)
        q = h @ q_w
        k = h @ k_w * scaling
        v = h @ v_w
        g = h @ g_w

        def split_heads(t):
            return t.reshape(B, S, H, Dh).transpose(0, 2, 1, 3)
        q, k, v_h = (split_heads(q), split_heads(k), split_heads(v))
        qr = theta_shift(q, sin, cos)
        kr = theta_shift(k, sin, cos)
        qk = jnp.einsum('bhsd,bhtd->bhst', qr, kr) * mask
        denom = jnp.clip(jnp.abs(jax.lax.stop_gradient(jnp.sum(qk, axis=-1, keepdims=True))), 1.0, None)
        qk = qk / denom
        o = jnp.einsum('bhst,bhtd->bhsd', qk, v_h)
        o = o.transpose(0, 2, 1, 3)
        o = rms(o)
        o = o.reshape(B, S, E)
        o = jax.nn.silu(g) * o
        o = o @ out_w
        x = residual + o
        residual = x
        h = rms(x, final_norm_w)
        h = jax.nn.gelu(h @ fc1_w + fc1_b)
        h = h @ fc2_w + fc2_b
        return residual + h

    def _L0_xattn_ref(batch_size, seq_len, embedding_dim, time_decay, time_first, k, v):
        import jax, jax.numpy as jnp
        import numpy as np

        def _wkv(time_decay, time_first, k, v):
            w = -jnp.exp(time_decay)
            u = time_first
            B, T, C = k.shape
            aa = jnp.zeros((B, C), dtype=k.dtype)
            bb = jnp.zeros((B, C), dtype=k.dtype)
            pp = jnp.full((B, C), -1e+38, dtype=k.dtype)

            def step(carry, kv_t):
                aa, bb, pp = carry
                kt, vt = kv_t
                ww = u + kt
                q = jnp.maximum(pp, ww)
                e1 = jnp.exp(pp - q)
                e2 = jnp.exp(ww - q)
                y_t = (e1 * aa + e2 * vt) / (e1 * bb + e2)
                ww2 = pp + w
                q2 = jnp.maximum(ww2, kt)
                e1b = jnp.exp(ww2 - q2)
                e2b = jnp.exp(kt - q2)
                new_carry = (e1b * aa + e2b * vt, e1b * bb + e2b, q2)
                return (new_carry, y_t)
            ks = jnp.transpose(k, (1, 0, 2))
            vs = jnp.transpose(v, (1, 0, 2))
            _, ys = jax.lax.scan(step, (aa, bb, pp), (ks, vs))
            return jnp.transpose(ys, (1, 0, 2))
        assert seq_len <= 256
        return _wkv(time_decay, time_first, k, v)

    def _L0_ffn_ref(hidden_states, gate_w, expert_bias, w_gate, w_up, w_down, sw_gate, sw_up, sw_down):
        import jax, jax.numpy as jnp
        import numpy as np
        from jax import lax
        TOP_K = 4
        ROUTED_SCALING = 1.0
        RENORMALIZE = True

        def _swiglu_ffn(x, wg, wu, wd):
            return jax.nn.silu(x @ wg.T) * (x @ wu.T) @ wd.T
        orig_shape = hidden_states.shape
        H = orig_shape[-1]
        x = hidden_states.reshape(-1, H)
        T = x.shape[0]
        logits = x.astype(jnp.float32) @ gate_w.T
        scores = jax.nn.sigmoid(logits)
        _, topk_idx = lax.top_k(scores + expert_bias[None, :], TOP_K)
        topk_w = jnp.take_along_axis(scores, topk_idx, axis=-1)
        if RENORMALIZE:
            topk_w = topk_w / jnp.sum(topk_w, axis=-1, keepdims=True)
        topk_w = topk_w * ROUTED_SCALING
        E = gate_w.shape[0]
        combine = jnp.zeros((T, E), dtype=x.dtype).at[jnp.arange(T)[:, None], topk_idx].set(topk_w.astype(x.dtype))

        def step(acc, ws):
            wg, wu, wd, cw = ws
            return (acc + cw[:, None] * _swiglu_ffn(x, wg, wu, wd), None)
        routed, _ = lax.scan(step, jnp.zeros_like(x), (w_gate, w_up, w_down, combine.T))
        shared = _swiglu_ffn(x, sw_gate, sw_up, sw_down)
        return (routed + shared).reshape(orig_shape)
    x = x + _L0_attn_ref(_layernorm(x, axis=-1), L0_attn_q_w, L0_attn_k_w, L0_attn_v_w, L0_attn_g_w, L0_attn_out_w, L0_attn_fc1_w, L0_attn_fc1_b, L0_attn_fc2_w, L0_attn_fc2_b, L0_attn_retn_norm_w, L0_attn_final_norm_w)
    x = x + _L0_xattn_ref(8, 256, 512, L0_xattn_time_decay, L0_xattn_time_first, _layernorm(x, axis=-1), ctx_2048)
    x = x + _L0_ffn_ref(_layernorm(x, axis=-1), L0_ffn_gate_w, L0_ffn_expert_bias, L0_ffn_w_gate, L0_ffn_w_up, L0_ffn_w_down, L0_ffn_sw_gate, L0_ffn_sw_up, L0_ffn_sw_down)
    return x

_drawn_inputs = setup_inputs


def setup_inputs(seed=0):
    import zlib

    import numpy as np

    out = dict(_drawn_inputs(seed))
    spreads = {'L0_attn_fc1_b': (0.0, 0.291),
     'L0_attn_fc2_b': (0.0, 0.1),
     'L0_attn_retn_norm_w': (1.0, 0.2),
     'L0_attn_final_norm_w': (1.0, 0.2)}
    factors = {'L0_ffn_gate_w': 8.0,
     'L0_ffn_expert_bias': 8.0,
     'L0_ffn_w_gate': 7.722,
     'L0_ffn_w_up': 7.543,
     'L0_ffn_w_down': 7.55,
     'L0_ffn_sw_gate': 3.843,
     'L0_ffn_sw_up': 3.791,
     'L0_ffn_sw_down': 3.764}
    for name, (base, spread) in spreads.items():
        noise = np.random.default_rng([zlib.crc32(name.encode()), seed]).standard_normal(out[name].shape)
        drawn = base * np.exp(spread * noise) if base else spread * noise
        out[name] = jnp.asarray(drawn.astype(out[name].dtype))
    for name, factor in factors.items():
        out[name] = (out[name] * factor).astype(out[name].dtype)
    return out
```

```python
from contextlib import ExitStack

import numpy as np

import concourse.bass as bass
from concourse import mybir

F32 = mybir.dt.float32
F32R = mybir.dt.float32r
ALU = mybir.AluOpType
ACT = mybir.ActivationFunctionType
AX_X = mybir.AxisListType.X

P = 128
B, S, D = 8, 256, 512
NT = B * S // P
ST = S // P
KC = D // P
H = 16
DH = D // H
HG = P // DH
HALF = H // 2
F = 2048
NE = 16
TOPK = 4
I = 256
IC = I // P
TB = 512
NB = B * S // TB
BT = TB // P
EPS = 1e-5
NEG = -1e38

PASSES = ((0, 0), (0, 1), (1, 0))


def bcast(ap, shape):
    return ap.to_broadcast(shape)


def attention_phase(nc, a, acc, ident):
    with ExitStack() as ctx:
        def sb(name, shape, dt=F32):
            return ctx.enter_context(nc.sbuf_tensor(name + "_sb", shape, dt))

        def sem(name):
            return ctx.enter_context(nc.semaphore(name))

        NW = 5
        whl = sb("attn_w_halves", [P, 2, NW, KC, D], F32R)
        scm = sb("scores_masked_sb", [P, HALF, 3 * P])
        wraw = scm[:, :, :].rearrange("p h n -> p (h n)")[:, 0:KC * D].rearrange("p (k n) -> p k n", k=KC)
        mask = sb("decay_mask", [P, H, 2, P])
        invn = sb("inv_mask_norm", [P, ST, H])
        cos = sb("cos_t", [P, ST, DH])
        sin = sb("sin_t", [P, ST, DH])
        rnw = sb("retn_w", [P, KC])
        xin = sb("xin", [P, ST, D])
        h = sb("h_rows", [P, ST, D])
        hT = sb("hT_halves", [P, 2, ST, KC, P], F32R)
        tcos = sb("rot_cos", [P, D])
        tsin = sb("rot_sin", [P, D])
        qk = sb("qk_rows", [P, 2, ST, D])
        qkT = sb("qk_cols", [P, 2, KC, S])
        v = sb("v_and_ones", [P, ST, H, DH + 1])
        gate = sb("gate_rows", [P, ST, D])
        o = sb("o_and_denom", [P, ST, H, DH + 1])
        on = sb("o_normed", [P, ST, D])
        oT = sb("oT_halves", [P, 2, ST, KC, P], F32R)
        st6 = sb("bn6", [P, ST, 6])
        mv = sb("mean_var", [P, ST, 2])
        lnc = sb("ln_consts", [P, 4, ST])
        mhalf = sb("minus_half", [P, ST * H])
        eps = sb("eps_t", [P, ST * H])
        inv_dh = sb("inv_dh", [P, ST * H])
        sm = sb("norm_small", [P, 6, ST, H])

        xps = ctx.enter_context(nc.psum_tensor("x_ps", [P, 2, 512], F32))
        yps = ctx.enter_context(nc.psum_tensor("y_ps", [P, 2, 512], F32))
        pps = ctx.enter_context(nc.psum_tensor("proj_ps", [P, 4, 512], F32))

        const_loaded = sem("a_const_loaded")
        w_loaded = sem("a_w_loaded")
        w_scaled = sem("a_w_scaled")
        w_hi = sem("a_w_hi")
        w_lo = sem("a_w_lo")
        ones_set = sem("a_ones_set")
        half_set = sem("a_half_set")
        x_loaded = sem("a_x_loaded")
        bn_made = sem("a_bn_made")
        bn_passed = sem("a_bn_passed")
        stats_made = sem("a_stats_made")
        ln_step = sem("a_ln_step")
        h_made = sem("a_h_made")
        hT_up = sem("a_hT_up")
        hT_hi = sem("a_hT_hi")
        hT_lo = sem("a_hT_lo")
        proj_up = sem("a_proj_up")
        rot_read = sem("a_rot_read")
        qk_rotated = sem("a_qk_rotated")
        v_copied = sem("a_v_copied")
        g_made = sem("a_g_made")
        qkT_up = sem("a_qkT_up")
        qkT_copied = sem("a_qkT_copied")
        scores_up = sem("a_scores_up")
        scores_masked = sem("a_scores_masked")
        o_up = sem("a_o_up")
        o_copied = sem("a_o_copied")
        o_squared = sem("a_o_squared")
        nv = sem("a_norm_dve")
        ng = sem("a_norm_pool")
        on_gated = sem("a_on_gated")
        oT_up = sem("a_oT_up")
        oT_hi = sem("a_oT_hi")
        oT_lo = sem("a_oT_lo")
        out_up = sem("a_out_up")
        r_added = sem("a_r_added")

        NV, NG, LN = 7, 6, 7
        xd = a["x"].rearrange("(b s p) d -> b p s d", p=P, s=ST)

        with nc.Block() as block:
            @block.sync
            def _(sp):
                sp.dma_start(rnw[:, :], a["retn_w"]).then_inc(const_loaded, 16)
                sp.dma_start(xin[:, :, :], xd[0]).then_inc(x_loaded, 16)
                for n in range(NW):
                    if n:
                        sp.wait_ge(w_lo, n)
                    sp.dma_start(wraw, a["attn_w"][n]).then_inc(w_loaded, 16)
                    if n == 0:
                        sp.wait_ge(const_loaded, 16)
                        sp.dma_start(ident[:, :], a["ident"]).then_inc(const_loaded, 16)
                        sp.wait_ge(const_loaded, 32)
                        sp.dma_start(cos[:, :, :], a["cos"]).then_inc(const_loaded, 16)
                        sp.wait_ge(const_loaded, 48)
                        sp.dma_start(sin[:, :, :], a["sin"]).then_inc(const_loaded, 16)
                        sp.wait_ge(const_loaded, 64)
                        sp.dma_start(invn[:, :, :], a["inv_norm"]).then_inc(const_loaded, 16)
                        sp.wait_ge(const_loaded, 80)
                        sp.dma_start(mask[:, :, :, :], a["mask"]).then_inc(const_loaded, 16)
                with sp.Fori(1, B) as b:
                    sp.wait_ge(h_made, b)
                    sp.dma_start(xin[:, :, :], xd[b]).then_inc(x_loaded, 16)

            @block.gpsimd
            def _(pool):
                pool.memset(v[:, :, :, DH:DH + 1], 1.0).then_inc(ones_set, 1)
                pool.memset(mhalf[:, :], -0.5).then_inc(half_set, 1)
                pool.memset(eps[:, :], EPS).then_inc(half_set, 1)
                pool.memset(inv_dh[:, :], 1.0 / DH).then_inc(half_set, 1)
                pool.wait_ge(half_set, 3)

                def heads(t):
                    return t[:, :].rearrange("p (s h) -> p s h", s=ST)

                def ln_scales(b):
                    var = mv[:, :, 1]
                    ve, rstd, t, s = (lnc[:, k, :] for k in range(4))
                    n = LN * b
                    pool.wait_ge(stats_made, ST * (b + 1))
                    if not (isinstance(b, int) and b == 0):
                        pool.wait_ge(h_made, b)
                    pool.tensor_tensor(ve, var, eps[:, 0:ST], ALU.add).then_inc(ln_step, 1)
                    pool.wait_ge(ln_step, n + 1)
                    pool.tensor_tensor(rstd, ve, mhalf[:, 0:ST], ALU.pow).then_inc(ln_step, 1)
                    pool.wait_ge(ln_step, n + 2)
                    pool.tensor_tensor(t, rstd, rstd, ALU.mult).then_inc(ln_step, 1)
                    pool.wait_ge(ln_step, n + 3)
                    pool.tensor_tensor(ve, t, var, ALU.mult).then_inc(ln_step, 1)
                    pool.wait_ge(ln_step, n + 4)
                    pool.tensor_tensor(t, ve, eps[:, 0:ST], ALU.add).then_inc(ln_step, 1)
                    pool.wait_ge(ln_step, n + 5)
                    pool.tensor_tensor(ve, t, mhalf[:, 0:ST], ALU.pow).then_inc(ln_step, 1)
                    pool.wait_ge(ln_step, n + 6)
                    pool.tensor_tensor(s, rstd, ve, ALU.mult).then_inc(ln_step, 1)

                def rotate(b, st, w):
                    n = 2 * ST * b + 2 * st + w
                    pool.wait_ge(rot_read, n + 1)
                    pool.wait_ge(qkT_up, 2 * ST * b)
                    pool.tensor_tensor(qk[:, w, st, :], tcos[:, :], tsin[:, :], ALU.add)\
                        .then_inc(qk_rotated, 1)

                def norm(b):
                    aa, ms, t, u, sc = (sm[:, k, :, :] for k in (1, 2, 3, 4, 5))
                    n = NG * b
                    pool.wait_ge(nv, NV * b + 6)
                    pool.tensor_tensor(t, aa, aa, ALU.mult).then_inc(ng, 1)
                    pool.wait_ge(ng, n + 1)
                    pool.tensor_tensor(u, t, ms, ALU.mult).then_inc(ng, 1)
                    pool.wait_ge(ng, n + 2)
                    pool.tensor_tensor(t, u, heads(inv_dh), ALU.mult).then_inc(ng, 1)
                    pool.wait_ge(ng, n + 3)
                    pool.tensor_tensor(u, t, heads(eps), ALU.add).then_inc(ng, 1)
                    pool.wait_ge(ng, n + 4)
                    pool.tensor_tensor(t, u, heads(mhalf), ALU.pow).then_inc(ng, 1)
                    pool.wait_ge(ng, n + 5)
                    pool.tensor_tensor(sc, t, aa, ALU.mult).then_inc(ng, 1)
                    pool.wait_ge(nv, NV * b + 7)
                    pool.wait_ge(g_made, ST * b + ST)
                    pool.tensor_tensor(on[:, :, :], on[:, :, :], gate[:, :, :], ALU.mult).then_inc(on_gated, 1)

                def turn(b, more):
                    if more:
                        ln_scales(b + 1)
                        rotate(b + 1, 0, 0)
                        rotate(b + 1, 0, 1)
                    norm(b)
                    if more:
                        rotate(b + 1, 1, 0)
                        rotate(b + 1, 1, 1)

                ln_scales(0)
                for st in range(ST):
                    rotate(0, st, 0)
                    rotate(0, st, 1)
                turn(0, True)
                with pool.Fori(1, B - 1) as b:
                    turn(b, True)
                turn(B - 1, False)

            @block.scalar
            def _(act):
                for n in range(NW):
                    act.wait_ge(w_loaded, 16 * (n + 1))
                    if n < NW - 1:
                        act.wait_ge(w_scaled, n + 1)
                    act.activation(whl[:, 0, n, :, :], wraw, ACT.Copy).then_inc(w_hi, 1)

                def hT_halves(b, st):
                    act.wait_ge(hT_up, ST * b + st + 1)
                    act.activation(hT[:, 0, st, :, :], xps[:, st, :].rearrange("p (k t) -> p k t", k=KC),
                                   ACT.Copy).then_inc(hT_hi, 1)

                def v_and_gate(b, st):
                    u = 4 * (ST * b + st)
                    act.wait_ge(proj_up, u + 3)
                    act.wait_ge(o_up, ST * b)
                    act.activation(v[:, st, :, 0:DH], pps[:, 2, :].rearrange("p (h d) -> p h d", h=H),
                                   ACT.Copy).then_inc(v_copied, 1)
                    act.wait_ge(proj_up, u + 4)
                    act.wait_ge(on_gated, b)
                    act.activation(gate[:, st, :], pps[:, 3, :], ACT.Silu).then_inc(g_made, 1)

                def turn(b, more):
                    for u in range(2 * ST):
                        w, st = u // ST, u % ST
                        act.wait_ge(qkT_up, 2 * ST * b + u + 1)
                        act.activation(qkT[:, w, :, st * P:(st + 1) * P],
                                       xps[:, u % 2, :].rearrange("p (k t) -> p k t", k=KC),
                                       ACT.Copy).then_inc(qkT_copied, 1)
                    if more:
                        hT_halves(b + 1, 0)
                    for half in range(2):
                        act.wait_ge(o_up, 2 * b + half + 1)
                        act.wait_ge(on_gated, b)
                        act.activation(o[:, :, half * HALF:(half + 1) * HALF, :],
                                       yps[:, :, 0:HALF * (DH + 1)].rearrange("p s (h d) -> p s h d", h=HALF),
                                       ACT.Copy).then_inc(o_copied, 1)
                    act.wait_ge(o_copied, 2 * b + 2)
                    act.wait_ge(oT_up, ST * b)
                    act.activation(on[:, :, :].rearrange("p s (h d) -> p (s h) d", h=H),
                                   o[:, :, :, 0:DH].rearrange("p s h d -> p (s h) d"),
                                   ACT.Square).then_inc(o_squared, 1)
                    if more:
                        v_and_gate(b + 1, 0)
                        hT_halves(b + 1, 1)
                        v_and_gate(b + 1, 1)
                    for st in range(ST):
                        act.wait_ge(oT_up, ST * b + st + 1)
                        act.activation(oT[:, 0, st, :, :], xps[:, st, :].rearrange("p (k t) -> p k t", k=KC),
                                       ACT.Copy).then_inc(oT_hi, 1)

                act.wait_ge(ones_set, 1)
                for st in range(ST):
                    hT_halves(0, st)
                    v_and_gate(0, st)
                turn(0, True)
                with act.Fori(1, B - 1) as b:
                    turn(b, True)
                turn(B - 1, False)

            @block.vector
            def _(dve):
                def ln_stats(b):
                    dve.wait_ge(x_loaded, 16 * (b + 1))
                    for st in range(ST):
                        dve.bn_stats(st6[:, st, :], xin[:, st, :]).then_inc(bn_made, 1)
                    dve.wait_ge(bn_made, ST * b + ST).then_inc(bn_passed, 1)
                    for st in range(ST):
                        dve.bn_aggr(mv[:, st, :], st6[:, st, :]).then_inc(stats_made, 1)

                def ln_rows(b):
                    dve.wait_ge(ln_step, LN * (b + 1))
                    dve.wait_ge(hT_up, ST * b)
                    for st in range(ST):
                        dve.tensor_scalar(acc[:, bass.ds(ST * b + st, 1), :].rearrange("p a d -> p (a d)"),
                                          xin[:, st, :], mv[:, st, 0:1], lnc[:, 1, st:st + 1],
                                          ALU.subtract, ALU.mult)
                        last = dve.tensor_scalar(h[:, st, :], xin[:, st, :], mv[:, st, 0:1],
                                                 lnc[:, 3, st:st + 1], ALU.subtract, ALU.mult)
                    last.then_inc(h_made, 1)

                def hT_rest(b, st):
                    dve.wait_ge(hT_hi, ST * b + st + 1)
                    dve.tensor_tensor(hT[:, 1, st, :, :], xps[:, st, :].rearrange("p (k t) -> p k t", k=KC),
                                      hT[:, 0, st, :, :].bitcast(F32), ALU.subtract).then_inc(hT_lo, 1)

                def rotate(b, st, w):
                    n = 2 * ST * b + 2 * st + w
                    dve.wait_ge(proj_up, 4 * (ST * b + st) + w + 1)
                    if not (isinstance(n, int) and n == 0):
                        dve.wait_ge(qk_rotated, n)
                    src = pps[:, w, :].rearrange("p (h d) -> p h d", h=H)
                    dve.tensor_tensor(tcos[:, :].rearrange("p (h d) -> p h d", h=H), src,
                                      bcast(cos[:, st:st + 1, :], [P, H, DH]), ALU.mult)
                    pair = pps[:, w, :].rearrange("p (h d t) -> p h d t", h=H, t=2)
                    swap = tsin[:, :].rearrange("p (h d t) -> p h d t", h=H, t=2)
                    sign = sin[:, st:st + 1, :].rearrange("p s (d t) -> p s d t", t=2)
                    for t in range(2):
                        last = dve.tensor_tensor(swap[:, :, :, t], pair[:, :, :, 1 - t],
                                                 bcast(sign[:, :, :, t], [P, H, DH // 2]), ALU.mult)
                    last.then_inc(rot_read, 1)

                def masks(b, half):
                    for j in range(HALF):
                        hh = half * HALF + j
                        dve.wait_ge(scores_up, H * b + hh + 1)
                        if j == 0:
                            dve.wait_ge(o_up, 2 * b + half)
                        x = hh % 2
                        dve.tensor_tensor(scm[:, j, 0:2 * P], xps[:, x, 0:2 * P],
                                          mask[:, hh, :, :].rearrange("p a t -> p (a t)"), ALU.mult)
                        dve.tensor_tensor(scm[:, j, 2 * P:3 * P], xps[:, x, 2 * P:3 * P],
                                          mask[:, hh, 0, :], ALU.mult).then_inc(scores_masked, 1)

                def norm(b):
                    den, aa, ms, t = (sm[:, k, :, :] for k in (0, 1, 2, 3))
                    n = NV * b
                    dve.wait_ge(o_copied, 2 * b + 2)
                    dve.wait_ge(ng, NG * b)
                    dve.tensor_tensor(den, o[:, :, :, DH], invn[:, :, :], ALU.mult).then_inc(nv, 1)
                    dve.wait_ge(nv, n + 1)
                    dve.scalar_tensor_tensor(out=t, in0=den, scalar=-1.0, in1=den,
                                             op0=ALU.mult, op1=ALU.max).then_inc(nv, 1)
                    dve.wait_ge(nv, n + 2)
                    dve.tensor_scalar(t, t, 1.0, None, ALU.max).then_inc(nv, 1)
                    dve.wait_ge(nv, n + 3)
                    dve.reciprocal(den, t).then_inc(nv, 1)
                    dve.wait_ge(nv, n + 4)
                    dve.tensor_tensor(aa, den, invn[:, :, :], ALU.mult).then_inc(nv, 1)
                    dve.wait_ge(o_squared, b + 1)
                    dve.wait_ge(nv, n + 5)
                    dve.tensor_reduce(ms, on[:, :, :].rearrange("p s (h d) -> p s h d", h=H), AX_X, ALU.add)\
                        .then_inc(nv, 1)
                    dve.wait_ge(ng, NG * b + NG)
                    dve.wait_ge(nv, n + 6)
                    dve.tensor_tensor(on[:, :, :].rearrange("p s (h d) -> p (s h) d", h=H),
                                      o[:, :, :, 0:DH].rearrange("p s h d -> p (s h) d"),
                                      bcast(sm[:, 5, :, :].rearrange("p s (h o) -> p (s h) o", o=1),
                                            [P, ST * H, DH]), ALU.mult).then_inc(nv, 1)

                def out_rows(b):
                    for st in range(ST):
                        dve.wait_ge(oT_hi, ST * b + st + 1)
                        dve.tensor_tensor(oT[:, 1, st, :, :], xps[:, st, :].rearrange("p (k t) -> p k t", k=KC),
                                          oT[:, 0, st, :, :].bitcast(F32), ALU.subtract).then_inc(oT_lo, 1)
                    for st in range(ST):
                        row = acc[:, bass.ds(ST * b + st, 1), :].rearrange("p a d -> p (a d)")
                        dve.wait_ge(out_up, ST * b + st + 1)
                        dve.wait_ge(h_made, b + 1)
                        dve.tensor_tensor(row, yps[:, st, :], row, ALU.add).then_inc(r_added, 1)

                def turn(b, more):
                    if more:
                        ln_stats(b + 1)
                    masks(b, 0)
                    if more:
                        ln_rows(b + 1)
                        hT_rest(b + 1, 0)
                        rotate(b + 1, 0, 0)
                    masks(b, 1)
                    if more:
                        rotate(b + 1, 0, 1)
                    norm(b)
                    if more:
                        hT_rest(b + 1, 1)
                        rotate(b + 1, 1, 0)
                        rotate(b + 1, 1, 1)
                    out_rows(b)

                ln_stats(0)
                dve.wait_ge(const_loaded, 16)
                for n in range(NW):
                    dve.wait_ge(w_loaded, 16 * (n + 1))
                    if n < NW - 1:
                        dve.tensor_tensor(wraw, wraw,
                                          bcast(rnw[:, :].rearrange("p (k o) -> p k o", o=1), [P, KC, D]),
                                          ALU.mult).then_inc(w_scaled, 1)
                    dve.wait_ge(w_hi, n + 1)
                    dve.tensor_tensor(whl[:, 1, n, :, :], wraw, whl[:, 0, n, :, :].bitcast(F32),
                                      ALU.subtract).then_inc(w_lo, 1)
                dve.wait_ge(const_loaded, 96)
                ln_rows(0)
                for st in range(ST):
                    hT_rest(0, st)
                    rotate(0, st, 0)
                    rotate(0, st, 1)
                turn(0, True)
                with dve.Fori(1, B - 1) as b:
                    turn(b, True)
                turn(B - 1, False)

            @block.tensor
            def _(pe):
                def hT_turn(b, st):
                    pe.wait_ge(h_made, b + 1)
                    if st == 0 and not isinstance(b, int):
                        pe.wait_ge(scores_masked, H * (b - 1) + HALF - 1)
                    elif not isinstance(b, int):
                        pe.wait_ge(scores_masked, H * (b - 1) + H - 1)
                    for k in range(KC):
                        last = pe.transpose(xps[:, st, k * P:(k + 1) * P], h[:, st, k * P:(k + 1) * P],
                                            ident[:, :])
                    last.then_inc(hT_up, 1)

                def project(b, st, w):
                    if w == 0:
                        pe.wait_ge(hT_lo, ST * b + st + 1)
                    if w < 2:
                        n = 2 * ST * b + 2 * st + w
                        if not (isinstance(n, int) and n < 2):
                            pe.wait_ge(rot_read, n - 1)
                    else:
                        pe.wait_ge(v_copied if w == 2 else g_made, ST * b + st)
                    for n, (i, j) in enumerate(PASSES):
                        for k in range(KC):
                            last = pe.matmul(pps[:, w, :], hT[:, i, st, k, :], whl[:, j, w, k, :],
                                             start=(n == 0 and k == 0), stop=(n == 2 and k == KC - 1))
                    last.then_inc(proj_up, 1)

                def qkT_turn(b, u):
                    w, st = u // ST, u % ST
                    pe.wait_ge(qk_rotated, 2 * ST * b + 2 * st + w + 1)
                    if u >= 2:
                        pe.wait_ge(qkT_copied, 2 * ST * b + u - 1)
                    for k in range(KC):
                        last = pe.transpose(xps[:, u % 2, k * P:(k + 1) * P], qk[:, w, st, k * P:(k + 1) * P],
                                            ident[:, :])
                    last.then_inc(qkT_up, 1)

                def scores(b, half):
                    for hh in range(half * HALF, (half + 1) * HALF):
                        if hh < 2:
                            pe.wait_ge(qkT_copied, 2 * ST * b + 2 * ST)
                        else:
                            pe.wait_ge(scores_masked, H * b + hh - 1)
                        r = slice(DH * (hh % HG), DH * (hh % HG + 1))
                        k = hh // HG
                        pe.matmul(xps[:, hh % 2, 0:S], qkT[r, 1, k, 0:P], qkT[r, 0, k, :],
                                  start=True, stop=True)
                        pe.matmul(xps[:, hh % 2, S:S + P], qkT[r, 1, k, P:S], qkT[r, 0, k, P:S],
                                  start=True, stop=True).then_inc(scores_up, 1)

                def values(b, half):
                    pe.wait_ge(scores_masked, H * b + (half + 1) * HALF)
                    pe.wait_ge(v_copied, ST * b + ST)
                    if half == 0:
                        pe.wait_ge(r_added, ST * b)
                    else:
                        pe.wait_ge(o_copied, 2 * b + 1)
                    n = DH + 1
                    for j in range(HALF):
                        hh = half * HALF + j
                        pe.matmul(yps[:, 0, j * n:(j + 1) * n], scm[:, j, 0:P], v[:, 0, hh, :],
                                  start=True, stop=True)
                        pe.matmul(yps[:, 1, j * n:(j + 1) * n], scm[:, j, P:2 * P], v[:, 0, hh, :],
                                  start=True, stop=False)
                        last = pe.matmul(yps[:, 1, j * n:(j + 1) * n], scm[:, j, 2 * P:3 * P], v[:, 1, hh, :],
                                         start=False, stop=True)
                    last.then_inc(o_up, 1)

                def out_proj(b):
                    pe.wait_ge(on_gated, b + 1)
                    for st in range(ST):
                        if st == 0:
                            pe.wait_ge(scores_masked, H * b + H)
                        for k in range(KC):
                            last = pe.transpose(xps[:, st, k * P:(k + 1) * P], on[:, st, k * P:(k + 1) * P],
                                                ident[:, :])
                        last.then_inc(oT_up, 1)
                    pe.wait_ge(o_copied, 2 * b + 2)
                    for st in range(ST):
                        pe.wait_ge(oT_lo, ST * b + st + 1)
                        for n, (i, j) in enumerate(PASSES):
                            for k in range(KC):
                                last = pe.matmul(yps[:, st, :], oT[:, i, st, k, :], whl[:, j, 4, k, :],
                                                 start=(n == 0 and k == 0), stop=(n == 2 and k == KC - 1))
                        last.then_inc(out_up, 1)

                def turn(b, more):
                    for u in range(2 * ST):
                        qkT_turn(b, u)
                    scores(b, 0)
                    if more:
                        hT_turn(b + 1, 0)
                        project(b + 1, 0, 0)
                    values(b, 0)
                    scores(b, 1)
                    if more:
                        project(b + 1, 0, 1)
                    values(b, 1)
                    if more:
                        project(b + 1, 0, 2)
                        project(b + 1, 0, 3)
                        hT_turn(b + 1, 1)
                        for w in range(4):
                            project(b + 1, 1, w)
                    out_proj(b)

                pe.wait_ge(const_loaded, 96)
                pe.wait_ge(w_lo, NW)
                for st in range(ST):
                    hT_turn(0, st)
                    for w in range(4):
                        project(0, st, w)
                turn(0, True)
                with pe.Fori(1, B - 1) as b:
                    turn(b, True)
                turn(B - 1, False)


def columns_phase(nc, acc, ident, cols):
    with ExitStack() as ctx:
        def sb(name, shape, dt=F32):
            return ctx.enter_context(nc.sbuf_tensor(name + "_sb", shape, dt))

        def sem(name):
            return ctx.enter_context(nc.semaphore(name))

        sq = sb("c_squares", [P, D])
        ms = sb("c_sums", [P, 2])
        sc = sb("c_scales", [P, 3, 2])
        consts = sb("c_consts", [P, 3])
        h = sb("c_rows", [P, 2, D])
        xps = ctx.enter_context(nc.psum_tensor("c_ps", [P, 2, 512], F32))

        const_set = sem("c_const_set")
        squared = sem("c_squared")
        act_passed = sem("c_act_passed")
        sc_step = sem("c_scale_step")
        h_made = sem("c_h_made")
        h_up = sem("c_h_up")
        hi_made = sem("c_hi_made")
        lo_made = sem("c_lo_made")

        def rows(t):
            return acc[:, bass.ds(t, 1), :].rearrange("p a d -> p (a d)")

        def place(half, t):
            return cols[:, half, :, bass.ds(P * t, P)]

        with nc.Block() as block:
            @block.gpsimd
            def _(pool):
                for n, value in enumerate((1.0 / D, EPS, -0.5)):
                    pool.memset(consts[:, n:n + 1], value).then_inc(const_set, 1)
                pool.wait_ge(const_set, 3)

                def scale(t, par):
                    s = [sc[:, k, par:par + 1] for k in range(3)]
                    pool.wait_ge(squared, t + 1)
                    pool.tensor_tensor(s[0], ms[:, par:par + 1], consts[:, 0:1], ALU.mult).then_inc(sc_step, 1)
                    pool.wait_ge(sc_step, 3 * t + 1)
                    pool.tensor_tensor(s[1], s[0], consts[:, 1:2], ALU.add).then_inc(sc_step, 1)
                    pool.wait_ge(sc_step, 3 * t + 2)
                    pool.tensor_tensor(s[2], s[1], consts[:, 2:3], ALU.pow).then_inc(sc_step, 1)

                scale(0, 0)
                scale(1, 1)
                with pool.Fori(1, NT // 2) as i:
                    for par in range(2):
                        pool.wait_ge(h_made, 2 * i + par - 1)
                        scale(2 * i + par, par)

            @block.scalar
            def _(act):
                def square(t, par):
                    act.activation(sq[:, :], rows(t), ACT.Square, accum_out=ms[:, par:par + 1])\
                       .then_inc(squared, 1)

                def hi(t, par):
                    act.wait_ge(h_up, t + 1).then_inc(act_passed, 1)
                    act.activation(place(0, t), xps[:, par, :].rearrange("p (k t) -> p k t", k=KC),
                                   ACT.Copy).then_inc(hi_made, 1)

                square(0, 0)
                act.wait_ge(squared, 1)
                square(1, 1)
                with act.Fori(0, NT // 2 - 1) as i:
                    for par in range(2):
                        act.wait_ge(squared, 2 * i + par + 2).then_inc(act_passed, 1)
                        act.wait_ge(sc_step, 3 * (2 * i + par) + 1).then_inc(act_passed, 1)
                        square(2 * i + par + 2, par)
                        hi(2 * i + par, par)
                hi(NT - 2, 0)
                hi(NT - 1, 1)

            @block.vector
            def _(dve):
                def turn(t, par, first=False):
                    dve.wait_ge(sc_step, 3 * t + 3)
                    if not first:
                        dve.wait_ge(h_up, t - 1)
                    dve.tensor_scalar(h[:, par, :], rows(t), sc[:, 2, par:par + 1], None, ALU.mult)\
                       .then_inc(h_made, 1)

                def lo(t, par):
                    dve.wait_ge(hi_made, t + 1)
                    dve.tensor_tensor(place(1, t), xps[:, par, :].rearrange("p (k t) -> p k t", k=KC),
                                      place(0, t).bitcast(F32), ALU.subtract).then_inc(lo_made, 1)

                turn(0, 0, True)
                turn(1, 1, True)
                with dve.Fori(0, NT // 2 - 1) as i:
                    for par in range(2):
                        lo(2 * i + par, par)
                        turn(2 * i + par + 2, par)
                lo(NT - 2, 0)
                lo(NT - 1, 1)

            @block.tensor
            def _(pe):
                def turn(t, par, first=False):
                    pe.wait_ge(h_made, t + 1)
                    if not first:
                        pe.wait_ge(lo_made, t - 1)
                    for k in range(KC):
                        last = pe.transpose(xps[:, par, k * P:(k + 1) * P], h[:, par, k * P:(k + 1) * P],
                                            ident[:, :])
                    last.then_inc(h_up, 1)

                turn(0, 0, True)
                turn(1, 1, True)
                with pe.Fori(1, NT // 2) as i:
                    for par in range(2):
                        turn(2 * i + par, par)


def expert_phase(nc, tag, count, gated, w_dram, acc, cols, cw=None, norm_w=None, bias=None, out=None):
    NU = 2 if gated else 1
    W1 = NU * KC * I
    WC = W1 + IC * D
    Q = WC // NB
    func = ACT.Silu if gated else ACT.Gelu_apprx_tanh

    with ExitStack() as ctx:
        def sb(name, shape, dt=F32):
            return ctx.enter_context(nc.sbuf_tensor(f"{tag}_{name}_sb", shape, dt))

        def sem(name):
            return ctx.enter_context(nc.semaphore(f"{tag}_{name}"))

        raw = sb("w_raw", [P, WC])
        whl = sb("w_halves", [P, 2, 2, WC], F32R)
        sil = sb("silu", [P, IC, TB])
        hid = sb("hidden", [P, IC, TB])
        hh = sb("hidden_halves", [P, 2, 2, IC, TB], F32R)
        nw = sb("norm_w", [P, KC]) if norm_w is not None else None
        b1 = sb("bias", [P, count * IC]) if bias is not None else None

        gps = ctx.enter_context(nc.psum_tensor(f"{tag}_g_ps", [P, IC, 2, TB], F32))
        dps = ctx.enter_context(nc.psum_tensor(f"{tag}_d_ps", [P, BT, D], F32))

        const_loaded = sem("const_loaded")
        w_loaded = sem("w_loaded")
        w_scaled = sem("w_scaled")
        w_hi = sem("w_hi")
        w_lo = sem("w_lo")
        first_up = sem("first_up")
        silu_made = sem("silu_made")
        hid_made = sem("hid_made")
        hid_hi = sem("hid_hi")
        hid_lo = sem("hid_lo")
        down_up = sem("down_up")
        added = sem("added")
        stored = sem("stored")
        act_passed = sem("act_passed")

        def w1(par, half, u, k, c):
            at = (u * KC + k) * I + c * P
            return whl[:, par, half, at:at + P]

        def w2(par, half, c):
            return whl[:, par, half, W1 + c * D:W1 + (c + 1) * D]

        SPLIT = NB
        pairs = (count - 1) // 2
        rest = count - 2 * pairs

        with nc.Block() as block:
            @block.sync
            def _(sp):
                if nw is not None:
                    sp.dma_start(nw[:, :], norm_w).then_inc(const_loaded, 16)
                    sp.wait_ge(const_loaded, 16)
                    sp.dma_start(b1[:, :], bias).then_inc(const_loaded, 16)
                sp.dma_start(raw[:, :], w_dram[0]).then_inc(w_loaded, 16)
                with sp.Fori(1, count) as e:
                    sp.wait_ge(w_lo, SPLIT * e)
                    sp.dma_start(raw[:, :], w_dram[e]).then_inc(w_loaded, 16)
                if out is not None:
                    n = NB * (count - 1)
                    for j in range(NB):
                        sp.wait_ge(added, BT * (n + j + 1))
                        sp.dma_start(out[j], acc[:, BT * j:BT * (j + 1), :]).then_inc(stored, 16)
                    sp.wait_ge(stored, 16 * NB)

            @block.gpsimd
            def _(pool):
                def w_rest(e, par, q):
                    at = slice(q * Q, (q + 1) * Q)
                    pool.wait_ge(w_hi, SPLIT * e + q + 1)
                    pool.tensor_tensor(whl[:, par, 1, at], raw[:, at], whl[:, par, 0, at].bitcast(F32),
                                       ALU.subtract).then_inc(w_lo, 1)

                def w_scale(e):
                    pool.wait_ge(w_loaded, 16 * (e + 1))
                    w = raw[:, 0:W1].rearrange("p (k n) -> p k n", k=KC)
                    pool.tensor_tensor(w, w, bcast(nw[:, :].rearrange("p (k o) -> p k o", o=1), [P, KC, I]),
                                       ALU.mult).then_inc(w_scaled, 1)

                def hidden_rest(n, par):
                    for c in range(IC):
                        pool.wait_ge(hid_hi, IC * n + c + 1)
                        pool.tensor_tensor(hh[:, par, 1, c, :], hid[:, c, :], hh[:, par, 0, c, :].bitcast(F32),
                                           ALU.subtract).then_inc(hid_lo, 1)

                def slice_(e, par, more):
                    if more and nw is not None:
                        w_scale(e + 1)
                    for j in range(NB):
                        hidden_rest(NB * e + j, j % 2)
                        if more:
                            w_rest(e + 1, 1 - par, j)

                if nw is not None:
                    pool.wait_ge(const_loaded, 32)
                    w_scale(0)
                for q in range(SPLIT):
                    w_rest(0, 0, q)
                with pool.Fori(0, pairs) as i:
                    for par in range(2):
                        slice_(2 * i + par, par, True)
                for k in range(rest):
                    slice_(2 * pairs + k, k, k < rest - 1)

            @block.scalar
            def _(act):
                def w_first(e, par, q):
                    at = slice(q * Q, (q + 1) * Q)
                    if q == 0:
                        act.wait_ge(w_loaded, 16 * (e + 1))
                        if nw is not None:
                            act.wait_ge(w_scaled, e + 1)
                    act.activation(whl[:, par, 0, at], raw[:, at], ACT.Copy).then_inc(w_hi, 1)

                def hidden(e, j, par, first=False):
                    n = NB * e + j
                    for c in range(IC):
                        act.wait_ge(first_up, IC * n + c + 1)
                        if not first:
                            act.wait_ge(hid_made if gated else hid_lo, IC * (n - 1) + c + 1)
                        if gated:
                            act.activation(sil[:, c, :], gps[:, c, 0, :], func).then_inc(silu_made, 1)
                        else:
                            act.wait_ge(const_loaded, 32).then_inc(act_passed, 1)
                            act.activation(hid[:, c, :], gps[:, c, 0, :], func,
                                           bias=b1[:, bass.ds(IC * e + c, 1)]).then_inc(hid_made, 1)
                    for c in range(IC):
                        act.wait_ge(hid_made, IC * n + c + 1)
                        if not (first or (isinstance(e, int) and NB * e + j < 2)):
                            act.wait_ge(down_up, BT * (n - 1))
                        act.activation(hh[:, j % 2, 0, c, :], hid[:, c, :], ACT.Copy).then_inc(hid_hi, 1)

                def slice_(e, par, more, first=False):
                    for j in range(NB):
                        hidden(e, j, par, first and j == 0)
                        if more:
                            if j == 0 and not first:
                                act.wait_ge(down_up, BT * NB * e)
                            w_first(e + 1, 1 - par, j)

                for q in range(SPLIT):
                    w_first(0, 0, q)
                slice_(0, 0, True, True)
                slice_(1, 1, True)
                with act.Fori(1, pairs) as i:
                    for par in range(2):
                        slice_(2 * i + par, par, True)
                for k in range(rest):
                    slice_(2 * pairs + k, k, k < rest - 1)

            @block.vector
            def _(dve):
                def multiply(n, first=False):
                    for c in range(IC):
                        dve.wait_ge(silu_made, IC * n + c + 1)
                        if not first:
                            dve.wait_ge(hid_lo, IC * (n - 1) + c + 1)
                        dve.tensor_tensor(hid[:, c, :], sil[:, c, :], gps[:, c, 1, :], ALU.mult)\
                           .then_inc(hid_made, 1)

                def add(e, j):
                    n = NB * e + j
                    for t in range(BT):
                        dve.wait_ge(down_up, BT * n + t + 1)
                        row = acc[:, BT * j + t, :]
                        if cw is None:
                            dve.tensor_tensor(row, dps[:, t, :], row, ALU.add).then_inc(added, 1)
                        else:
                            weight = cw[:, bass.ds(e, 1), BT * j + t:BT * j + t + 1]
                            dve.scalar_tensor_tensor(out=row, in0=dps[:, t, :],
                                                     scalar=weight.rearrange("p a b -> p (a b)"), in1=row,
                                                     op0=ALU.mult, op1=ALU.add).then_inc(added, 1)

                def slice_(e, first=False):
                    for j in range(NB):
                        if gated:
                            multiply(NB * e + j, first and j == 0)
                        if not first and j == 0:
                            dve.wait_ge(added, BT * NB * e - BT)
                        if not (first and j == 0):
                            add(e if j else e - 1, (j - 1) % NB)

                slice_(0, True)
                with dve.Fori(1, count) as e:
                    slice_(e)
                add(count - 1, NB - 1)

            @block.tensor
            def _(pe):
                def first(e, j, par):
                    n = NB * e + j
                    if j == 0:
                        pe.wait_ge(w_lo, SPLIT * (e + 1))
                    for c in range(IC):
                        for u in range(NU):
                            if not (isinstance(n, int) and n == 0):
                                if gated:
                                    pe.wait_ge(silu_made if u == 0 else hid_made, IC * (n - 1) + c + 1)
                                else:
                                    pe.wait_ge(hid_made, IC * (n - 1) + c + 1)
                            for m, (s, v) in enumerate(PASSES):
                                for k in range(KC):
                                    last = pe.matmul(gps[:, c, u, :], w1(par, s, u, k, c),
                                                     cols[:, v, k, j * TB:(j + 1) * TB],
                                                     start=(m == 0 and k == 0), stop=(m == 2 and k == KC - 1))
                        last.then_inc(first_up, 1)

                def down(e, j, par):
                    n = NB * e + j
                    pe.wait_ge(hid_lo, IC * (n + 1))
                    for t in range(BT):
                        if not (isinstance(n, int) and n == 0):
                            pe.wait_ge(added, BT * (n - 1) + t + 1)
                        for m, (s, v) in enumerate(PASSES):
                            for c in range(IC):
                                last = pe.matmul(dps[:, t, :], hh[:, j % 2, s, c, t * P:(t + 1) * P],
                                                 w2(par, v, c),
                                                 start=(m == 0 and c == 0), stop=(m == 2 and c == IC - 1))
                        last.then_inc(down_up, 1)

                def slice_(e, par, more):
                    for j in range(NB):
                        if j < NB - 1:
                            first(e, j + 1, par)
                        elif more:
                            first(e + 1, 0, 1 - par)
                        down(e, j, par)

                if nw is not None:
                    pe.wait_ge(const_loaded, 32)
                first(0, 0, 0)
                slice_(0, 0, True)
                slice_(1, 1, True)
                with pe.Fori(1, pairs) as i:
                    for par in range(2):
                        slice_(2 * i + par, par, True)
                for k in range(rest):
                    slice_(2 * pairs + k, k, k < rest - 1)


def wkv_phase(nc, a, acc, ident, cols, cw):
    with ExitStack() as ctx:
        def sb(name, shape, dt=F32):
            return ctx.enter_context(nc.sbuf_tensor(f"k_{name}_sb", shape, dt))

        def sem(name):
            return ctx.enter_context(nc.semaphore(f"k_{name}"))

        xin = sb("x", [P, ST, D])
        f2b = sb("fc2_b", [P, D])
        kr = sb("rows", [P, ST, D])
        kT = sb("kT", [P, KC, S])
        vT = sb("vT", [P, KC, S])
        pp = sb("pp", [P, KC, S + 1])
        av = sb("aa", [P, KC, S + 1])
        bv = sb("bb", [P, KC, S + 1])
        decay = sb("decay", [P, KC])
        dexp = sb("decay_exp", [P, KC])
        u = sb("first", [P, KC])
        wneg = sb("w_cols", [P, KC, S])
        e1b = sb("e1b", [P, KC, S])
        e2b = sb("e2b", [P, KC, S])
        e1 = sb("e1", [P, KC, S])
        e2 = sb("e2", [P, KC, S])
        q = sb("q", [P, KC, S])
        t1 = sb("t1", [P, KC, S])
        xT = sb("xT", [P, ST, KC, P])
        st6 = sb("bn6", [P, ST, 6])
        mv = sb("mean_var", [P, ST, 2])
        rstd = sb("rstd", [P, 2, ST])
        consts = sb("consts", [P, 2, ST])
        gw = sb("gate_w", [P, KC, NE])
        ebias = sb("expert_bias", [P, NE])
        ones = sb("ones", [P, NE])
        score = sb("score", [P, ST, NE])
        biased = sb("biased", [P, ST, NE])
        top8 = sb("top8", [P, ST, 8])
        over = sb("over", [P, ST, NE])
        ties = sb("ties", [P, ST, NE])
        rank = sb("rank", [P, ST, NE])
        chosen = sb("chosen", [P, ST, NE])
        nover = sb("nover", [P, ST])
        total = sb("total", [P, ST])

        xps = ctx.enter_context(nc.psum_tensor("k_x_ps", [P, ST, 512], F32))
        yps = ctx.enter_context(nc.psum_tensor("k_y_ps", [P, ST, 512], F32))
        lps = ctx.enter_context(nc.psum_tensor("k_l_ps", [P, ST, NE], F32))

        const_loaded = sem("const_loaded")
        const_set = sem("const_set")
        x_loaded = sem("x_loaded")
        v_loaded = sem("v_loaded")
        x_biased = sem("x_biased")
        x_added = sem("x_added")
        ln_stats = sem("ln_stats")
        ln_step = sem("ln_step")
        passed = sem("passed")
        act_passed = sem("act_passed")
        rows_made = sem("rows_made")
        rows_up = sem("rows_up")
        kT_copied = sem("kT_copied")
        pp_made = sem("pp_made")
        d1_made = sem("d1_made")
        d2_made = sem("d2_made")
        q_made = sem("q_made")
        d3_made = sem("d3_made")
        d4_made = sem("d4_made")
        state_exp = sem("state_exp")
        out_exp = sem("out_exp")
        bv_made = sem("bv_made")
        scans_made = sem("scans_made")
        n2_made = sem("n2_made")
        d_made = sem("d_made")
        y_step = sem("y_step")
        y_made = sem("y_made")
        y_up = sem("y_up")
        y_added = sem("y_added")
        cols_up = sem("cols_up")
        xT_copied = sem("xT_copied")
        cols_hi = sem("cols_hi")
        cols_lo = sem("cols_lo")
        logits_up = sem("logits_up")
        logits_exp = sem("logits_exp")
        route = sem("route")

        xd = a["x"].rearrange("(b s p) d -> b p s d", p=P, s=ST)
        LN, RS = 3, 2 + 10 * ST

        def rows(b, st):
            return acc[:, bass.ds(ST * b + st, 1), :].rearrange("p a d -> p (a d)")

        def place(half, b, st):
            return cols[:, half, :, bass.ds(S * b + P * st, P)]

        with nc.Block() as block:
            @block.sync
            def _(sp):
                loads = ((f2b[:, :], a["fc2_b"].partition_broadcast(P)), (decay[:, :], a["time_decay"]),
                         (u[:, :], a["time_first"]), (gw[:, :, :], a["gate_w"]),
                         (ebias[:, :], a["expert_bias"].partition_broadcast(P)))
                for n, (dst, src) in enumerate(loads):
                    sp.dma_start(dst, src).then_inc(const_loaded, 16)
                    sp.wait_ge(const_loaded, 16 * (n + 1))
                sp.dma_start(xin[:, :, :], xd[0]).then_inc(x_loaded, 16)
                sp.dma_start(vT[:, :, :], a["ctx"][0]).then_inc(v_loaded, 16)
                with sp.Fori(1, B) as b:
                    sp.wait_ge(x_added, ST * b)
                    sp.dma_start(xin[:, :, :], xd[b]).then_inc(x_loaded, 16)
                    sp.wait_ge(n2_made, b)
                    sp.dma_start(vT[:, :, :], a["ctx"][b]).then_inc(v_loaded, 16)

            @block.gpsimd
            def _(pool):
                pool.memset(consts[:, 0, :], EPS).then_inc(const_set, 1)
                pool.memset(consts[:, 1, :], -0.5).then_inc(const_set, 1)
                pool.memset(ones[:, :], 1.0).then_inc(const_set, 1)
                pool.memset(pp[:, :, 0:1], NEG).then_inc(const_set, 1)
                pool.memset(av[:, :, 0:1], 0.0).then_inc(const_set, 1)
                pool.memset(bv[:, :, 0:1], 0.0).then_inc(const_set, 1)
                pool.memset(cw[:, 0:1, :], 1.0).then_inc(const_set, 1)
                pool.wait_ge(const_set, 7)
                pool.wait_ge(const_loaded, 80)

                def scales(n):
                    pool.wait_ge(ln_stats, 2 * ST * (n + 1))
                    pool.tensor_tensor(rstd[:, 0, :], mv[:, :, 1], consts[:, 0, :], ALU.add).then_inc(ln_step, 1)
                    pool.wait_ge(ln_step, 2 * n + 1)
                    pool.tensor_tensor(rstd[:, 1, :], rstd[:, 0, :], consts[:, 1, :], ALU.pow).then_inc(ln_step, 1)

                def turn(b):
                    pool.wait_ge(x_loaded, 16 * (b + 1))
                    pool.tensor_tensor(xin[:, :, :], xin[:, :, :], bcast(f2b[:, :].rearrange("p (o d) -> p o d", o=1), [P, ST, D]), ALU.add)\
                        .then_inc(x_biased, 1)
                    scales(2 * b)
                    pool.wait_ge(pp_made, b + 1)
                    pool.tensor_tensor(e2b[:, :, :], kT[:, :, :], pp[:, :, 1:S + 1], ALU.subtract).then_inc(d2_made, 1)
                    pool.wait_ge(q_made, b + 1)
                    pool.tensor_tensor(e1[:, :, :], pp[:, :, 0:S], q[:, :, :], ALU.subtract).then_inc(d3_made, 1)
                    pool.wait_ge(state_exp, 2 * b + 2)
                    pool.wait_ge(v_loaded, 16 * (b + 1))
                    pool.wait_ge(d4_made, b + 1)
                    pool.wait_ge(d3_made, b + 1)
                    pool.tensor_tensor(q[:, :, :], e2b[:, :, :], vT[:, :, :], ALU.mult).then_inc(bv_made, 1)
                    pool.wait_ge(out_exp, 2 * b + 2)
                    pool.tensor_tensor(t1[:, :, :], e2[:, :, :], vT[:, :, :], ALU.mult).then_inc(n2_made, 1)
                    pool.wait_ge(scans_made, b + 1)
                    pool.tensor_tensor(e1b[:, :, :], e1[:, :, :], bv[:, :, 0:S], ALU.mult).then_inc(d_made, 1)
                    pool.wait_ge(d_made, 2 * b + 1)
                    pool.tensor_tensor(e1b[:, :, :], e1b[:, :, :], e2[:, :, :], ALU.add).then_inc(d_made, 1)
                    scales(2 * b + 1)

                turn(0)
                with pool.Fori(1, B) as b:
                    turn(b)

            @block.scalar
            def _(act):
                act.wait_ge(const_loaded, 80)
                act.activation(dexp[:, :], decay[:, :], ACT.Exp).then_inc(act_passed, 1)

                def turn(b):
                    for st in range(ST):
                        act.wait_ge(rows_up, ST * b + st + 1)
                        act.activation(kT[:, :, st * P:(st + 1) * P],
                                       xps[:, st, :].rearrange("p (k t) -> p k t", k=KC), ACT.Copy).then_inc(kT_copied, 1)
                    act.wait_ge(d1_made, b + 1)
                    act.activation(e1b[:, :, :], e1b[:, :, :], ACT.Exp).then_inc(state_exp, 1)
                    act.wait_ge(d2_made, b + 1)
                    act.activation(e2b[:, :, :], e2b[:, :, :], ACT.Exp).then_inc(state_exp, 1)
                    act.wait_ge(d4_made, b + 1)
                    act.activation(e2[:, :, :], e2[:, :, :], ACT.Exp).then_inc(out_exp, 1)
                    act.wait_ge(d3_made, b + 1)
                    act.activation(e1[:, :, :], e1[:, :, :], ACT.Exp).then_inc(out_exp, 1)
                    for st in range(ST):
                        act.wait_ge(cols_up, ST * b + st + 1)
                        act.activation(xT[:, st, :, :], xps[:, st, :].rearrange("p (k t) -> p k t", k=KC),
                                       ACT.Copy).then_inc(xT_copied, 1)
                    act.wait_ge(logits_up, b + 1)
                    act.activation(score[:, :, :], lps[:, :, :], ACT.Exp, scale=-1.0).then_inc(logits_exp, 1)

                turn(0)
                with act.Fori(1, B) as b:
                    turn(b)

            @block.vector
            def _(dve):
                dve.wait_ge(act_passed, 1)
                dve.wait_ge(const_loaded, 80)
                dve.wait_ge(const_set, 7)
                dve.tensor_scalar(dexp[:, :], dexp[:, :], -1.0, None, ALU.mult).then_inc(passed, 1)
                dve.wait_ge(passed, 1)
                dve.memset(t1[:, :, :], 0.0).then_inc(passed, 1)
                dve.wait_ge(passed, 2)
                for c in range(KC):
                    dve.tensor_scalar(wneg[:, c, :], t1[:, c, :], dexp[:, c:c + 1], None, ALU.add).then_inc(passed, 1)
                dve.wait_ge(passed, 2 + KC)

                def norm(n, b):
                    for st in range(ST):
                        dve.bn_stats(st6[:, st, :], rows(b, st)).then_inc(ln_stats, 1)
                    dve.wait_ge(ln_stats, 2 * ST * n + ST).then_inc(passed, 1)
                    for st in range(ST):
                        dve.bn_aggr(mv[:, st, :], st6[:, st, :]).then_inc(ln_stats, 1)
                    dve.wait_ge(ln_step, 2 * n + 2)
                    for st in range(ST):
                        dve.tensor_scalar(kr[:, st, :], rows(b, st), mv[:, st, 0:1], rstd[:, 1, st:st + 1],
                                          ALU.subtract, ALU.mult).then_inc(rows_made, 1)

                def turn(b):
                    dve.wait_ge(x_biased, b + 1)
                    for st in range(ST):
                        dve.tensor_tensor(rows(b, st), rows(b, st), xin[:, st, :], ALU.add).then_inc(x_added, 1)
                    dve.wait_ge(x_added, ST * b + ST).then_inc(passed, 1)
                    norm(2 * b, b)
                    dve.wait_ge(kT_copied, ST * b + ST)
                    for c in range(KC):
                        last = dve.tensor_tensor_scan(pp[:, c, 1:S + 1], wneg[:, c, :], kT[:, c, :], NEG,
                                                      ALU.add, ALU.max)
                    last.then_inc(pp_made, 1)
                    dve.wait_ge(pp_made, b + 1)
                    for c in range(KC):
                        last = dve.scalar_tensor_tensor(out=e1b[:, c, :], in0=pp[:, c, 0:S], scalar=dexp[:, c:c + 1],
                                                        in1=pp[:, c, 1:S + 1], op0=ALU.add, op1=ALU.subtract)
                    last.then_inc(d1_made, 1)
                    for c in range(KC):
                        last = dve.scalar_tensor_tensor(out=q[:, c, :], in0=kT[:, c, :], scalar=u[:, c:c + 1],
                                                        in1=pp[:, c, 0:S], op0=ALU.add, op1=ALU.max)
                    last.then_inc(q_made, 1)
                    dve.wait_ge(q_made, b + 1)
                    for c in range(KC):
                        last = dve.scalar_tensor_tensor(out=e2[:, c, :], in0=kT[:, c, :], scalar=u[:, c:c + 1],
                                                        in1=q[:, c, :], op0=ALU.add, op1=ALU.subtract)
                    last.then_inc(d4_made, 1)
                    dve.wait_ge(state_exp, 2 * b + 2)
                    for c in range(KC):
                        dve.tensor_tensor_scan(bv[:, c, 1:S + 1], e1b[:, c, :], e2b[:, c, :], 0.0, ALU.mult, ALU.add)
                    dve.wait_ge(bv_made, b + 1)
                    for c in range(KC):
                        last = dve.tensor_tensor_scan(av[:, c, 1:S + 1], e1b[:, c, :], q[:, c, :], 0.0,
                                                      ALU.mult, ALU.add)
                    last.then_inc(scans_made, 1)
                    dve.wait_ge(out_exp, 2 * b + 2)
                    dve.wait_ge(scans_made, b + 1)
                    dve.tensor_tensor(q[:, :, :], e1[:, :, :], av[:, :, 0:S], ALU.mult).then_inc(y_step, 1)
                    dve.wait_ge(n2_made, b + 1)
                    dve.wait_ge(y_step, 3 * b + 1)
                    dve.tensor_tensor(q[:, :, :], q[:, :, :], t1[:, :, :], ALU.add).then_inc(y_step, 1)
                    dve.wait_ge(d_made, 2 * b + 2)
                    dve.reciprocal(e1b[:, :, :], e1b[:, :, :]).then_inc(y_step, 1)
                    dve.wait_ge(y_step, 3 * b + 3)
                    dve.tensor_tensor(q[:, :, :], q[:, :, :], e1b[:, :, :], ALU.mult).then_inc(y_made, 1)
                    for st in range(ST):
                        dve.wait_ge(y_up, ST * b + st + 1)
                        dve.tensor_tensor(rows(b, st), yps[:, st, :], rows(b, st), ALU.add).then_inc(y_added, 1)
                    dve.wait_ge(y_added, ST * b + ST).then_inc(passed, 1)
                    norm(2 * b + 1, b)
                    for st in range(ST):
                        dve.wait_ge(xT_copied, ST * b + st + 1)
                        dve.tensor_scalar(place(0, b, st), xT[:, st, :, :], 1.0, None, ALU.mult).then_inc(cols_hi, 1)
                    for st in range(ST):
                        dve.wait_ge(cols_hi, ST * b + st + 1)
                        dve.tensor_tensor(place(1, b, st), xT[:, st, :, :], place(0, b, st).bitcast(F32),
                                          ALU.subtract).then_inc(cols_lo, 1)
                    n = RS * b
                    dve.wait_ge(logits_exp, b + 1)
                    dve.tensor_scalar(score[:, :, :], score[:, :, :], 1.0, None, ALU.add).then_inc(route, 1)
                    dve.wait_ge(route, n + 1)
                    dve.reciprocal(score[:, :, :], score[:, :, :]).then_inc(route, 1)
                    n += 2

                    def stage(k, op):
                        dve.wait_ge(route, n + ST * k).then_inc(passed, 1)
                        for st in range(ST):
                            op(st).then_inc(route, 1)

                    stage(0, lambda st: dve.tensor_tensor(biased[:, st, :], score[:, st, :], ebias[:, :], ALU.add))
                    stage(1, lambda st: dve.max(top8[:, st, :], biased[:, st, :]))
                    stage(2, lambda st: dve.tensor_scalar(over[:, st, :], biased[:, st, :],
                                                          top8[:, st, TOPK - 1:TOPK], 0.0, ALU.is_gt, ALU.add,
                                                          accum_out=nover[:, st:st + 1]))
                    stage(3, lambda st: dve.tensor_scalar(ties[:, st, :], biased[:, st, :],
                                                          top8[:, st, TOPK - 1:TOPK], None, ALU.is_equal))
                    stage(4, lambda st: dve.tensor_tensor_scan(rank[:, st, :], ones[:, :], ties[:, st, :],
                                                               nover[:, st:st + 1], ALU.mult, ALU.add))
                    stage(5, lambda st: dve.scalar_tensor_tensor(out=chosen[:, st, :], in0=rank[:, st, :],
                                                                 scalar=float(TOPK), in1=ties[:, st, :],
                                                                 op0=ALU.is_le, op1=ALU.mult))
                    stage(6, lambda st: dve.tensor_tensor(over[:, st, :], over[:, st, :], chosen[:, st, :], ALU.add))
                    stage(7, lambda st: dve.scalar_tensor_tensor(out=chosen[:, st, :], in0=over[:, st, :], scalar=1.0,
                                                                 in1=score[:, st, :], op0=ALU.mult, op1=ALU.mult,
                                                                 accum_out=total[:, st:st + 1]))
                    stage(8, lambda st: dve.reciprocal(total[:, st:st + 1], total[:, st:st + 1]))
                    stage(9, lambda st: dve.tensor_scalar(
                        cw[:, 1:NE + 1, bass.ds(ST * b + st, 1)].rearrange("p e o -> p (e o)"),
                        chosen[:, st, :], total[:, st:st + 1], None, ALU.mult))

                turn(0)
                with dve.Fori(1, B) as b:
                    turn(b)

            @block.tensor
            def _(pe):
                def turned(dst, src):
                    for k in range(KC):
                        last = pe.transpose(dst(k), src(k), ident[:, :])
                    return last

                def turn(b):
                    for st in range(ST):
                        pe.wait_ge(rows_made, 2 * ST * b + st + 1)
                        pe.wait_ge(xT_copied, ST * b)
                        turned(lambda k: xps[:, st, k * P:(k + 1) * P],
                               lambda k: kr[:, st, k * P:(k + 1) * P]).then_inc(rows_up, 1)
                    pe.wait_ge(y_made, b + 1)
                    pe.wait_ge(y_added, ST * b)
                    for st in range(ST):
                        turned(lambda k: yps[:, st, k * P:(k + 1) * P],
                               lambda k: q[:, k, st * P:(st + 1) * P]).then_inc(y_up, 1)
                    for st in range(ST):
                        pe.wait_ge(rows_made, 2 * ST * b + ST + st + 1)
                        turned(lambda k: xps[:, st, k * P:(k + 1) * P],
                               lambda k: kr[:, st, k * P:(k + 1) * P]).then_inc(cols_up, 1)
                    pe.wait_ge(logits_exp, b)
                    for st in range(ST):
                        pe.wait_ge(xT_copied, ST * b + st + 1)
                        for k in range(KC):
                            last = pe.matmul(lps[:, st, :], xT[:, st, k, :], gw[:, k, :],
                                             start=(k == 0), stop=(k == KC - 1))
                    last.then_inc(logits_up, 1)

                pe.wait_ge(const_loaded, 80)
                turn(0)
                with pe.Fori(1, B) as b:
                    turn(b)


def build(nc, a, out, stop=9):
    with ExitStack() as ctx:
        acc = ctx.enter_context(nc.sbuf_tensor("acc", [P, NT, D], F32))
        ident = ctx.enter_context(nc.sbuf_tensor("identity", [P, P], F32))
        out_rows = out.rearrange("(j n p) d -> j p n d", j=NB, p=P)
        attention_phase(nc, a, acc, ident)
        cols = ctx.enter_context(nc.sbuf_tensor("cols_halves", [P, 2, KC, B * S], F32R))
        cw = ctx.enter_context(nc.sbuf_tensor("expert_weights", [P, NE + 1, NT], F32))
        if stop > 1:
            columns_phase(nc, acc, ident, cols)
            expert_phase(nc, "f", F // I, False, a["ffn_w"], acc, cols, norm_w=a["final_w"], bias=a["fc1_b"])
        if stop > 2:
            wkv_phase(nc, a, acc, ident, cols, cw)
        if stop > 3:
            expert_phase(nc, "m", NE + 1, True, a["moe_w"], acc, cols, cw=cw, out=out_rows)
        else:
            stored = ctx.enter_context(nc.semaphore("out_stored"))
            with nc.Block() as block:
                @block.sync
                def _(sp):
                    sp.dma_start(out.rearrange("(n p) d -> p n d", p=P), acc[:, :, :]).then_inc(stored, 16)
                    sp.wait_ge(stored, 16)


def attention_constants():
    angle = (1.0 / 10000.0 ** np.linspace(0.0, 1.0, DH // 2, dtype=np.float32)).astype(np.float32)
    phase = np.arange(S, dtype=np.float32)[:, None] * np.repeat(angle, 2)[None, :]
    sign = np.where(np.arange(DH) % 2 == 0, -1.0, 1.0).astype(np.float32)
    rows = lambda t: np.ascontiguousarray(t.reshape(ST, P, -1).transpose(1, 0, 2).astype(np.float32))
    decay = np.log(1.0 - 2.0 ** (-5.0 - np.arange(H)))
    i, t = np.arange(S)[:, None], np.arange(S)[None, :]
    m = np.where(i >= t, np.exp(np.where(i >= t, i - t, 0)[None] * decay[:, None, None]), 0.0)
    inv = 1.0 / np.sqrt(m.sum(-1))
    mt = m.transpose(2, 0, 1)[:P].reshape(P, H, 2, P) * DH ** -0.5
    return {"cos": rows(np.cos(phase)), "sin": rows(np.sin(phase) * sign),
            "inv_norm": rows(inv.T), "mask": np.ascontiguousarray(mt.astype(np.float32)),
            "ident": np.eye(P, dtype=np.float32)}


def kernel(**inputs):
    from concourse import bacc
    from concourse.bass_utils import run_bass_kernel_spmd

    x = {n: np.asarray(v) for n, v in inputs.items()}
    arrays = layouts(x)
    nc = bacc.Bacc("TRN2", target_bir_lowering=False, num_devices=1)
    aps = {n: nc.dram_tensor(n, v.shape, mybir.dt.from_np(v.dtype), kind="ExternalInput").ap()
           for n, v in arrays.items()}
    out = nc.dram_tensor("out", (B * S, D), F32, kind="ExternalOutput").ap()
    build(nc, aps, out)
    r = run_bass_kernel_spmd(nc, [arrays], core_ids=[0])
    return r.results[0]["out"].reshape(B, S, D)


def layouts(x):
    def chunks(w):
        return w.reshape(-1, P, w.shape[-1]).transpose(1, 0, 2)

    arrays = dict(attention_constants())
    arrays["x"] = x["x"].reshape(B * S, D)
    arrays["attn_w"] = np.stack([chunks(x[f"L0_attn_{n}_w"]) for n in ("q", "k", "v", "g", "out")])
    arrays["retn_w"] = x["L0_attn_retn_norm_w"].reshape(KC, P).T
    arrays["final_w"] = x["L0_attn_final_norm_w"].reshape(KC, P).T

    def joined(*parts):
        return np.concatenate([p.reshape(p.shape[0], P, -1) for p in parts], axis=2)

    def slice_chunks(w):
        return w.reshape(w.shape[0], -1, P, w.shape[-1]).transpose(0, 2, 1, 3)

    fc1 = x["L0_attn_fc1_w"].reshape(D, F // I, I).transpose(1, 0, 2)
    fc2 = x["L0_attn_fc2_w"].reshape(F // I, I, D)
    arrays["ffn_w"] = joined(slice_chunks(fc1), slice_chunks(fc2))
    arrays["fc1_b"] = x["L0_attn_fc1_b"].reshape(F // P, P).T
    arrays["fc2_b"] = x["L0_attn_fc2_b"].reshape(1, D)
    experts = [np.concatenate([x[f"L0_ffn_sw_{n}"][None], x[f"L0_ffn_w_{n}"]]) for n in ("gate", "up", "down")]
    arrays["moe_w"] = joined(*(slice_chunks(w.transpose(0, 2, 1)) for w in experts))
    arrays["ctx"] = x["ctx_2048"].reshape(B, S, KC, P).transpose(0, 3, 2, 1)
    arrays["time_decay"] = x["L0_xattn_time_decay"].reshape(KC, P).T
    arrays["time_first"] = x["L0_xattn_time_first"].reshape(KC, P).T
    arrays["gate_w"] = chunks(x["L0_ffn_gate_w"].T)
    arrays["expert_bias"] = x["L0_ffn_expert_bias"].reshape(1, NE)
    return {n: np.ascontiguousarray(v) for n, v in arrays.items()}
```

```python
from contextlib import ExitStack

import numpy as np

import concourse.bass as bass
from concourse import mybir

F32 = mybir.dt.float32
F32R = mybir.dt.float32r
I32 = mybir.dt.int32
ALU = mybir.AluOpType
ACT = mybir.ActivationFunctionType
AX_X = mybir.AxisListType.X

P = 128
B, S, D = 8, 256, 512
NT = B * S // P
ST = S // P
KC = D // P
H = 16
DH = D // H
HG = P // DH
HALF = H // 2
F = 2048
NE = 16
TOPK = 4
I = 256
IC = I // P
TB = 512
NB = B * S // TB
BT = TB // P
UT = 256
UR = UT // P
SU = B * S // UT
RU = (B * S * TOPK + NE * (UT - 1)) // UT
LR = RU * UR
EPS = 1e-5
NEG = -1e38

PASSES = ((0, 0), (0, 1), (1, 0))


def bcast(ap, shape):
    return ap.to_broadcast(shape)


def attention_phase(nc, a, acc, ident):
    with ExitStack() as ctx:
        def sb(name, shape, dt=F32):
            return ctx.enter_context(nc.sbuf_tensor(name + "_sb", shape, dt))

        def sem(name):
            return ctx.enter_context(nc.semaphore(name))

        NW = 5
        whl = sb("attn_w_halves", [P, 2, NW, KC, D], F32R)
        scm = sb("scores_masked_sb", [P, HALF, 3 * P])
        mask = sb("decay_mask", [P, H, 2, P])
        invn = sb("inv_mask_norm", [P, ST, H])
        cos = sb("cos_t", [P, ST, DH])
        sin = sb("sin_t", [P, ST, DH])
        rnw = sb("retn_w", [P, KC])
        xin = sb("xin", [P, ST, D])
        h = sb("h_rows", [P, ST, D])
        hT = sb("hT_halves", [P, 2, ST, KC, P], F32R)
        tcos = sb("rot_cos", [P, D])
        tsin = sb("rot_sin", [P, D])
        qk = sb("qk_rows", [P, 2, ST, D])
        qT = sb("q_cols", [P, KC, S])
        kT = sb("k_cols", [P, HG, KC, S])
        wraw = [scm[:, :, :].rearrange("p h n -> p (h n)")[:, 0:KC * D].rearrange("p (k n) -> p k n", k=KC),
                qk[:, :, :, :].rearrange("p w s d -> p (w s) d")]
        v = sb("v_and_ones", [P, ST, H, DH + 1])
        gate = sb("gate_rows", [P, ST, D])
        o = sb("o_and_denom", [P, ST, H, DH + 1])
        on = sb("o_normed", [P, ST, D])
        oT = hT
        st6 = sb("bn6", [P, ST, 6])
        mv = sb("mean_var", [P, ST, 2])
        lnc = sb("ln_consts", [P, 4, ST])
        mhalf = sb("minus_half", [P, ST * H])
        eps = sb("eps_t", [P, ST * H])
        sm = sb("norm_small", [P, 6, ST, H])

        xps = ctx.enter_context(nc.psum_tensor("x_ps", [P, 2, 512], F32))
        yps = ctx.enter_context(nc.psum_tensor("y_ps", [P, 2, 512], F32))
        pps = ctx.enter_context(nc.psum_tensor("proj_ps", [P, 4, 512], F32))

        rnw_loaded = sem("a_rnw_loaded")
        ident_loaded = sem("a_ident_loaded")
        rot_loaded = [sem("a_cos_loaded"), sem("a_sin_loaded")]
        invn_loaded = sem("a_invn_loaded")
        mask_loaded = sem("a_mask_loaded")
        w_loaded = [sem("a_w_even_loaded"), sem("a_w_odd_loaded")]
        zeros_set = sem("a_zeros_set")
        w_hi = sem("a_w_hi")
        w_lo = sem("a_w_lo")
        ones_set = sem("a_ones_set")
        half_set = sem("a_half_set")
        x_loaded = sem("a_x_loaded")
        bn_made = sem("a_bn_made")
        bn_passed = sem("a_bn_passed")
        stats_made = sem("a_stats_made")
        ln_step = sem("a_ln_step")
        h_made = sem("a_h_made")
        hT_up = sem("a_hT_up")
        hT_hi = sem("a_hT_hi")
        hT_lo = sem("a_hT_lo")
        proj_up = sem("a_proj_up")
        rot_read = sem("a_rot_read")
        qk_rotated = sem("a_qk_rotated")
        v_copied = sem("a_v_copied")
        g_made = sem("a_g_made")
        qkT_up = sem("a_qkT_up")
        qkT_copied = sem("a_qkT_copied")
        scores_up = sem("a_scores_up")
        scores_masked = sem("a_scores_masked")
        o_up = sem("a_o_up")
        o_copied = sem("a_o_copied")
        o_squared = sem("a_o_squared")
        nv = sem("a_norm_dve")
        ng = sem("a_norm_pool")
        on_gated = sem("a_on_gated")
        oT_up = sem("a_oT_up")
        oT_hi = sem("a_oT_hi")
        oT_lo = sem("a_oT_lo")
        out_up = sem("a_out_up")
        r_added = sem("a_r_added")

        NV, LN = 11, 7
        xd = a["x"].rearrange("(b s p) d -> b p s d", p=P, s=ST)

        with nc.Block() as block:
            @block.sync
            def _(sp):
                def load_w(n):
                    sp.dma_start(wraw[n % 2], a["attn_w"][n]).then_inc(w_loaded[n % 2], 16)

                sp.dma_start(xin[:, :, :], xd[0]).then_inc(x_loaded, 16)
                sp.dma_start(rnw[:, :], a["retn_w"]).then_inc(rnw_loaded, 16)
                load_w(0)
                sp.dma_start(ident[:, :], a["ident"]).then_inc(ident_loaded, 16)
                load_w(1)
                sp.dma_start(cos[:, :, :], a["cos"]).then_inc(rot_loaded[0], 16)
                sp.dma_start(sin[:, :, :], a["sin"]).then_inc(rot_loaded[1], 16)
                sp.dma_start(invn[:, :, :], a["inv_norm"]).then_inc(invn_loaded, 16)
                for n in range(2, NW):
                    sp.wait_ge(w_lo, n - 1)
                    load_w(n)
                sp.dma_start(mask[:, :, :, :], a["mask"]).then_inc(mask_loaded, 16)
                with sp.Fori(1, B) as b:
                    sp.wait_ge(h_made, b)
                    sp.dma_start(xin[:, :, :], xd[b]).then_inc(x_loaded, 16)

            @block.gpsimd
            def _(pool):
                pool.memset(mhalf[:, :], -0.5).then_inc(half_set, 1)
                pool.memset(eps[:, :], EPS).then_inc(half_set, 1)
                pool.memset(v[:, :, :, DH:DH + 1], 1.0).then_inc(ones_set, 1)
                pool.memset(kT[:, :, :, :], 0.0).then_inc(zeros_set, 1)
                pool.wait_ge(half_set, 2)

                def heads(t):
                    return t[:, :].rearrange("p (s h) -> p s h", s=ST)

                def ln_scales(b):
                    var = mv[:, :, 1]
                    ve, rstd, t, s = (lnc[:, k, :] for k in range(4))
                    n = LN * b
                    pool.wait_ge(stats_made, ST * (b + 1))
                    if not (isinstance(b, int) and b == 0):
                        pool.wait_ge(h_made, b)
                    pool.tensor_tensor(ve, var, eps[:, 0:ST], ALU.add).then_inc(ln_step, 1)
                    pool.wait_ge(ln_step, n + 1)
                    pool.tensor_tensor(rstd, ve, mhalf[:, 0:ST], ALU.pow).then_inc(ln_step, 1)
                    pool.wait_ge(ln_step, n + 2)
                    pool.tensor_tensor(t, rstd, rstd, ALU.mult).then_inc(ln_step, 1)
                    pool.wait_ge(ln_step, n + 3)
                    pool.tensor_tensor(ve, t, var, ALU.mult).then_inc(ln_step, 1)
                    pool.wait_ge(ln_step, n + 4)
                    pool.tensor_tensor(t, ve, eps[:, 0:ST], ALU.add).then_inc(ln_step, 1)
                    pool.wait_ge(ln_step, n + 5)
                    pool.tensor_tensor(ve, t, mhalf[:, 0:ST], ALU.pow).then_inc(ln_step, 1)
                    pool.wait_ge(ln_step, n + 6)
                    pool.tensor_tensor(s, rstd, ve, ALU.mult).then_inc(ln_step, 1)

                def rotate(b, st, w):
                    n = 2 * ST * b + 2 * st + w
                    pool.wait_ge(rot_read, n + 1)
                    if isinstance(b, int) and b == 0:
                        pool.wait_ge(w_lo, NW - 1)
                    else:
                        pool.wait_ge(qkT_up, 2 * ST * b)
                    pool.tensor_tensor(qk[:, w, st, :], tcos[:, :], tsin[:, :], ALU.add)\
                        .then_inc(qk_rotated, 1)

                def norm(b):
                    pool.wait_ge(nv, NV * b + 9)
                    pool.tensor_tensor(sm[:, 3, :, :], sm[:, 4, :, :], heads(mhalf), ALU.pow).then_inc(ng, 1)
                    pool.wait_ge(nv, NV * b + NV)
                    pool.wait_ge(g_made, ST * b + ST)
                    pool.tensor_tensor(on[:, :, :], on[:, :, :], gate[:, :, :], ALU.mult).then_inc(on_gated, 1)

                def turn(b, after):
                    if after:
                        rotate(b + 1, 0, 0)
                        rotate(b + 1, 0, 1)
                    norm(b)
                    if after > 1:
                        ln_scales(b + 2)
                    if after:
                        rotate(b + 1, 1, 0)
                        rotate(b + 1, 1, 1)

                ln_scales(0)
                for st in range(ST):
                    rotate(0, st, 0)
                    rotate(0, st, 1)
                ln_scales(1)
                turn(0, 2)
                with pool.Fori(1, B - 2) as b:
                    turn(b, 2)
                turn(B - 2, 1)
                turn(B - 1, 0)

            @block.scalar
            def _(act):
                def weight_first(n):
                    act.wait_ge(w_loaded[n % 2], 16 * (n // 2 + 1))
                    if n < NW - 1:
                        act.wait_ge(rnw_loaded, 16)
                        for k in range(KC):
                            last = act.activation(whl[:, 0, n, k, :], wraw[n % 2][:, k, :], ACT.Copy,
                                                  scale=rnw[:, k:k + 1])
                    else:
                        last = act.activation(whl[:, 0, n, :, :], wraw[n % 2], ACT.Copy)
                    last.then_inc(w_hi, 1)

                def hT_halves(b, st):
                    act.wait_ge(hT_up, ST * b + st + 1)
                    act.activation(hT[:, 0, st, :, :], pps[:, 2 + st, :].rearrange("p (k t) -> p k t", k=KC),
                                   ACT.Copy).then_inc(hT_hi, 1)

                def values_out(b, st):
                    u = 4 * (ST * b + st)
                    act.wait_ge(proj_up, u + 3)
                    act.wait_ge(o_up, ST * b)
                    act.activation(v[:, st, :, 0:DH], pps[:, 2, :].rearrange("p (h d) -> p h d", h=H),
                                   ACT.Copy).then_inc(v_copied, 1)

                def gate_out(b, st):
                    act.wait_ge(proj_up, 4 * (ST * b + st) + 4)
                    act.wait_ge(on_gated, b)
                    act.activation(gate[:, st, :], pps[:, 3, :], ACT.Silu).then_inc(g_made, 1)

                def turn(b, more):
                    for u in range(2 * ST):
                        w, st = u // ST, u % ST
                        act.wait_ge(qkT_up, 2 * ST * b + u + 1)
                        if w == 0:
                            last = act.activation(qT[:, :, st * P:(st + 1) * P],
                                                  xps[:, u % 2, :].rearrange("p (k t) -> p k t", k=KC), ACT.Copy)
                        else:
                            for g in range(HG):
                                r = slice(DH * g, DH * (g + 1))
                                last = act.activation(kT[r, g, :, st * P:(st + 1) * P],
                                                      xps[r, u % 2, :].rearrange("p (k t) -> p k t", k=KC),
                                                      ACT.Copy)
                        last.then_inc(qkT_copied, 1)
                    if more:
                        hT_halves(b + 1, 0)
                        hT_halves(b + 1, 1)
                    for half in range(2):
                        act.wait_ge(o_up, 2 * b + half + 1)
                        act.wait_ge(on_gated, b)
                        act.activation(o[:, :, half * HALF:(half + 1) * HALF, :],
                                       yps[:, :, 0:HALF * (DH + 1)].rearrange("p s (h d) -> p s h d", h=HALF),
                                       ACT.Copy).then_inc(o_copied, 1)
                    act.wait_ge(o_copied, 2 * b + 2)
                    act.wait_ge(oT_up, ST * b)
                    act.activation(on[:, :, :].rearrange("p s (h d) -> p (s h) d", h=H),
                                   o[:, :, :, 0:DH].rearrange("p s h d -> p (s h) d"),
                                   ACT.Square).then_inc(o_squared, 1)
                    if more:
                        values_out(b + 1, 0)
                        gate_out(b + 1, 0)
                        values_out(b + 1, 1)
                        gate_out(b + 1, 1)
                    for st in range(ST):
                        act.wait_ge(oT_up, ST * b + st + 1)
                        act.activation(oT[:, 0, st, :, :], pps[:, 2 + st, :].rearrange("p (k t) -> p k t", k=KC),
                                       ACT.Copy).then_inc(oT_hi, 1)

                weight_first(0)
                weight_first(1)
                hT_halves(0, 0)
                hT_halves(0, 1)
                weight_first(2)
                weight_first(3)
                act.wait_ge(ones_set, 1)
                values_out(0, 0)
                gate_out(0, 0)
                weight_first(4)
                values_out(0, 1)
                gate_out(0, 1)
                act.wait_ge(zeros_set, 1)
                turn(0, True)
                with act.Fori(1, B - 1) as b:
                    turn(b, True)
                turn(B - 1, False)

            @block.vector
            def _(dve):
                def ln_stats(b):
                    dve.wait_ge(x_loaded, 16 * (b + 1))
                    for st in range(ST):
                        dve.bn_stats(st6[:, st, :], xin[:, st, :]).then_inc(bn_made, 1)
                    dve.wait_ge(bn_made, ST * b + ST).then_inc(bn_passed, 1)
                    for st in range(ST):
                        dve.bn_aggr(mv[:, st, :], st6[:, st, :]).then_inc(stats_made, 1)

                def ln_rows(b):
                    dve.wait_ge(ln_step, LN * (b + 1))
                    dve.wait_ge(hT_up, ST * b)
                    for st in range(ST):
                        dve.tensor_scalar(acc[:, bass.ds(ST * b + st, 1), :].rearrange("p a d -> p (a d)"),
                                          xin[:, st, :], mv[:, st, 0:1], lnc[:, 1, st:st + 1],
                                          ALU.subtract, ALU.mult)
                        last = dve.tensor_scalar(h[:, st, :], xin[:, st, :], mv[:, st, 0:1],
                                                 lnc[:, 3, st:st + 1], ALU.subtract, ALU.mult)
                    last.then_inc(h_made, 1)

                def hT_rest(b, st):
                    dve.wait_ge(hT_hi, ST * b + st + 1)
                    dve.tensor_tensor(hT[:, 1, st, :, :], pps[:, 2 + st, :].rearrange("p (k t) -> p k t", k=KC),
                                      hT[:, 0, st, :, :].bitcast(F32), ALU.subtract).then_inc(hT_lo, 1)

                def rotate(b, st, w):
                    n = 2 * ST * b + 2 * st + w
                    dve.wait_ge(proj_up, 4 * (ST * b + st) + w + 1)
                    if not (isinstance(n, int) and n == 0):
                        dve.wait_ge(qk_rotated, n)
                    src = pps[:, w, :].rearrange("p (h d) -> p h d", h=H)
                    dve.tensor_tensor(tcos[:, :].rearrange("p (h d) -> p h d", h=H), src,
                                      bcast(cos[:, st:st + 1, :], [P, H, DH]), ALU.mult)
                    pair = pps[:, w, :].rearrange("p (h d t) -> p h d t", h=H, t=2)
                    swap = tsin[:, :].rearrange("p (h d t) -> p h d t", h=H, t=2)
                    sign = sin[:, st:st + 1, :].rearrange("p s (d t) -> p s d t", t=2)
                    for t in range(2):
                        last = dve.tensor_tensor(swap[:, :, :, t], pair[:, :, :, 1 - t],
                                                 bcast(sign[:, :, :, t], [P, H, DH // 2]), ALU.mult)
                    last.then_inc(rot_read, 1)

                def masks(b, half, first=0, end=HALF):
                    for j in range(first, end):
                        hh = half * HALF + j
                        dve.wait_ge(scores_up, H * b + hh + 1)
                        if j == 0:
                            dve.wait_ge(o_up, 2 * b + half)
                        x = hh % 2
                        dve.tensor_tensor(scm[:, j, 0:2 * P], xps[:, x, 0:2 * P],
                                          mask[:, hh, :, :].rearrange("p a t -> p (a t)"), ALU.mult)
                        dve.tensor_tensor(scm[:, j, 2 * P:3 * P], xps[:, x, 2 * P:3 * P],
                                          mask[:, hh, 0, :], ALU.mult).then_inc(scores_masked, 1)

                def norm(b):
                    den, aa, ms, t, u = (sm[:, k, :, :] for k in range(5))
                    n = NV * b
                    dve.wait_ge(o_copied, 2 * b + 2)
                    dve.tensor_tensor(den, o[:, :, :, DH], invn[:, :, :], ALU.mult).then_inc(nv, 1)
                    dve.wait_ge(nv, n + 1)
                    dve.scalar_tensor_tensor(out=t, in0=den, scalar=-1.0, in1=den,
                                             op0=ALU.mult, op1=ALU.max).then_inc(nv, 1)
                    dve.wait_ge(nv, n + 2)
                    dve.tensor_scalar(t, t, 1.0, None, ALU.max).then_inc(nv, 1)
                    dve.wait_ge(nv, n + 3)
                    dve.reciprocal(den, t).then_inc(nv, 1)
                    dve.wait_ge(nv, n + 4)
                    dve.tensor_tensor(aa, den, invn[:, :, :], ALU.mult).then_inc(nv, 1)
                    dve.wait_ge(o_squared, b + 1)
                    dve.wait_ge(nv, n + 5)
                    dve.tensor_reduce(ms, on[:, :, :].rearrange("p s (h d) -> p s h d", h=H), AX_X, ALU.add)\
                        .then_inc(nv, 1)
                    dve.tensor_tensor(u, aa, aa, ALU.mult).then_inc(nv, 1)
                    dve.wait_ge(nv, n + 7)
                    dve.tensor_tensor(t, u, ms, ALU.mult).then_inc(nv, 1)
                    dve.wait_ge(nv, n + 8)
                    dve.tensor_scalar(u, t, 1.0 / DH, EPS, ALU.mult, ALU.add).then_inc(nv, 1)

                def normed(b):
                    n = NV * b
                    dve.wait_ge(ng, b + 1)
                    dve.tensor_tensor(sm[:, 5, :, :], sm[:, 3, :, :], sm[:, 1, :, :], ALU.mult).then_inc(nv, 1)
                    dve.wait_ge(nv, n + 10)
                    dve.tensor_tensor(on[:, :, :].rearrange("p s (h d) -> p (s h) d", h=H),
                                      o[:, :, :, 0:DH].rearrange("p s h d -> p (s h) d"),
                                      bcast(sm[:, 5, :, :].rearrange("p s (h o) -> p (s h) o", o=1),
                                            [P, ST * H, DH]), ALU.mult).then_inc(nv, 1)

                def oT_rest(b):
                    for st in range(ST):
                        dve.wait_ge(oT_hi, ST * b + st + 1)
                        dve.tensor_tensor(oT[:, 1, st, :, :], pps[:, 2 + st, :].rearrange("p (k t) -> p k t", k=KC),
                                          oT[:, 0, st, :, :].bitcast(F32), ALU.subtract).then_inc(oT_lo, 1)

                def out_rows(b):
                    for st in range(ST):
                        row = acc[:, bass.ds(ST * b + st, 1), :].rearrange("p a d -> p (a d)")
                        dve.wait_ge(out_up, ST * b + st + 1)
                        dve.wait_ge(h_made, b + 1)
                        dve.tensor_tensor(row, yps[:, st, :], row, ALU.add).then_inc(r_added, 1)

                def turn(b, after):
                    more = after > 0
                    if more:
                        ln_rows(b + 1)
                    if not (isinstance(b, int) and b == 0):
                        out_rows(b - 1)
                    masks(b, 0, 0, HALF // 2)
                    if more:
                        hT_rest(b + 1, 0)
                    masks(b, 0, HALF // 2)
                    if more:
                        hT_rest(b + 1, 1)
                        rotate(b + 1, 0, 0)
                    masks(b, 1)
                    if more:
                        rotate(b + 1, 0, 1)
                    norm(b)
                    normed(b)
                    if after > 1:
                        ln_stats(b + 2)
                    if more:
                        rotate(b + 1, 1, 0)
                        rotate(b + 1, 1, 1)
                    oT_rest(b)

                def weight_rest(n):
                    dve.wait_ge(w_hi, n + 1)
                    if n < NW - 1:
                        for k in range(KC):
                            last = dve.scalar_tensor_tensor(out=whl[:, 1, n, k, :], in0=wraw[n % 2][:, k, :],
                                                            scalar=rnw[:, k:k + 1],
                                                            in1=whl[:, 0, n, k, :].bitcast(F32),
                                                            op0=ALU.mult, op1=ALU.subtract)
                    else:
                        last = dve.tensor_tensor(whl[:, 1, n, :, :], wraw[n % 2],
                                                 whl[:, 0, n, :, :].bitcast(F32), ALU.subtract)
                    last.then_inc(w_lo, 1)

                ln_stats(0)
                dve.wait_ge(w_loaded[0], 16)
                dve.wait_ge(rnw_loaded, 16)
                weight_rest(0)
                ln_rows(0)
                dve.wait_ge(w_loaded[1], 16)
                weight_rest(1)
                hT_rest(0, 0)
                hT_rest(0, 1)
                weight_rest(2)
                weight_rest(3)
                for loaded in (*rot_loaded, invn_loaded):
                    dve.wait_ge(loaded, 16)
                rotate(0, 0, 0)
                rotate(0, 0, 1)
                weight_rest(4)
                dve.wait_ge(mask_loaded, 16)
                rotate(0, 1, 0)
                rotate(0, 1, 1)
                ln_stats(1)
                turn(0, 2)
                with dve.Fori(1, B - 2) as b:
                    turn(b, 2)
                turn(B - 2, 1)
                turn(B - 1, 0)
                out_rows(B - 1)

            @block.tensor
            def _(pe):
                def hT_turn(b, st):
                    pe.wait_ge(h_made, b + 1)
                    pe.wait_ge((v_copied, g_made)[st], ST * b)
                    for k in range(KC):
                        last = pe.transpose(pps[:, 2 + st, k * P:(k + 1) * P], h[:, st, k * P:(k + 1) * P],
                                            ident[:, :])
                    last.then_inc(hT_up, 1)

                def project(b, st, w):
                    if w == 0:
                        pe.wait_ge(hT_lo, ST * b + st + 1)
                    if w < 2:
                        n = 2 * ST * b + 2 * st + w
                        if not (isinstance(n, int) and n < 2):
                            pe.wait_ge(rot_read, n - 1)
                    else:
                        pe.wait_ge(v_copied if w == 2 else g_made, ST * b + st)
                        pe.wait_ge(hT_lo, ST * b + w - 1)
                    for n, (i, j) in enumerate(PASSES):
                        for k in range(KC):
                            last = pe.matmul(pps[:, w, :], hT[:, i, st, k, :], whl[:, j, w, k, :],
                                             start=(n == 0 and k == 0), stop=(n == 2 and k == KC - 1))
                    last.then_inc(proj_up, 1)

                def qkT_turn(b, u):
                    w, st = u // ST, u % ST
                    pe.wait_ge(qk_rotated, 2 * ST * b + 2 * st + w + 1)
                    if u >= 2:
                        pe.wait_ge(qkT_copied, 2 * ST * b + u - 1)
                    for k in range(KC):
                        last = pe.transpose(xps[:, u % 2, k * P:(k + 1) * P], qk[:, w, st, k * P:(k + 1) * P],
                                            ident[:, :])
                    last.then_inc(qkT_up, 1)

                def scores(b, half):
                    for hh in range(half * HALF, (half + 1) * HALF):
                        if hh < 2:
                            pe.wait_ge(qkT_copied, 2 * ST * b + 2 * ST)
                        else:
                            pe.wait_ge(scores_masked, H * b + hh - 1)
                        g, k = hh % HG, hh // HG
                        pe.matmul(xps[:, hh % 2, 0:S], kT[:, g, k, 0:P], qT[:, k, :],
                                  start=True, stop=True)
                        pe.matmul(xps[:, hh % 2, S:S + P], kT[:, g, k, P:S], qT[:, k, P:S],
                                  start=True, stop=True).then_inc(scores_up, 1)

                def values(b, half):
                    pe.wait_ge(scores_masked, H * b + (half + 1) * HALF)
                    pe.wait_ge(v_copied, ST * b + ST)
                    if half == 0:
                        pe.wait_ge(r_added, ST * b)
                    else:
                        pe.wait_ge(o_copied, 2 * b + 1)
                    n = DH + 1
                    for j in range(HALF):
                        hh = half * HALF + j
                        pe.matmul(yps[:, 0, j * n:(j + 1) * n], scm[:, j, 0:P], v[:, 0, hh, :],
                                  start=True, stop=True)
                        pe.matmul(yps[:, 1, j * n:(j + 1) * n], scm[:, j, P:2 * P], v[:, 0, hh, :],
                                  start=True, stop=False)
                        last = pe.matmul(yps[:, 1, j * n:(j + 1) * n], scm[:, j, 2 * P:3 * P], v[:, 1, hh, :],
                                         start=False, stop=True)
                    last.then_inc(o_up, 1)

                def oT_turn(b, more):
                    pe.wait_ge(on_gated, b + 1)
                    for st in range(ST):
                        pe.wait_ge((v_copied, g_made)[st], ST * (b + 1 + more))
                        for k in range(KC):
                            last = pe.transpose(pps[:, 2 + st, k * P:(k + 1) * P], on[:, st, k * P:(k + 1) * P],
                                                ident[:, :])
                        last.then_inc(oT_up, 1)

                def out_proj(b):
                    pe.wait_ge(o_copied, 2 * b + 2)
                    for st in range(ST):
                        pe.wait_ge(oT_lo, ST * b + st + 1)
                        for n, (i, j) in enumerate(PASSES):
                            for k in range(KC):
                                last = pe.matmul(yps[:, st, :], oT[:, i, st, k, :], whl[:, j, 4, k, :],
                                                 start=(n == 0 and k == 0), stop=(n == 2 and k == KC - 1))
                        last.then_inc(out_up, 1)

                def turn(b, more):
                    for u in range(2 * ST):
                        qkT_turn(b, u)
                    if not (isinstance(b, int) and b == 0):
                        out_proj(b - 1)
                    if more:
                        hT_turn(b + 1, 0)
                        hT_turn(b + 1, 1)
                    scores(b, 0)
                    if more:
                        project(b + 1, 0, 0)
                    values(b, 0)
                    scores(b, 1)
                    if more:
                        project(b + 1, 0, 1)
                    values(b, 1)
                    if more:
                        project(b + 1, 0, 2)
                        project(b + 1, 0, 3)
                        for w in range(4):
                            project(b + 1, 1, w)
                    oT_turn(b, more)

                pe.wait_ge(ident_loaded, 16)
                for st in range(ST):
                    hT_turn(0, st)
                for st in range(ST):
                    for w in range(4):
                        pe.wait_ge(w_lo, w + 1)
                        project(0, st, w)
                pe.wait_ge(w_lo, NW)
                turn(0, True)
                with pe.Fori(1, B - 1) as b:
                    turn(b, True)
                turn(B - 1, False)
                out_proj(B - 1)


def columns_phase(nc, weight, acc, ident, cols):
    with ExitStack() as ctx:
        def sb(name, shape, dt=F32):
            return ctx.enter_context(nc.sbuf_tensor(name + "_sb", shape, dt))

        def sem(name):
            return ctx.enter_context(nc.semaphore(name))

        sq = sb("c_squares", [P, D])
        ms = sb("c_sums", [P, 2])
        sc = sb("c_scales", [P, 3, 2])
        consts = sb("c_consts", [P, 3])
        h = sb("c_rows", [P, 2, D])
        w = sb("c_weight", [P, D])
        xps = ctx.enter_context(nc.psum_tensor("c_ps", [P, 2, 512], F32))

        const_set = sem("c_const_set")
        w_loaded = sem("c_w_loaded")
        squared = sem("c_squared")
        act_passed = sem("c_act_passed")
        sc_step = sem("c_scale_step")
        h_made = sem("c_h_made")
        h_up = sem("c_h_up")
        hi_made = sem("c_hi_made")
        lo_made = sem("c_lo_made")

        def rows(t):
            return acc[:, bass.ds(t, 1), :].rearrange("p a d -> p (a d)")

        def place(half, t):
            return cols[:, half, :, bass.ds(P * t, P)]

        with nc.Block() as block:
            @block.sync
            def _(sp):
                sp.dma_start(w[:, :], weight.partition_broadcast(P)).then_inc(w_loaded, 16)

            @block.gpsimd
            def _(pool):
                for n, value in enumerate((1.0 / D, EPS, -0.5)):
                    pool.memset(consts[:, n:n + 1], value).then_inc(const_set, 1)
                pool.wait_ge(const_set, 3)

                def scale(t, par):
                    s = [sc[:, k, par:par + 1] for k in range(3)]
                    pool.wait_ge(squared, t + 1)
                    pool.tensor_tensor(s[0], ms[:, par:par + 1], consts[:, 0:1], ALU.mult).then_inc(sc_step, 1)
                    pool.wait_ge(sc_step, 3 * t + 1)
                    pool.tensor_tensor(s[1], s[0], consts[:, 1:2], ALU.add).then_inc(sc_step, 1)
                    pool.wait_ge(sc_step, 3 * t + 2)
                    pool.tensor_tensor(s[2], s[1], consts[:, 2:3], ALU.pow).then_inc(sc_step, 1)

                scale(0, 0)
                scale(1, 1)
                with pool.Fori(1, NT // 2) as i:
                    for par in range(2):
                        pool.wait_ge(h_made, 2 * i + par - 1)
                        scale(2 * i + par, par)

            @block.scalar
            def _(act):
                def square(t, par):
                    act.activation(sq[:, :], rows(t), ACT.Square, accum_out=ms[:, par:par + 1])\
                       .then_inc(squared, 1)

                def hi(t, par):
                    act.wait_ge(h_up, t + 1).then_inc(act_passed, 1)
                    act.activation(place(0, t), xps[:, par, :].rearrange("p (k t) -> p k t", k=KC),
                                   ACT.Copy).then_inc(hi_made, 1)

                square(0, 0)
                act.wait_ge(squared, 1)
                square(1, 1)
                with act.Fori(0, NT // 2 - 1) as i:
                    for par in range(2):
                        act.wait_ge(squared, 2 * i + par + 2).then_inc(act_passed, 1)
                        act.wait_ge(sc_step, 3 * (2 * i + par) + 1).then_inc(act_passed, 1)
                        square(2 * i + par + 2, par)
                        hi(2 * i + par, par)
                hi(NT - 2, 0)
                hi(NT - 1, 1)

            @block.vector
            def _(dve):
                def turn(t, par, first=False):
                    dve.wait_ge(sc_step, 3 * t + 3)
                    if not first:
                        dve.wait_ge(h_up, t - 1)
                    dve.scalar_tensor_tensor(out=h[:, par, :], in0=rows(t), scalar=sc[:, 2, par:par + 1],
                                             in1=w[:, :], op0=ALU.mult, op1=ALU.mult).then_inc(h_made, 1)

                def lo(t, par):
                    dve.wait_ge(hi_made, t + 1)
                    dve.tensor_tensor(place(1, t), xps[:, par, :].rearrange("p (k t) -> p k t", k=KC),
                                      place(0, t).bitcast(F32), ALU.subtract).then_inc(lo_made, 1)

                dve.wait_ge(w_loaded, 16)
                turn(0, 0, True)
                turn(1, 1, True)
                with dve.Fori(0, NT // 2 - 1) as i:
                    for par in range(2):
                        lo(2 * i + par, par)
                        turn(2 * i + par + 2, par)
                lo(NT - 2, 0)
                lo(NT - 1, 1)

            @block.tensor
            def _(pe):
                def turn(t, par, first=False):
                    pe.wait_ge(h_made, t + 1)
                    if not first:
                        pe.wait_ge(lo_made, t - 1)
                    for k in range(KC):
                        last = pe.transpose(xps[:, par, k * P:(k + 1) * P], h[:, par, k * P:(k + 1) * P],
                                            ident[:, :])
                    last.then_inc(h_up, 1)

                turn(0, 0, True)
                turn(1, 1, True)
                with pe.Fori(1, NT // 2) as i:
                    for par in range(2):
                        turn(2 * i + par, par)


def ffn_wkv_phase(nc, a, acc, ident, cols, cw, mask, xn):
    FS = F // I
    BB = TB // S
    QS = FS // BB
    LAG = BB
    NQ = NB * BB
    W1 = KC * I
    W2 = IC * D
    BR = 32

    with ExitStack() as ctx:
        def sb(name, shape, dt=F32):
            return ctx.enter_context(nc.sbuf_tensor(f"k_{name}_sb", shape, dt))

        def sem(name):
            return ctx.enter_context(nc.semaphore(f"k_{name}"))

        raw1 = sb("w1_raw", [P, W1])
        raw2 = sb("w2_raw", [P, W2])
        w1h = sb("w1_halves", [P, 2, 2, W1], F32R)
        w2h = sb("w2_halves", [P, 2, 2, W2], F32R)
        hid = sb("hidden", [P, IC, TB])
        hh = sb("hidden_halves", [P, 2, 2, IC, TB], F32R)
        b1 = sb("fc1_b", [P, F // P])
        b2h = sb("fc2_b_halves", [BR + 1, D], F32R)
        oneh = sb("one_rows_r", [BR + 1, P], F32R)
        xin = sb("x", [P, ST, D])
        kT = sb("kT", [P, KC, S])
        vT = sb("vT", [P, KC, S])
        pp = sb("pp", [P, KC, S + 1])
        av = sb("aa", [P, KC, S + 1])
        bv = sb("bb", [P, KC, S + 1])
        e1b = sb("e1b", [P, KC, S])
        e2b = sb("e2b", [P, KC, S])
        e1 = sb("e1", [P, KC, S])
        e2 = sb("e2", [P, KC, S])
        t1 = sb("t1", [P, KC, S])
        kr = [t[:, :, :].rearrange("p k s -> p (k s)").rearrange("p (s d) -> p s d", s=ST) for t in (e2, e1)]
        xT = t1[:, :, :].rearrange("p k s -> p (k s)").rearrange("p (s k t) -> p s k t", s=ST, k=KC)
        b2 = e1b[0:BR + 1, 0:D // S, :].rearrange("p k s -> p (k s)")
        one = e2[0:BR + 1, 0, 0:P]
        decay = sb("decay", [P, KC])
        dexp = sb("decay_exp", [P, KC])
        u = sb("first", [P, KC])
        st6 = sb("bn6", [P, 2, ST, 6])
        mv = sb("mean_var", [P, 2, ST, 2])
        rstd = sb("rstd", [P, 2, 2, ST])
        consts = sb("consts", [P, 2, ST])
        gw = sb("gate_w", [P, KC, NE])
        ebias = sb("expert_bias", [P, NE])
        ones = sb("ones", [P, NE])
        score = sb("score", [P, ST, NE])
        biased = sb("biased", [P, ST, NE])
        top8 = sb("top8", [P, ST, 8])
        over = sb("over", [P, ST, NE])
        ties = sb("ties", [P, ST, NE])
        rank = sb("rank", [P, ST, NE])
        chosen = sb("chosen", [P, ST, NE])
        nover = sb("nover", [P, ST])
        total = sb("total", [P, ST])

        gps = ctx.enter_context(nc.psum_tensor("k_g_ps", [P, IC, TB], F32))
        dps = ctx.enter_context(nc.psum_tensor("k_d_ps", [P, BT, D], F32))
        xps = ctx.enter_context(nc.psum_tensor("k_x_ps", [P, ST, 512], F32))

        const_loaded = sem("const_loaded")
        const_set = sem("const_set")
        act_passed = sem("act_passed")
        passed = sem("passed")
        w1_loaded = sem("w1_loaded")
        w1_hi = sem("w1_hi")
        w1_lo = sem("w1_lo")
        w2_loaded = sem("w2_loaded")
        w2_hi = sem("w2_hi")
        w2_lo = sem("w2_lo")
        b2_hi = sem("b2_hi")
        b2_lo = sem("b2_lo")
        first_up = sem("first_up")
        hid_made = sem("hid_made")
        hid_hi = sem("hid_hi")
        hid_lo = sem("hid_lo")
        down_up = sem("down_up")
        added = sem("added")
        x_loaded = sem("x_loaded")
        v_loaded = sem("v_loaded")
        x_added = sem("x_added")
        ln1_stats = sem("ln1_stats")
        ln1_step = sem("ln1_step")
        ln2_stats = sem("ln2_stats")
        ln2_step = sem("ln2_step")
        rows_made = sem("rows_made")
        rows_up = sem("rows_up")
        kT_copied = sem("kT_copied")
        decay_exp = sem("decay_exp")
        pp_made = sem("pp_made")
        d1_made = sem("d1_made")
        d2_made = sem("d2_made")
        q_made = sem("q_made")
        d3_made = sem("d3_made")
        d4_made = sem("d4_made")
        exps = sem("exps")
        bv_made = sem("bv_made")
        bb_made = sem("bb_made")
        aa_made = sem("aa_made")
        n2_made = sem("n2_made")
        d_made = sem("d_made")
        y_step = sem("y_step")
        y_made = sem("y_made")
        y_up = sem("y_up")
        y_added = sem("y_added")
        rows2_made = sem("rows2_made")
        cols_up = sem("cols_up")
        xT_copied = sem("xT_copied")
        xn_stored = sem("xn_stored")
        logits_up = sem("logits_up")
        logits_exp = sem("logits_exp")
        route = sem("route")

        xd = a["x"].rearrange("(b s p) d -> b p s d", p=P, s=ST)
        RS = 2 + 10 * ST
        def known(v):
            return isinstance(v, int)

        def rows(b, st):
            return acc[:, bass.ds(ST * b + st, 1), :].rearrange("p a d -> p (a d)")

        xn_rows = xn.rearrange("(b s p) d -> b p s d", p=P, s=ST)

        with nc.Block() as block:
            @block.sync
            def _(sp):
                def load_w(n, e1_, e2_):
                    if e1_ is not None:
                        sp.wait_ge(w1_lo, n + 2)
                        sp.dma_start(raw1[:, :], a["ffn_w"][e1_, :, 0:W1]).then_inc(w1_loaded, 16)
                    if e2_ is not None:
                        sp.wait_ge(w2_lo, n + 1)
                        sp.dma_start(raw2[:, :], a["ffn_w"][e2_, :, W1:W1 + W2]).then_inc(w2_loaded, 16)

                def load_x(b):
                    if not (known(b) and b == 0):
                        sp.wait_ge(x_added, ST * b)
                    sp.dma_start(xin[:, :, :], xd[b]).then_inc(x_loaded, 16)

                def load_v(b):
                    if not (known(b) and b == 0):
                        sp.wait_ge(n2_made, b)
                    sp.dma_start(vT[:, :, :], a["ctx"][b]).then_inc(v_loaded, 16)

                def store_xn(b):
                    sp.wait_ge(rows2_made, ST * (b + 1))
                    sp.dma_start(xn_rows[b], kr[1]).then_inc(xn_stored, 16)

                def quarter(m, hb):
                    for s in range(QS):
                        e = QS * hb + s
                        load_w(QS * m + s, (e + 2) % FS, (e + 1) % FS)
                        if s == 0 and not (known(m) and m == LAG):
                            store_xn(m - LAG - 1)
                        if s == 1:
                            load_x(m - LAG + 1)
                        if s == 3:
                            load_v(m - LAG + 1)

                sp.dma_start(raw1[:, :], a["ffn_w"][0, :, 0:W1]).then_inc(w1_loaded, 16)
                sp.dma_start(raw2[:, :], a["ffn_w"][0, :, W1:W1 + W2]).then_inc(w2_loaded, 16)
                loads = ((b1[:, :], a["fc1_b"]), (b2[0:1, :], a["fc2_b"]),
                         (b2[BR:BR + 1, :], a["fc2_b"]), (decay[:, :], a["time_decay"]),
                         (u[:, :], a["time_first"]), (gw[:, :, :], a["gate_w"]),
                         (ebias[:, :], a["expert_bias"].partition_broadcast(P)))
                for n, (dst, src) in enumerate(loads):
                    sp.dma_start(dst, src).then_inc(const_loaded, 16)
                    sp.wait_ge(const_loaded, 16 * (n + 1))
                sp.wait_ge(w1_lo, 1)
                sp.dma_start(raw1[:, :], a["ffn_w"][1, :, 0:W1]).then_inc(w1_loaded, 16)
                with sp.Fori(0, QS * LAG - 2) as e:
                    load_w(e, e + 2, e + 1)
                load_x(0)
                load_v(0)
                load_w(FS - 2, 0, FS - 1)
                load_w(FS - 1, 1, 0)
                for hb in range(BB):
                    quarter(LAG + hb, hb)
                with sp.Fori(2, NB - 1) as j:
                    for hb in range(BB):
                        quarter(BB * j + hb, hb)
                for s in range(QS):
                    load_w(QS * (NQ - 2) + s, s + 2, s + 1)
                    if s == 0:
                        store_xn(NQ - LAG - 3)
                    if s == 1:
                        load_x(NQ - LAG - 1)
                    if s == 3:
                        load_v(NQ - LAG - 1)
                for s in range(QS):
                    e = QS + s
                    load_w(QS * (NQ - 1) + s, e + 2 if e + 2 < FS else None, e + 1 if e + 1 < FS else None)
                    if s == 0:
                        store_xn(NQ - LAG - 2)
                    if s == 1:
                        load_x(NQ - LAG)
                    if s == 3:
                        load_v(NQ - LAG)
                store_xn(B - LAG - 1)
                for b in range(B - LAG + 1, B):
                    load_x(b)
                    load_v(b)
                    store_xn(b - 1)
                store_xn(B - 1)
                sp.wait_ge(xn_stored, 16 * B)

            @block.gpsimd
            def _(pool):
                for dst, value in ((consts[:, 0, :], EPS), (consts[:, 1, :], -0.5), (ones[:, :], 1.0),
                                   (pp[:, :, 0:1], NEG), (av[:, :, 0:1], 0.0), (bv[:, :, 0:1], 0.0),
                                   (one[:, :], 1.0), (b2h[:, :].bitcast(F32), 0.0)):
                    pool.memset(dst, value).then_inc(const_set, 1)
                pool.wait_ge(const_set, 8)

                def w1_rest(n, par):
                    pool.wait_ge(w1_hi, n + 1)
                    pool.tensor_tensor(w1h[:, par, 1, :], raw1[:, :], w1h[:, par, 0, :].bitcast(F32),
                                       ALU.subtract).then_inc(w1_lo, 1)

                def w2_rest(n, par):
                    pool.wait_ge(w2_hi, n + 1)
                    pool.tensor_tensor(w2h[:, par, 1, :], raw2[:, :], w2h[:, par, 0, :].bitcast(F32),
                                       ALU.subtract).then_inc(w2_lo, 1)

                def hidden_rest(n, par):
                    for c in range(IC):
                        pool.wait_ge(hid_hi, IC * n + c + 1)
                        pool.tensor_tensor(hh[:, par, 1, c, :], hid[:, c, :], hh[:, par, 0, c, :].bitcast(F32),
                                           ALU.subtract).then_inc(hid_lo, 1)

                def scales(b, ln, stats, step):
                    pool.wait_ge(stats, 2 * ST * (b + 1))
                    pool.tensor_tensor(rstd[:, ln, 0, :], mv[:, ln, :, 1], consts[:, 0, :], ALU.add).then_inc(step, 1)
                    pool.wait_ge(step, 2 * b + 1)
                    pool.tensor_tensor(rstd[:, ln, 1, :], rstd[:, ln, 0, :], consts[:, 1, :], ALU.pow).then_inc(step, 1)

                def differences(b):
                    pool.wait_ge(pp_made, b + 1)
                    pool.tensor_tensor(e2b[:, :, :], kT[:, :, :], pp[:, :, 1:S + 1], ALU.subtract).then_inc(d2_made, 1)

                def differences_out(b):
                    pool.wait_ge(d4_made, b + 1)
                    pool.tensor_tensor(e1[:, :, :], pp[:, :, 0:S], e1[:, :, :], ALU.subtract).then_inc(d3_made, 1)

                def values(b):
                    pool.wait_ge(v_loaded, 16 * (b + 1))
                    pool.wait_ge(exps, 4 * b + 4)
                    pool.tensor_tensor(kT[:, :, :], e2b[:, :, :], vT[:, :, :], ALU.mult).then_inc(bv_made, 1)

                def values_out(b):
                    if not (known(b) and b == 0):
                        pool.wait_ge(logits_up, b)
                    pool.tensor_tensor(t1[:, :, :], e2[:, :, :], vT[:, :, :], ALU.mult).then_inc(n2_made, 1)

                def denominator(b):
                    pool.wait_ge(bb_made, b + 1)
                    pool.wait_ge(aa_made, b + 1)
                    pool.tensor_tensor(e1b[:, :, :], e1[:, :, :], bv[:, :, 0:S], ALU.mult).then_inc(d_made, 1)
                    pool.wait_ge(d_made, 2 * b + 1)
                    pool.tensor_tensor(e1b[:, :, :], e1b[:, :, :], e2[:, :, :], ALU.add).then_inc(d_made, 1)

                def slot(m, s, left=None):
                    n = QS * m + s
                    w = not (known(m) and m < LAG)
                    b = m - LAG
                    if w and s == 2:
                        values(b)
                    if w and s == 3:
                        denominator(b)
                    if left is None or left > 2:
                        w1_rest(n + 2, s % 2)
                    if left is None or left > 1:
                        w2_rest(n + 1, (s + 1) % 2)
                    if w and s == 0:
                        scales(b, 0, ln1_stats, ln1_step)
                    if w and s == 1:
                        differences(b)
                    if left is None or left > 1:
                        hidden_rest(n + 1, (s + 1) % 2)
                    if w and s == 0 and not (known(b) and b == 0):
                        scales(b - 1, 1, ln2_stats, ln2_step)
                    if w and s == 1:
                        differences_out(b)
                    if w and s == 2:
                        values_out(b)

                w1_rest(0, 0)
                w2_rest(0, 0)
                w1_rest(1, 1)
                hidden_rest(0, 0)
                for m in range(LAG + 1):
                    for s in range(QS):
                        slot(m, s)
                with pool.Fori(LAG + 1, NQ - 1) as m:
                    for s in range(QS):
                        slot(m, s)
                for s in range(QS):
                    slot(NQ - 1, s, QS - s)
                for b in range(B - LAG, B):
                    scales(b, 0, ln1_stats, ln1_step)
                    scales(b - 1, 1, ln2_stats, ln2_step)
                    differences(b)
                    differences_out(b)
                    values(b)
                    values_out(b)
                    denominator(b)
                scales(B - 1, 1, ln2_stats, ln2_step)

            @block.scalar
            def _(act):
                def w1_first(n, par):
                    act.wait_ge(w1_loaded, 16 * (n + 1))
                    if not (known(n) and n < 2):
                        act.wait_ge(first_up, IC * (n - 1))
                    act.activation(w1h[:, par, 0, :], raw1[:, :], ACT.Copy).then_inc(w1_hi, 1)

                def w2_first(n, par):
                    act.wait_ge(w2_loaded, 16 * (n + 1))
                    if not (known(n) and n < 2):
                        act.wait_ge(down_up, BT * (n - 1))
                    act.activation(w2h[:, par, 0, :], raw2[:, :], ACT.Copy).then_inc(w2_hi, 1)

                def hidden(n, s, hb):
                    for c in range(IC):
                        act.wait_ge(first_up, IC * n + c + 1)
                        if not (known(n) and n == 0):
                            act.wait_ge(hid_lo, IC * (n - 1) + c + 1)
                        act.wait_ge(const_loaded, 112).then_inc(act_passed, 1)
                        act.activation(hid[:, c, :], gps[:, c, :], ACT.Gelu_apprx_tanh,
                                       bias=b1[:, bass.ds(IC * QS * hb + IC * s + c, 1)]).then_inc(hid_made, 1)
                    for c in range(IC):
                        act.wait_ge(hid_made, IC * n + c + 1)
                        if not (known(n) and n < 2):
                            act.wait_ge(down_up, BT * (n - 1))
                        act.activation(hh[:, s % 2, 0, c, :], hid[:, c, :], ACT.Copy).then_inc(hid_hi, 1)

                def k_columns(b):
                    if not (known(b) and b == 0):
                        act.wait_ge(aa_made, b)
                    for st in range(ST):
                        act.wait_ge(rows_up, ST * b + st + 1)
                        act.activation(kT[:, :, st * P:(st + 1) * P],
                                       xps[:, st, :].rearrange("p (k t) -> p k t", k=KC), ACT.Copy)\
                           .then_inc(kT_copied, 1)

                def x_columns(b):
                    act.wait_ge(y_made, b + 1)
                    for st in range(ST):
                        act.wait_ge(cols_up, ST * b + st + 1)
                        act.activation(xT[:, st, :, :], xps[:, st, :].rearrange("p (k t) -> p k t", k=KC),
                                       ACT.Copy).then_inc(xT_copied, 1)

                def logit_exps(b):
                    act.wait_ge(logits_up, b + 1)
                    act.activation(score[:, :, :], xps[:, 0, 0:ST * NE].rearrange("p (s e) -> p s e", s=ST),
                                   ACT.Exp, scale=-1.0).then_inc(logits_exp, 1)

                def wkv_exps(b):
                    for ready, buf in ((d1_made, e1b), (d4_made, e2), (d2_made, e2b), (d3_made, e1)):
                        act.wait_ge(ready, b + 1)
                        act.activation(buf[:, :, :], buf[:, :, :], ACT.Exp).then_inc(exps, 1)

                def slot(m, s, hb, left=None):
                    n = QS * m + s
                    w = not (known(m) and m < LAG)
                    b = m - LAG
                    if left is None or left > 2:
                        w1_first(n + 2, s % 2)
                    if left is None or left > 1:
                        w2_first(n + 1, (s + 1) % 2)
                        hidden(n + 1, (s + 1) % QS, hb if s < QS - 1 else (hb + 1) % BB)
                    if w and s == 0:
                        k_columns(b)
                    if w and s == 1:
                        if not (known(b) and b == 0):
                            x_columns(b - 1)
                        wkv_exps(b)
                        if not (known(b) and b == 0):
                            logit_exps(b - 1)

                act.wait_ge(const_loaded, 112)
                act.activation(dexp[:, :], decay[:, :], ACT.Exp).then_inc(decay_exp, 1)
                act.wait_ge(const_set, 8)
                for row in (0, BR):
                    act.activation(b2h[row:row + 1, :], b2[row:row + 1, :], ACT.Copy).then_inc(b2_hi, 1)
                act.activation(oneh[:, :], one[:, :], ACT.Copy).then_inc(b2_hi, 1)
                w1_first(0, 0)
                w2_first(0, 0)
                w1_first(1, 1)
                hidden(0, 0, 0)
                for m in range(LAG + BB):
                    for s in range(QS):
                        slot(m, s, m % BB)
                with act.Fori(2, NB - 1) as j:
                    for hb in range(BB):
                        for s in range(QS):
                            slot(BB * j + hb, s, hb)
                for hb in range(BB):
                    for s in range(QS):
                        slot(NQ - BB + hb, s, hb, FS - QS * hb - s)
                for b in range(B - LAG, B):
                    k_columns(b)
                    x_columns(b - 1)
                    wkv_exps(b)
                    logit_exps(b - 1)
                x_columns(B - 1)
                logit_exps(B - 1)

            @block.vector
            def _(dve):
                def stats(b, ln, sem_):
                    for st in range(ST):
                        dve.bn_stats(st6[:, ln, st, :], rows(b, st)).then_inc(sem_, 1)
                    dve.wait_ge(sem_, 2 * ST * b + ST).then_inc(passed, 1)
                    for st in range(ST):
                        dve.bn_aggr(mv[:, ln, st, :], st6[:, ln, st, :]).then_inc(sem_, 1)

                def ln_rows(b, ln, step, made):
                    dve.wait_ge(step, 2 * b + 2)
                    for st in range(ST):
                        dve.tensor_scalar(kr[ln][:, st, :], rows(b, st), mv[:, ln, st, 0:1],
                                          rstd[:, ln, 1, st:st + 1], ALU.subtract, ALU.mult).then_inc(made, 1)

                def x1(b):
                    dve.wait_ge(x_loaded, 16 * (b + 1))
                    for st in range(ST):
                        dve.tensor_tensor(rows(b, st), rows(b, st), xin[:, st, :], ALU.add).then_inc(x_added, 1)
                    dve.wait_ge(x_added, ST * b + ST).then_inc(passed, 1)
                    stats(b, 0, ln1_stats)

                def y_rows(b):
                    for st in range(ST):
                        dve.wait_ge(y_up, ST * b + st + 1)
                        dve.tensor_tensor(rows(b, st), xps[:, st, :], rows(b, st), ALU.add).then_inc(y_added, 1)
                    dve.wait_ge(y_added, ST * b + ST).then_inc(passed, 1)
                    stats(b, 1, ln2_stats)

                def maxima(b):
                    dve.wait_ge(kT_copied, ST * b + ST)
                    for c in range(KC):
                        last = dve.tensor_tensor_scan(pp[:, c, 1:S + 1], bcast(dexp[:, c:c + 1], [P, S]),
                                                      kT[:, c, :], NEG, ALU.add, ALU.max)
                    last.then_inc(pp_made, 1)
                    dve.wait_ge(pp_made, b + 1).then_inc(passed, 1)
                    if not (known(b) and b == 0):
                        dve.wait_ge(cols_up, ST * b)
                        dve.wait_ge(xn_stored, 16 * b)
                    for c in range(KC):
                        last = dve.scalar_tensor_tensor(out=e1[:, c, :], in0=kT[:, c, :], scalar=u[:, c:c + 1],
                                                        in1=pp[:, c, 0:S], op0=ALU.add, op1=ALU.max)
                    last.then_inc(q_made, 1)
                    for c in range(KC):
                        last = dve.scalar_tensor_tensor(out=e1b[:, c, :], in0=pp[:, c, 0:S],
                                                        scalar=dexp[:, c:c + 1], in1=pp[:, c, 1:S + 1],
                                                        op0=ALU.add, op1=ALU.subtract)
                    last.then_inc(d1_made, 1)
                    dve.wait_ge(q_made, b + 1)
                    for c in range(KC):
                        last = dve.scalar_tensor_tensor(out=e2[:, c, :], in0=kT[:, c, :], scalar=u[:, c:c + 1],
                                                        in1=e1[:, c, :], op0=ALU.add, op1=ALU.subtract)
                    last.then_inc(d4_made, 1)

                def bb_scan(b):
                    dve.wait_ge(exps, 4 * b + 3)
                    for c in range(KC):
                        last = dve.tensor_tensor_scan(bv[:, c, 1:S + 1], e1b[:, c, :], e2b[:, c, :], 0.0,
                                                      ALU.mult, ALU.add)
                    last.then_inc(bb_made, 1)

                def aa_scan(b):
                    dve.wait_ge(bv_made, b + 1)
                    for c in range(KC):
                        last = dve.tensor_tensor_scan(av[:, c, 1:S + 1], e1b[:, c, :], kT[:, c, :], 0.0,
                                                      ALU.mult, ALU.add)
                    last.then_inc(aa_made, 1)

                def quotient(b):
                    dve.wait_ge(aa_made, b + 1)
                    dve.wait_ge(d_made, 2 * b + 1)
                    dve.tensor_tensor(e1[:, :, :], e1[:, :, :], av[:, :, 0:S], ALU.mult).then_inc(y_step, 1)
                    dve.wait_ge(n2_made, b + 1)
                    dve.wait_ge(y_step, 3 * b + 1)
                    dve.tensor_tensor(e1[:, :, :], e1[:, :, :], t1[:, :, :], ALU.add).then_inc(y_step, 1)
                    dve.wait_ge(d_made, 2 * b + 2)
                    dve.reciprocal(e1b[:, :, :], e1b[:, :, :]).then_inc(y_step, 1)
                    dve.wait_ge(y_step, 3 * b + 3)
                    dve.tensor_tensor(e1[:, :, :], e1[:, :, :], e1b[:, :, :], ALU.mult).then_inc(y_made, 1)

                def routed(b):
                    n = RS * b
                    dve.wait_ge(logits_exp, b + 1)
                    dve.tensor_scalar(score[:, :, :], score[:, :, :], 1.0, None, ALU.add).then_inc(route, 1)
                    dve.wait_ge(route, n + 1)
                    dve.reciprocal(score[:, :, :], score[:, :, :]).then_inc(route, 1)
                    n += 2

                    def stage(k, op):
                        dve.wait_ge(route, n + ST * k).then_inc(passed, 1)
                        for st in range(ST):
                            op(st).then_inc(route, 1)

                    stage(0, lambda st: dve.tensor_tensor(biased[:, st, :], score[:, st, :], ebias[:, :], ALU.add))
                    stage(1, lambda st: dve.max(top8[:, st, :], biased[:, st, :]))
                    stage(2, lambda st: dve.tensor_scalar(over[:, st, :], biased[:, st, :],
                                                          top8[:, st, TOPK - 1:TOPK], 0.0, ALU.is_gt, ALU.add,
                                                          accum_out=nover[:, st:st + 1]))
                    stage(3, lambda st: dve.tensor_scalar(ties[:, st, :], biased[:, st, :],
                                                          top8[:, st, TOPK - 1:TOPK], None, ALU.is_equal))
                    stage(4, lambda st: dve.tensor_tensor_scan(rank[:, st, :], ones[:, :], ties[:, st, :],
                                                               nover[:, st:st + 1], ALU.mult, ALU.add))
                    stage(5, lambda st: dve.scalar_tensor_tensor(out=chosen[:, st, :], in0=rank[:, st, :],
                                                                 scalar=float(TOPK), in1=ties[:, st, :],
                                                                 op0=ALU.is_le, op1=ALU.mult))
                    def kept(st):
                        return mask[:, :, bass.ds(ST * b + st, 1)].rearrange("p e o -> p (e o)")

                    stage(6, lambda st: dve.tensor_tensor(kept(st), over[:, st, :], chosen[:, st, :], ALU.add))
                    stage(7, lambda st: dve.scalar_tensor_tensor(out=chosen[:, st, :], in0=kept(st), scalar=1.0,
                                                                 in1=score[:, st, :], op0=ALU.mult, op1=ALU.mult,
                                                                 accum_out=total[:, st:st + 1]))
                    stage(8, lambda st: dve.reciprocal(total[:, st:st + 1], total[:, st:st + 1]))
                    stage(9, lambda st: dve.tensor_scalar(
                        cw[:, :, bass.ds(ST * b + st, 1)].rearrange("p e o -> p (e o)"),
                        chosen[:, st, :], total[:, st:st + 1], None, ALU.mult))

                def add(n, j):
                    if not (known(n) and n < 1):
                        dve.wait_ge(added, BT * n)
                    for t in range(BT):
                        dve.wait_ge(down_up, BT * n + t + 1)
                        row = acc[:, bass.ds(BT * j + t, 1), :].rearrange("p a d -> p (a d)")
                        dve.tensor_tensor(row, dps[:, t, :], row, ALU.add).then_inc(added, 1)

                def slot(m, s, j, hb):
                    n = QS * m + s
                    if not (known(n) and n == 0):
                        add(n - 1, j if (s or hb) else j - 1)
                    if known(m) and m < LAG:
                        return
                    b = m - LAG
                    before = not (known(b) and b == 0)
                    if s == 0:
                        dve.wait_ge(added, BT * n)
                        x1(b)
                        if before:
                            y_rows(b - 1)
                        ln_rows(b, 0, ln1_step, rows_made)
                        if before:
                            ln_rows(b - 1, 1, ln2_step, rows2_made)
                    elif s == 1:
                        maxima(b)
                    elif s == 2:
                        bb_scan(b)
                        if before:
                            routed(b - 1)
                        aa_scan(b)
                    else:
                        quotient(b)

                dve.wait_ge(decay_exp, 1)
                dve.wait_ge(const_loaded, 112)
                dve.wait_ge(const_set, 8)
                dve.tensor_scalar(dexp[:, :], dexp[:, :], -1.0, None, ALU.mult).then_inc(passed, 1)
                dve.wait_ge(b2_hi, 3)
                dve.tensor_tensor(b2h[BR:BR + 1, :], b2[BR:BR + 1, :], b2h[BR:BR + 1, :].bitcast(F32),
                                  ALU.subtract).then_inc(b2_lo, 1)
                dve.wait_ge(passed, 1)
                for m in range(2 * LAG):
                    for s in range(QS):
                        slot(m, s, m // BB, m % BB)
                with dve.Fori(2, NB) as j:
                    for hb in range(BB):
                        for s in range(QS):
                            slot(BB * j + hb, s, j, hb)
                add(QS * NQ - 1, NB - 1)
                dve.wait_ge(added, BT * QS * NQ)
                for b in range(B - LAG, B):
                    x1(b)
                    y_rows(b - 1)
                    ln_rows(b, 0, ln1_step, rows_made)
                    ln_rows(b - 1, 1, ln2_step, rows2_made)
                    maxima(b)
                    bb_scan(b)
                    routed(b - 1)
                    aa_scan(b)
                    quotient(b)
                y_rows(B - 1)
                ln_rows(B - 1, 1, ln2_step, rows2_made)
                routed(B - 1)

            @block.tensor
            def _(pe):
                def w1(par, half, k, c):
                    return w1h[:, par, half, k * I + c * P:k * I + (c + 1) * P]

                def w2(par, half, c):
                    return w2h[:, par, half, c * D:(c + 1) * D]

                def first(n, par, j):
                    pe.wait_ge(w1_lo, n + 1)
                    for c in range(IC):
                        if not (known(n) and n == 0):
                            pe.wait_ge(hid_made, IC * (n - 1) + c + 1)
                        for m, (x, y) in enumerate(PASSES):
                            for k in range(KC):
                                last = pe.matmul(gps[:, c, :], w1(par, x, k, c), cols[:, y, k, bass.ds(j * TB, TB)],
                                                 start=(m == 0 and k == 0), stop=(m == 2 and k == KC - 1))
                        last.then_inc(first_up, 1)

                def down(n, par, biased_):
                    pe.wait_ge(hid_lo, IC * (n + 1))
                    pe.wait_ge(w2_lo, n + 1)
                    for t in range(BT):
                        if not (known(n) and n == 0):
                            pe.wait_ge(added, BT * (n - 1) + t + 1)
                        for m, (x, y) in enumerate(PASSES):
                            for c in range(IC):
                                last = pe.matmul(dps[:, t, :], hh[:, par, x, c, t * P:(t + 1) * P], w2(par, y, c),
                                                 start=(m == 0 and c == 0),
                                                 stop=(m == 2 and c == IC - 1 and not biased_))
                        if biased_:
                            last = pe.matmul(dps[:, t, :], oneh[:, :], b2h[:, :], start=False, stop=True)
                        last.then_inc(down_up, 1)

                def turned(st, src):
                    for k in range(KC):
                        last = pe.transpose(xps[:, st, k * P:(k + 1) * P], src(k), ident[:, :])
                    return last

                def k_turn(b):
                    for st in range(ST):
                        pe.wait_ge(rows_made, ST * b + st + 1)
                        if not (known(b) and b == 0):
                            pe.wait_ge(y_added, ST * b)
                        turned(st, lambda k: kr[0][:, st, k * P:(k + 1) * P]).then_inc(rows_up, 1)

                def logits(b):
                    pe.wait_ge(xT_copied, ST * b + ST)
                    for st in range(ST):
                        for k in range(KC):
                            last = pe.matmul(xps[:, 0, st * NE:(st + 1) * NE], xT[:, st, k, :], gw[:, k, :],
                                             start=(k == 0), stop=(k == KC - 1))
                    last.then_inc(logits_up, 1)

                def y_turn(b):
                    pe.wait_ge(y_made, b + 1)
                    if not (known(b) and b == 0):
                        pe.wait_ge(logits_exp, b)
                    for st in range(ST):
                        turned(st, lambda k: e1[:, k, st * P:(st + 1) * P]).then_inc(y_up, 1)

                def x_turn(b, b_next):
                    for st in range(ST):
                        pe.wait_ge(rows2_made, ST * b + st + 1)
                        if b_next is not None:
                            pe.wait_ge(kT_copied, ST * b_next + ST)
                        turned(st, lambda k: kr[1][:, st, k * P:(k + 1) * P]).then_inc(cols_up, 1)

                def slot(m, s, j, hb, last=False):
                    n = QS * m + s
                    w = not (known(m) and m < LAG)
                    b = m - LAG
                    before = w and not (known(b) and b == 0)
                    if not last:
                        first(n + 1, (s + 1) % 2, j + 1 if hb == BB - 1 and s == QS - 1 else j)
                    if s == 0 and before:
                        y_turn(b - 1)
                    if s == 1 and before:
                        x_turn(b - 1, b)
                    down(n, s % 2, s == 0 and hb == 0)
                    if s == 0 and w:
                        k_turn(b)
                    if s == 1 and before:
                        logits(b - 1)

                pe.wait_ge(const_loaded, 112)
                pe.wait_ge(b2_lo, 1)
                first(0, 0, 0)
                for m in range(LAG + BB):
                    for s in range(QS):
                        slot(m, s, m // BB, m % BB)
                with pe.Fori(2, NB - 1) as j:
                    for hb in range(BB):
                        for s in range(QS):
                            slot(BB * j + hb, s, j, hb)
                for hb in range(BB):
                    for s in range(QS):
                        slot(NQ - BB + hb, s, NB - 1, hb, hb == BB - 1 and s == QS - 1)
                for b in range(B - LAG, B):
                    y_turn(b - 1)
                    k_turn(b)
                    x_turn(b - 1, b)
                    logits(b - 1)
                y_turn(B - 1)
                x_turn(B - 1, None)
                logits(B - 1)


def moe_phase(nc, a, acc, ident, cw, mask, xn, listed, yr, out):
    W1 = 2 * KC * I
    W2 = IC * D
    UN = SU + RU
    XR = 2 * TOPK
    PLACED = 19

    with ExitStack() as ctx:
        def sb(name, shape, dt=F32):
            return ctx.enter_context(nc.sbuf_tensor(f"m_{name}_sb", shape, dt))

        def sem(name):
            return ctx.enter_context(nc.semaphore(f"m_{name}"))

        raw1 = sb("w1_raw", [P, 2, W1])
        raw2 = sb("w2_raw", [P, 2, W2])
        w1h = sb("w1_halves", [P, 2, 2, W1], F32R)
        w2h = sb("w2_halves", [P, 2, 2, W2], F32R)
        xr = sb("x_rows", [P, 2, UR, D])
        xh = sb("xT_halves", [P, 2, 2, KC, UT], F32R)
        gate = sb("gate", [P, IC, UT])
        hid = sb("hidden", [P, IC, UT])
        hh = sb("hidden_halves", [P, 2, 2, IC, UT], F32R)
        y = sb("y_rows", [P, 2, UR, D])
        yg = sb("y_gathered", [P, XR, D])
        before = sb("before", [P, P])
        ones = sb("ones", [P, P])
        same = sb("same_run", [P, NT, NE])
        starts = sb("unit_starts", [P, SU])
        unit_no = sb("unit_numbers", [P, RU])
        expert_row = sb("expert_row", [P, 1])
        ids = sb("token_ids", [P, NT], I32)
        zeros = sb("zeros", [LR, P], I32)
        tot = sb("tile_counts", [P, NE, NT])
        incl = sb("counts_incl", [P, NE, NT])
        rank = sb("rank", [P, NE, NT])
        over = sb("units_over", [P, NE, SU])
        units = sb("units", [P, NE])
        ends = sb("unit_ends", [P, NE])
        first = sb("first_place", [P, NE])
        turned = sb("mask_turned", [P, NT, NE])
        nth = sb("nth_chosen", [P, NT, NE])
        pick = sb("picked", [P, TOPK, NT, NE])
        place = sb("places", [P, TOPK, NT])
        placei = sb("places_int", [P, TOPK, NT], I32)
        wk = sb("place_weights", [P, TOPK, NT])
        past = sb("experts_past", [P, RU, NE - 1])
        unit_e = sb("unit_expert", [P, RU])
        w_rows = sb("weight_rows", [P, RU])
        list_i = sb("list_int", [LR, P], I32)
        list_f = sb("list", [LR, P])
        x_tok = sb("unit_tokens", [P, LR])
        w_at = sb("w_at", [P, 2, 1], I32)
        x_at = sb("x_at", [P, 2, UR], I32)
        y_at = sb("y_at", [P, XR], I32)

        xps = ctx.enter_context(nc.psum_tensor("m_x_ps", [P, UR, 512], F32))
        gps = ctx.enter_context(nc.psum_tensor("m_g_ps", [P, 2, 2, IC, UT], F32))
        dps = ctx.enter_context(nc.psum_tensor("m_d_ps", [P, UR, D], F32))

        const_loaded = sem("const_loaded")
        const_set = sem("const_set")
        pool_passed = sem("pool_passed")
        zeroed = sem("list_zeroed")
        ranks_up = sem("ranks_up")
        rt = sem("routing_step")
        scattered = sem("scattered")
        list_loaded = sem("list_loaded")
        list_made = sem("list_made")
        list_up = sem("list_up")
        at_set = sem("at_set")
        w1_got = [sem("w1_got_even"), sem("w1_got_odd")]
        w2_got = [sem("w2_got_even"), sem("w2_got_odd")]
        x_got = [[sem(f"x_got_{n}_{h}") for h in range(UR)] for n in ("even", "odd")]
        s1_got = [sem("s1_got_even"), sem("s1_got_odd")]
        s2_got = [sem("s2_got_even"), sem("s2_got_odd")]
        sx_got = [sem("sx_got_even"), sem("sx_got_odd")]
        w1_hi = sem("w1_hi")
        w1_lo = sem("w1_lo")
        w2_hi = sem("w2_hi")
        w2_lo = sem("w2_lo")
        x_up = sem("x_up")
        x_hi = sem("x_hi")
        x_lo = sem("x_lo")
        first_up = sem("first_up")
        gate_made = sem("gate_made")
        hid_made = sem("hid_made")
        hid_hi = sem("hid_hi")
        hid_lo = sem("hid_lo")
        down_up = sem("down_up")
        added = sem("added")
        y_made = sem("y_made")
        y_stored = [sem("y_stored_even"), sem("y_stored_odd")]
        y_at_set = sem("y_at_set")
        y_got = [sem(f"y_got_{r}") for r in range(XR)]
        summed = sem("summed")
        out_stored = sem("out_stored")

        class Unit:

            def __init__(self, i, c):
                self.i, self.c = i, c
                self.known = isinstance(i, int)
                self.n = 2 * i + c
                self.par = c % 2
                self.routed = not self.known or c >= SU
                self.exists = not self.known or c < UN
                self.u = 2 * i + (c - SU)
                self.turn = i + (c - SU) // 2
                self.splits = self.exists and (self.routed or c < 2)
                self.split = 2 * i + (c - (SU - 2) if self.routed else c)

            def __add__(self, k):
                return Unit(self.i, self.c + k)

            def first(self, n):
                return self.known and self.c < n

        HEAD, TAIL = SU + 2, 5

        def slots(eng, slot, start=0, end=UN - TAIL):
            for c in range(start, HEAD):
                slot(Unit(0, c))
            turns = (end - HEAD) // 2
            with eng.Fori(0, turns) as i:
                slot(Unit(i, HEAD))
                slot(Unit(i, HEAD + 1))
            for c in range(HEAD + 2 * turns, UN):
                slot(Unit(0, c))

        yd = yr.rearrange("(u h p) d -> u p h d", p=P, h=UR)
        xd = xn.rearrange("(u h p) d -> u p h d", p=P, h=UR)
        out_rows = out.rearrange("(t p) d -> t p d", p=P)
        w1_rows = a["moe_w1"].rearrange("e p c -> (e p) c")
        w2_rows = a["moe_w2"].rearrange("e p c -> (e p) c")

        with nc.Block() as block:
            @block.sync
            def _(sp):
                def x_shared(g):
                    if g > 1:
                        sp.wait_ge(x_up, UR * (g - 1))
                    sp.dma_start(xr[:, g % 2, :, :], xd[g]).then_inc(sx_got[g % 2], 16)

                def store(g):
                    sp.wait_ge(y_made, UR * (g.u + 1))
                    sp.dma_start(yd[g.u], y[:, g.par, :, :]).then_inc(y_stored[g.par], 16)

                x_shared(0)
                for par in range(2):
                    sp.dma_start(raw1[:, par, :], a["moe_w1"][0]).then_inc(s1_got[par], 16)
                    sp.dma_start(raw2[:, par, :], a["moe_w2"][0]).then_inc(s2_got[par], 16)
                    if par == 0:
                        loads = ((before, "before"), (starts, "unit_starts"), (unit_no, "unit_numbers"),
                                 (expert_row, "expert_row"), (ids, "token_ids"))
                        for n, (dst, src) in enumerate(loads):
                            sp.dma_start(dst[:, :], a[src]).then_inc(const_loaded, 16)
                            sp.wait_ge(const_loaded, 16 * (n + 1))
                        sp.dma_start(same[:, :, :].rearrange("p t e -> p (t e)"), a["same_run"])\
                          .then_inc(const_loaded, 16)
                for g in range(1, SU):
                    x_shared(g)
                sp.wait_ge(scattered, 16 * NT * TOPK)
                sp.dma_start(list_i[:, :], listed.rearrange("(r p) o -> r (p o)", p=P)).then_inc(list_loaded, 16)
                slots(sp, store, SU, UN)
                with sp.Fori(0, NT) as t:
                    sp.wait_ge(summed, TOPK * t + TOPK)
                    sp.dma_start(out_rows[t], acc[:, bass.ds(t, 1), :].rearrange("p a d -> p (a d)"))\
                      .then_inc(out_stored, 16)
                sp.wait_ge(out_stored, 16 * NT)

            @block.gpsimd
            def _(pool):
                def gather_w(buf, src, par, got):
                    pool.indirect_dma_start(buf[:, par, :], None, src,
                                            bass.IndirectOffsetOnAxis(w_at[:, par, :], 0)).then_inc(got[par], 16)

                def fetch(g):
                    pool.wait_ge(at_set, 2 * (g.u + 1)).then_inc(pool_passed, 1)
                    pool.wait_ge(w1_lo, g.split - 1).then_inc(pool_passed, 1)
                    gather_w(raw1, w1_rows, g.par, w1_got)
                    pool.wait_ge(x_up, UR * (g.n - 1)).then_inc(pool_passed, 1)
                    for h in range(UR):
                        pool.indirect_dma_start(xr[:, g.par, h, :], None, xn,
                                                bass.IndirectOffsetOnAxis(x_at[:, g.par, h:h + 1], 0))\
                            .then_inc(x_got[g.par][h], 16)
                    pool.wait_ge(w2_lo, g.split - 1).then_inc(pool_passed, 1)
                    gather_w(raw2, w2_rows, g.par, w2_got)

                pool.memset(zeros[:, :], 0).then_inc(const_set, 1)
                pool.memset(ones[:, :], 1.0).then_inc(const_set, 1)
                pool.wait_ge(const_set, 1)
                pool.dma_start(listed.rearrange("(r p) o -> r (p o)", p=P), zeros[:, :]).then_inc(zeroed, 16)
                pool.wait_ge(zeroed, 16)
                pool.wait_ge(const_loaded, 6 * 16)
                pool.wait_ge(rt, PLACED)
                for t in range(NT):
                    for k in range(TOPK):
                        pool.indirect_dma_start(listed, bass.IndirectOffsetOnAxis(placei[:, k, t:t + 1], 0),
                                                ids[:, t:t + 1], None).then_inc(scattered, 16)
                slots(pool, fetch, SU, UN)
                for par in range(2):
                    pool.wait_ge(y_stored[par], 16 * len(range(SU + par, UN, 2)))

                def collect(t2):
                    for r in range(XR):
                        pool.wait_ge(y_at_set, XR * t2 + (r + 1)).then_inc(pool_passed, 1)
                        if not isinstance(t2, int):
                            pool.wait_ge(summed, XR * t2 + (r + 1 - XR)).then_inc(pool_passed, 1)
                        pool.indirect_dma_start(yg[:, r, :], None, yr,
                                                bass.IndirectOffsetOnAxis(y_at[:, r:r + 1], 0))\
                            .then_inc(y_got[r], 16)

                collect(0)
                with pool.Fori(1, NT // 2) as t2:
                    collect(t2)

            @block.scalar
            def _(act):
                def w1_first(g):
                    if g.routed:
                        act.wait_ge(w1_got[g.par], 16 * (g.turn + 1))
                        act.wait_ge(first_up, 2 * IC * (g.n - 1))
                    else:
                        act.wait_ge(s1_got[g.par], 16)
                    act.activation(w1h[:, g.par, 0, :], raw1[:, g.par, :], ACT.Copy).then_inc(w1_hi, 1)

                def w2_first(g):
                    if g.routed:
                        act.wait_ge(w2_got[g.par], 16 * (g.turn + 1))
                        act.wait_ge(down_up, UR * (g.n - 1))
                    else:
                        act.wait_ge(s2_got[g.par], 16)
                    act.activation(w2h[:, g.par, 0, :], raw2[:, g.par, :], ACT.Copy).then_inc(w2_hi, 1)

                def x_first(g):
                    if not g.first(2):
                        act.wait_ge(first_up, 2 * IC * (g.n - 1))
                    for h in range(UR):
                        act.wait_ge(x_up, UR * g.n + (h + 1))
                        act.activation(xh[:, g.par, 0, :, h * P:(h + 1) * P],
                                       xps[:, h, :].rearrange("p (k t) -> p k t", k=KC), ACT.Copy).then_inc(x_hi, 1)

                def gated(g):
                    act.wait_ge(first_up, 2 * IC * g.n + IC)
                    if not g.first(1):
                        act.wait_ge(hid_made, g.n)
                    act.activation(gate[:, :, :], gps[:, g.par, 0, :, :], ACT.Silu).then_inc(gate_made, 1)

                def hidden_first(g):
                    act.wait_ge(hid_made, g.n + 1)
                    if not g.first(2):
                        act.wait_ge(down_up, UR * (g.n - 1))
                    act.activation(hh[:, g.par, 0, :, :], hid[:, :, :], ACT.Copy).then_inc(hid_hi, 1)

                def results(g):
                    if not g.first(SU + 2):
                        act.wait_ge(y_stored[g.par], 16 * g.turn)
                    for h in range(UR):
                        act.wait_ge(down_up, UR * g.n + (h + 1))
                        act.activation(y[:, g.par, h, :], dps[:, h, :], ACT.Copy).then_inc(y_made, 1)

                def slot(g):
                    if (g + 1).splits:
                        w2_first(g + 1)
                    if (g + 2).exists:
                        x_first(g + 2)
                    if (g + 2).splits:
                        w1_first(g + 2)
                    if (g + 1).exists:
                        gated(g + 1)
                        hidden_first(g + 1)
                    if g.routed:
                        results(g)

                w1_first(Unit(0, 0))
                x_first(Unit(0, 0))
                w2_first(Unit(0, 0))
                w1_first(Unit(0, 1))
                x_first(Unit(0, 1))
                gated(Unit(0, 0))
                hidden_first(Unit(0, 0))
                slots(act, slot)

            @block.vector
            def _(dve):
                def w1_rest(g):
                    dve.wait_ge(w1_hi, g.split + 1)
                    dve.tensor_tensor(w1h[:, g.par, 1, :], raw1[:, g.par, :], w1h[:, g.par, 0, :].bitcast(F32),
                                      ALU.subtract).then_inc(w1_lo, 1)

                def w2_rest(g):
                    dve.wait_ge(w2_hi, g.split + 1)
                    dve.tensor_tensor(w2h[:, g.par, 1, :], raw2[:, g.par, :], w2h[:, g.par, 0, :].bitcast(F32),
                                      ALU.subtract).then_inc(w2_lo, 1)

                def x_rest(g):
                    for h in range(UR):
                        part = slice(h * P, (h + 1) * P)
                        dve.wait_ge(x_hi, UR * g.n + (h + 1))
                        dve.tensor_tensor(xh[:, g.par, 1, :, part],
                                          xps[:, h, :].rearrange("p (k t) -> p k t", k=KC),
                                          xh[:, g.par, 0, :, part].bitcast(F32), ALU.subtract).then_inc(x_lo, 1)

                def hidden(g):
                    dve.wait_ge(gate_made, g.n + 1)
                    dve.wait_ge(first_up, 2 * IC * (g.n + 1))
                    if not g.first(1):
                        dve.wait_ge(hid_lo, g.n)
                    dve.tensor_tensor(hid[:, :, :], gate[:, :, :], gps[:, g.par, 1, :, :], ALU.mult)\
                       .then_inc(hid_made, 1)

                def hidden_rest(g):
                    dve.wait_ge(hid_hi, g.n + 1)
                    dve.tensor_tensor(hh[:, g.par, 1, :, :], hid[:, :, :], hh[:, g.par, 0, :, :].bitcast(F32),
                                      ALU.subtract).then_inc(hid_lo, 1)

                def add(g):
                    for h in range(UR):
                        dve.wait_ge(down_up, UR * g.n + h + 1)
                        dve.tensor_tensor(acc[:, UR * g.n + h, :], dps[:, h, :], acc[:, UR * g.n + h, :], ALU.add)\
                           .then_inc(added, 1)

                def set_at(g):
                    if not g.first(SU + 2):
                        for got in (w1_got[g.par], w2_got[g.par], *x_got[g.par]):
                            dve.wait_ge(got, 16 * g.turn)
                    dve.tensor_scalar(w_at[:, g.par, :], w_rows[:, bass.ds(g.u, 1)], 1.0, None, ALU.mult)\
                       .then_inc(at_set, 1)
                    dve.tensor_scalar(x_at[:, g.par, :], x_tok[:, bass.ds(UR * g.u, UR)], 1.0, None, ALU.mult)\
                       .then_inc(at_set, 1)

                def turned_list():
                    dve.wait_ge(list_loaded, 16)
                    dve.tensor_scalar(list_f[:, :], list_i[:, :], 1.0, None, ALU.mult).then_inc(list_made, 1)
                    dve.wait_ge(list_up, 1)
                    dve.tensor_scalar(x_tok[:, :], xps[:, 0, 0:LR], 1.0, None, ALU.mult).then_inc(list_made, 1)
                    dve.wait_ge(list_made, 2)

                steps = [0]

                def step(op):
                    if steps[0]:
                        dve.wait_ge(rt, steps[0])
                    op().then_inc(rt, 1)
                    steps[0] += 1

                def flat(t):
                    return t[:, :, :].rearrange("p a b -> p (a b)")

                def places():
                    dve.wait_ge(const_loaded, 6 * 16)
                    dve.wait_ge(ranks_up, 1)
                    step(lambda: dve.tensor_scalar(flat(tot), xps[:, 1, 0:NE * NT], 1.0, None, ALU.mult))
                    step(lambda: dve.tensor_tensor_scan(flat(incl), flat(same), flat(tot), 0.0, ALU.mult, ALU.add))
                    step(lambda: dve.tensor_tensor(flat(tot), flat(incl), flat(tot), ALU.subtract))
                    step(lambda: dve.tensor_tensor(flat(rank), xps[:, 0, 0:NE * NT], flat(tot), ALU.add))
                    step(lambda: dve.tensor_tensor(over[:, :, :], bcast(incl[:, :, NT - 1:NT], [P, NE, SU]),
                                                   bcast(starts[:, :].rearrange("p (o s) -> p o s", o=1),
                                                         [P, NE, SU]), ALU.is_gt))
                    step(lambda: dve.tensor_reduce(units[:, :], over[:, :, :], AX_X, ALU.add))
                    step(lambda: dve.tensor_tensor_scan(ends[:, :], ones[:, 0:NE], units[:, :], 0.0,
                                                        ALU.mult, ALU.add))
                    step(lambda: dve.tensor_tensor(first[:, :], ends[:, :], units[:, :], ALU.subtract))
                    step(lambda: dve.tensor_scalar(first[:, :], first[:, :], float(UT), None, ALU.mult))
                    step(lambda: dve.tensor_tensor(rank[:, :, :], rank[:, :, :],
                                                   bcast(first[:, :].rearrange("p (e o) -> p e o", o=1),
                                                         [P, NE, NT]), ALU.add))
                    step(lambda: dve.tensor_scalar(turned[:, :, :], mask[:, :, :].rearrange("p e t -> p t e"),
                                                   1.0, None, ALU.mult))
                    step(lambda: dve.tensor_tensor_scan(flat(nth), flat(same), flat(turned), 0.0,
                                                        ALU.mult, ALU.add))
                    step(lambda: dve.tensor_tensor(flat(nth), flat(nth), flat(turned), ALU.mult))
                    for src, dst in ((rank, place), (cw, wk)):
                        for k in range(TOPK):
                            step(lambda: dve.scalar_tensor_tensor(
                                out=pick[:, k, :, :], in0=nth[:, :, :], scalar=float(k + 1),
                                in1=src[:, :, :].rearrange("p e t -> p t e"), op0=ALU.is_equal, op1=ALU.mult))
                        step(lambda: dve.tensor_reduce(dst[:, :, :], pick[:, :, :, :], AX_X, ALU.add))
                        if dst is place:
                            step(lambda: dve.tensor_scalar(placei[:, :, :], place[:, :, :], 1.0, None, ALU.mult))
                            assert steps[0] == PLACED
                    step(lambda: dve.tensor_tensor(past[:, :, :],
                                                   bcast(unit_no[:, :].rearrange("p (u o) -> p u o", o=1),
                                                         [P, RU, NE - 1]),
                                                   bcast(ends[:, 0:NE - 1].rearrange("p (o e) -> p o e", o=1),
                                                         [P, RU, NE - 1]), ALU.is_ge))
                    step(lambda: dve.tensor_reduce(unit_e[:, :], past[:, :, :], AX_X, ALU.add))
                    step(lambda: dve.tensor_scalar(w_rows[:, :], unit_e[:, :], float(P), expert_row[:, 0:1],
                                                   ALU.mult, ALU.add))
                    dve.wait_ge(rt, steps[0])

                def slot(g):
                    if (g + 1).splits:
                        w2_rest(g + 1)
                    if (g + 2).exists:
                        x_rest(g + 2)
                    if (g + 2).splits:
                        w1_rest(g + 2)
                    if (g + 4).exists and not (g + 4).first(SU + 2):
                        set_at(g + 4)
                    if (g + 1).exists:
                        hidden(g + 1)
                        hidden_rest(g + 1)
                    if not g.routed:
                        add(g)
                    if g.known and g.c == SU - 3:
                        turned_list()
                        set_at(g + 3)
                        set_at(g + 4)

                def point(t2, r):
                    t, k = 2 * t2 + r // TOPK, r % TOPK
                    dve.tensor_scalar(y_at[:, r:r + 1], place[:, k, bass.ds(t, 1)], 1.0, None, ALU.mult)\
                       .then_inc(y_at_set, 1)

                def total(t2, last=False):
                    for r in range(XR):
                        t, k = 2 * t2 + r // TOPK, r % TOPK
                        dve.wait_ge(y_got[r], 16 * (t2 + 1))
                        if not (isinstance(t2, int) and t2 == 0 and r == 0):
                            dve.wait_ge(summed, XR * t2 + r)
                        row = acc[:, bass.ds(t, 1), :].rearrange("p a d -> p (a d)")
                        dve.scalar_tensor_tensor(out=row, in0=yg[:, r, :], scalar=wk[:, k, bass.ds(t, 1)],
                                                 in1=row, op0=ALU.mult, op1=ALU.add).then_inc(summed, 1)
                        if not last:
                            point(t2 + 1, r)

                dve.wait_ge(const_set, 2)
                w1_rest(Unit(0, 0))
                x_rest(Unit(0, 0))
                w2_rest(Unit(0, 0))
                w1_rest(Unit(0, 1))
                places()
                x_rest(Unit(0, 1))
                hidden(Unit(0, 0))
                hidden_rest(Unit(0, 0))
                slots(dve, slot)
                for r in range(XR):
                    point(0, r)
                dve.wait_ge(added, UR * SU)
                total(0)
                with dve.Fori(1, NT // 2 - 1) as t2:
                    total(t2)
                total(NT // 2 - 1, last=True)

            @block.tensor
            def _(pe):
                def turn(g):
                    for h in range(UR):
                        if g.routed:
                            pe.wait_ge(x_got[g.par][h], 16 * (g.turn + 1))
                        else:
                            pe.wait_ge(sx_got[g.par], 16 * (g.c // 2 + 1))
                        if not g.first(1):
                            pe.wait_ge(x_lo, UR * (g.n - 1) + (h + 1))
                        for k in range(KC):
                            last = pe.transpose(xps[:, h, k * P:(k + 1) * P], xr[:, g.par, h, k * P:(k + 1) * P],
                                                ident[:, :])
                        last.then_inc(x_up, 1)

                def first_layer(g):
                    pe.wait_ge(x_lo, UR * (g.n + 1))
                    if g.splits:
                        pe.wait_ge(w1_lo, g.split + 1)
                    if not g.first(2):
                        pe.wait_ge(hid_made, g.n - 1)
                    for part in range(2):
                        for c in range(IC):
                            for m, (i, j) in enumerate(PASSES):
                                for k in range(KC):
                                    w = (part * KC + k) * I + c * P
                                    last = pe.matmul(gps[:, g.par, part, c, :], w1h[:, g.par, i, w:w + P],
                                                     xh[:, g.par, j, k, :],
                                                     start=(m == 0 and k == 0), stop=(m == 2 and k == KC - 1))
                            last.then_inc(first_up, 1)

                def down(g):
                    pe.wait_ge(hid_lo, g.n + 1)
                    if g.splits:
                        pe.wait_ge(w2_lo, g.split + 1)
                    for h in range(UR):
                        if (g + -1).routed:
                            pe.wait_ge(y_made, UR * (g + -1).u + (h + 1))
                        elif not g.first(1):
                            pe.wait_ge(added, UR * (g.n - 1) + (h + 1))
                        for m, (i, j) in enumerate(PASSES):
                            for c in range(IC):
                                last = pe.matmul(dps[:, h, :], hh[:, g.par, i, c, h * P:(h + 1) * P],
                                                 w2h[:, g.par, j, c * D:(c + 1) * D],
                                                 start=(m == 0 and c == 0), stop=(m == 2 and c == IC - 1))
                        last.then_inc(down_up, 1)

                def slot(g):
                    if (g + 2).exists:
                        turn(g + 2)
                    if (g + 1).exists:
                        first_layer(g + 1)
                    down(g)
                    if g.known and g.c == SU - 3:
                        pe.wait_ge(list_made, 1)
                        pe.wait_ge(x_lo, UR * SU)
                        pe.transpose(xps[:, 0, 0:LR], list_f[:, :], ident[0:LR, 0:LR]).then_inc(list_up, 1)
                        pe.wait_ge(list_made, 2)

                turn(Unit(0, 0))
                pe.wait_ge(const_loaded, 6 * 16)
                pe.wait_ge(const_set, 2)
                pe.wait_ge(x_lo, UR)
                for b, m in enumerate((before, ones)):
                    last = pe.matmul(xps[:, b, 0:NE * NT], m[:, :], mask[:, :, :].rearrange("p e t -> p (e t)"),
                                     start=True, stop=True)
                last.then_inc(ranks_up, 1)
                pe.wait_ge(rt, 4)
                turn(Unit(0, 1))
                first_layer(Unit(0, 0))
                slots(pe, slot)


def build(nc, a, out, stop=9):
    def dram(name, shape, dt=F32):
        return nc.dram_tensor(name, shape, dt, kind="Internal").ap()

    xn = dram("xn_rows", (B * S, D))
    listed = dram("listed_tokens", (RU * UT, 1), I32)
    yr = dram("expert_rows", (RU * UT, D))
    with ExitStack() as ctx:
        acc = ctx.enter_context(nc.sbuf_tensor("acc", [P, NT, D], F32))
        ident = ctx.enter_context(nc.sbuf_tensor("identity", [P, P], F32))
        attention_phase(nc, a, acc, ident)
        cw = ctx.enter_context(nc.sbuf_tensor("expert_weights", [P, NE, NT], F32))
        mask = ctx.enter_context(nc.sbuf_tensor("expert_mask", [P, NE, NT], F32))
        if stop > 1:
            with ExitStack() as inner:
                cols = inner.enter_context(nc.sbuf_tensor("cols_halves", [P, 2, KC, B * S], F32R))
                columns_phase(nc, a["final_w"], acc, ident, cols)
                ffn_wkv_phase(nc, a, acc, ident, cols, cw, mask, xn)
        if stop > 3:
            moe_phase(nc, a, acc, ident, cw, mask, xn, listed, yr, out)
        else:
            stored = ctx.enter_context(nc.semaphore("out_stored"))
            with nc.Block() as block:
                @block.sync
                def _(sp):
                    sp.dma_start(out.rearrange("(n p) d -> p n d", p=P), acc[:, :, :]).then_inc(stored, 16)
                    sp.wait_ge(stored, 16)


def attention_constants():
    angle = (1.0 / 10000.0 ** np.linspace(0.0, 1.0, DH // 2, dtype=np.float32)).astype(np.float32)
    phase = np.arange(S, dtype=np.float32)[:, None] * np.repeat(angle, 2)[None, :]
    sign = np.where(np.arange(DH) % 2 == 0, -1.0, 1.0).astype(np.float32)
    rows = lambda t: np.ascontiguousarray(t.reshape(ST, P, -1).transpose(1, 0, 2).astype(np.float32))
    decay = np.log(1.0 - 2.0 ** (-5.0 - np.arange(H)))
    i, t = np.arange(S)[:, None], np.arange(S)[None, :]
    m = np.where(i >= t, np.exp(np.where(i >= t, i - t, 0)[None] * decay[:, None, None]), 0.0)
    inv = 1.0 / np.sqrt(m.sum(-1))
    mt = m.transpose(2, 0, 1)[:P].reshape(P, H, 2, P) * DH ** -0.5
    return {"cos": rows(np.cos(phase)), "sin": rows(np.sin(phase) * sign),
            "inv_norm": rows(inv.T), "mask": np.ascontiguousarray(mt.astype(np.float32)),
            "ident": np.eye(P, dtype=np.float32)}


def routing_constants():
    rows = lambda v: np.broadcast_to(np.asarray(v, dtype=np.float32).reshape(1, -1), (P, np.size(v)))
    same = np.arange(NE * NT) % NT != 0
    assert NE == NT
    return {"before": np.triu(np.ones((P, P), np.float32), 1),
            "same_run": rows(same), "unit_starts": rows(UT * np.arange(SU)), "unit_numbers": rows(np.arange(RU)),
            "expert_row": float(P) + np.arange(P, dtype=np.float32).reshape(P, 1),
            "token_ids": (P * np.arange(NT)[None, :] + np.arange(P)[:, None]).astype(np.int32)}


def kernel(**inputs):
    from concourse import bacc
    from concourse.bass_utils import run_bass_kernel_spmd

    x = {n: np.asarray(v) for n, v in inputs.items()}
    arrays = layouts(x)
    nc = bacc.Bacc("TRN2", target_bir_lowering=False, num_devices=1)
    aps = {n: nc.dram_tensor(n, v.shape, mybir.dt.from_np(v.dtype), kind="ExternalInput").ap()
           for n, v in arrays.items()}
    out = nc.dram_tensor("out", (B * S, D), F32, kind="ExternalOutput").ap()
    build(nc, aps, out)
    r = run_bass_kernel_spmd(nc, [arrays], core_ids=[0])
    return r.results[0]["out"].reshape(B, S, D)


def layouts(x):
    def chunks(w):
        return w.reshape(-1, P, w.shape[-1]).transpose(1, 0, 2)

    arrays = dict(attention_constants())
    arrays["x"] = x["x"].reshape(B * S, D)
    arrays["attn_w"] = np.stack([chunks(x[f"L0_attn_{n}_w"]) for n in ("q", "k", "v", "g", "out")])
    arrays["retn_w"] = x["L0_attn_retn_norm_w"].reshape(KC, P).T
    arrays["final_w"] = x["L0_attn_final_norm_w"].reshape(1, D)

    def joined(*parts):
        return np.concatenate([p.reshape(p.shape[0], P, -1) for p in parts], axis=2)

    def slice_chunks(w):
        return w.reshape(w.shape[0], -1, P, w.shape[-1]).transpose(0, 2, 1, 3)

    fc1 = x["L0_attn_fc1_w"].reshape(D, F // I, I).transpose(1, 0, 2)
    fc2 = x["L0_attn_fc2_w"].reshape(F // I, I, D)
    arrays["ffn_w"] = joined(slice_chunks(fc1), slice_chunks(fc2))
    arrays["fc1_b"] = x["L0_attn_fc1_b"].reshape(F // P, P).T
    arrays["fc2_b"] = x["L0_attn_fc2_b"].reshape(1, D)
    experts = [np.concatenate([x[f"L0_ffn_sw_{n}"][None], x[f"L0_ffn_w_{n}"]]) for n in ("gate", "up", "down")]
    gate, up, down = (slice_chunks(w.transpose(0, 2, 1)) for w in experts)
    arrays["moe_w1"] = joined(gate, up)
    arrays["moe_w2"] = joined(down)
    arrays.update(routing_constants())
    arrays["ctx"] = x["ctx_2048"].reshape(B, S, KC, P).transpose(0, 3, 2, 1)
    arrays["time_decay"] = x["L0_xattn_time_decay"].reshape(KC, P).T
    arrays["time_first"] = x["L0_xattn_time_first"].reshape(KC, P).T
    arrays["gate_w"] = chunks(x["L0_ffn_gate_w"].T)
    arrays["expert_bias"] = x["L0_ffn_expert_bias"].reshape(1, NE)
    return {n: np.ascontiguousarray(v) for n, v in arrays.items()}
```

```python
from contextlib import ExitStack

import numpy as np

import concourse.bass as bass
from concourse import mybir

F32 = mybir.dt.float32
F32R = mybir.dt.float32r
I32 = mybir.dt.int32
ALU = mybir.AluOpType
ACT = mybir.ActivationFunctionType
AX_X = mybir.AxisListType.X

P = 128
B, S, D = 8, 256, 512
NT = B * S // P
ST = S // P
KC = D // P
H = 16
DH = D // H
HG = P // DH
HALF = H // 2
F = 2048
NE = 16
TOPK = 4
I = 256
IC = I // P
TB = 512
NB = B * S // TB
BT = TB // P
UT = 256
UR = UT // P
SU = B * S // UT
RU = (B * S * TOPK + NE * (UT - 1)) // UT
LR = RU * UR
EPS = 1e-5
NEG = -1e38

PASSES = ((0, 0), (0, 1), (1, 0))


def bcast(ap, shape):
    return ap.to_broadcast(shape)


def attention_phase(nc, a, acc, ident):
    with ExitStack() as ctx:
        def sb(name, shape, dt=F32):
            return ctx.enter_context(nc.sbuf_tensor(name + "_sb", shape, dt))

        def sem(name):
            return ctx.enter_context(nc.semaphore(name))

        NW = 5
        whl = sb("attn_w_halves", [P, 2, NW, KC, D], F32R)
        scm = sb("scores_masked_sb", [P, HALF, 3 * P])
        mask = sb("decay_mask", [P, H, 2, P])
        invn = sb("inv_mask_norm", [P, ST, H])
        cos = sb("cos_t", [P, ST, DH])
        sin = sb("sin_t", [P, ST, DH])
        rnw = sb("retn_w", [P, KC])
        xin = sb("xin", [P, ST, D])
        h = sb("h_rows", [P, ST, D])
        hT = sb("hT_halves", [P, 2, ST, KC, P], F32R)
        tcos = sb("rot_cos", [P, D])
        tsin = sb("rot_sin", [P, D])
        qk = sb("qk_rows", [P, 2, ST, D])
        qT = sb("q_cols", [P, KC, S])
        kT = sb("k_cols", [P, HG, KC, S])
        wraw = [scm[:, :, :].rearrange("p h n -> p (h n)")[:, 0:KC * D].rearrange("p (k n) -> p k n", k=KC),
                qk[:, :, :, :].rearrange("p w s d -> p (w s) d")]
        v = sb("v_and_ones", [P, ST, H, DH + 1])
        gate = sb("gate_rows", [P, ST, D])
        o = sb("o_and_denom", [P, ST, H, DH + 1])
        on = sb("o_normed", [P, ST, D])
        oT = hT
        st6 = sb("bn6", [P, ST, 6])
        mv = sb("mean_var", [P, ST, 2])
        lnc = sb("ln_consts", [P, 4, ST])
        mhalf = sb("minus_half", [P, ST * H])
        eps = sb("eps_t", [P, ST * H])
        sm = sb("norm_small", [P, 6, ST, H])

        xps = ctx.enter_context(nc.psum_tensor("x_ps", [P, 2, 512], F32))
        yps = ctx.enter_context(nc.psum_tensor("y_ps", [P, 2, 512], F32))
        pps = ctx.enter_context(nc.psum_tensor("proj_ps", [P, 4, 512], F32))

        rnw_loaded = sem("a_rnw_loaded")
        ident_loaded = sem("a_ident_loaded")
        rot_loaded = [sem("a_cos_loaded"), sem("a_sin_loaded")]
        invn_loaded = sem("a_invn_loaded")
        mask_loaded = sem("a_mask_loaded")
        w_loaded = [sem("a_w_even_loaded"), sem("a_w_odd_loaded")]
        zeros_set = sem("a_zeros_set")
        w_hi = sem("a_w_hi")
        w_lo = sem("a_w_lo")
        ones_set = sem("a_ones_set")
        half_set = sem("a_half_set")
        x_loaded = sem("a_x_loaded")
        bn_made = sem("a_bn_made")
        bn_passed = sem("a_bn_passed")
        stats_made = sem("a_stats_made")
        ln_step = sem("a_ln_step")
        h_made = sem("a_h_made")
        hT_up = sem("a_hT_up")
        hT_hi = sem("a_hT_hi")
        hT_lo = sem("a_hT_lo")
        proj_up = sem("a_proj_up")
        rot_read = sem("a_rot_read")
        qk_rotated = sem("a_qk_rotated")
        v_copied = sem("a_v_copied")
        g_made = sem("a_g_made")
        qkT_up = sem("a_qkT_up")
        qkT_copied = sem("a_qkT_copied")
        scores_up = sem("a_scores_up")
        scores_masked = sem("a_scores_masked")
        o_up = sem("a_o_up")
        o_copied = sem("a_o_copied")
        o_squared = sem("a_o_squared")
        nv = sem("a_norm_dve")
        ng = sem("a_norm_pool")
        on_gated = sem("a_on_gated")
        oT_up = sem("a_oT_up")
        oT_hi = sem("a_oT_hi")
        oT_lo = sem("a_oT_lo")
        out_up = sem("a_out_up")
        r_added = sem("a_r_added")

        NV, LN = 11, 7
        xd = a["x"].rearrange("(b s p) d -> b p s d", p=P, s=ST)

        with nc.Block() as block:
            @block.sync
            def _(sp):
                def load_w(n):
                    sp.dma_start(wraw[n % 2], a["attn_w"][n]).then_inc(w_loaded[n % 2], 16)

                sp.dma_start(xin[:, :, :], xd[0]).then_inc(x_loaded, 16)
                sp.dma_start(rnw[:, :], a["retn_w"]).then_inc(rnw_loaded, 16)
                load_w(0)
                sp.dma_start(ident[:, :], a["ident"]).then_inc(ident_loaded, 16)
                load_w(1)
                sp.dma_start(cos[:, :, :], a["cos"]).then_inc(rot_loaded[0], 16)
                sp.dma_start(sin[:, :, :], a["sin"]).then_inc(rot_loaded[1], 16)
                sp.dma_start(invn[:, :, :], a["inv_norm"]).then_inc(invn_loaded, 16)
                for n in range(2, NW):
                    sp.wait_ge(w_lo, n - 1)
                    load_w(n)
                sp.dma_start(mask[:, :, :, :], a["mask"]).then_inc(mask_loaded, 16)
                with sp.Fori(1, B) as b:
                    sp.wait_ge(h_made, b)
                    sp.dma_start(xin[:, :, :], xd[b]).then_inc(x_loaded, 16)

            @block.gpsimd
            def _(pool):
                pool.memset(mhalf[:, :], -0.5).then_inc(half_set, 1)
                pool.memset(eps[:, :], EPS).then_inc(half_set, 1)
                pool.memset(v[:, :, :, DH:DH + 1], 1.0).then_inc(ones_set, 1)
                pool.memset(kT[:, :, :, :], 0.0).then_inc(zeros_set, 1)
                pool.wait_ge(half_set, 2)

                def heads(t):
                    return t[:, :].rearrange("p (s h) -> p s h", s=ST)

                def ln_scales(b):
                    var = mv[:, :, 1]
                    ve, rstd, t, s = (lnc[:, k, :] for k in range(4))
                    n = LN * b
                    pool.wait_ge(stats_made, ST * (b + 1))
                    if not (isinstance(b, int) and b == 0):
                        pool.wait_ge(h_made, b)
                    pool.tensor_tensor(ve, var, eps[:, 0:ST], ALU.add).then_inc(ln_step, 1)
                    pool.wait_ge(ln_step, n + 1)
                    pool.tensor_tensor(rstd, ve, mhalf[:, 0:ST], ALU.pow).then_inc(ln_step, 1)
                    pool.wait_ge(ln_step, n + 2)
                    pool.tensor_tensor(t, rstd, rstd, ALU.mult).then_inc(ln_step, 1)
                    pool.wait_ge(ln_step, n + 3)
                    pool.tensor_tensor(ve, t, var, ALU.mult).then_inc(ln_step, 1)
                    pool.wait_ge(ln_step, n + 4)
                    pool.tensor_tensor(t, ve, eps[:, 0:ST], ALU.add).then_inc(ln_step, 1)
                    pool.wait_ge(ln_step, n + 5)
                    pool.tensor_tensor(ve, t, mhalf[:, 0:ST], ALU.pow).then_inc(ln_step, 1)
                    pool.wait_ge(ln_step, n + 6)
                    pool.tensor_tensor(s, rstd, ve, ALU.mult).then_inc(ln_step, 1)

                def rotate(b, st, w):
                    n = 2 * ST * b + 2 * st + w
                    pool.wait_ge(rot_read, n + 1)
                    if isinstance(b, int) and b == 0:
                        pool.wait_ge(w_lo, NW - 1)
                    else:
                        pool.wait_ge(qkT_up, 2 * ST * b)
                    pool.tensor_tensor(qk[:, w, st, :], tcos[:, :], tsin[:, :], ALU.add)\
                        .then_inc(qk_rotated, 1)

                def norm(b):
                    pool.wait_ge(nv, NV * b + 9)
                    pool.tensor_tensor(sm[:, 3, :, :], sm[:, 4, :, :], heads(mhalf), ALU.pow).then_inc(ng, 1)
                    pool.wait_ge(nv, NV * b + NV)
                    pool.wait_ge(g_made, ST * b + ST)
                    pool.tensor_tensor(on[:, :, :], on[:, :, :], gate[:, :, :], ALU.mult).then_inc(on_gated, 1)

                def turn(b, after):
                    if after:
                        rotate(b + 1, 0, 0)
                        rotate(b + 1, 0, 1)
                    norm(b)
                    if after > 1:
                        ln_scales(b + 2)
                    if after:
                        rotate(b + 1, 1, 0)
                        rotate(b + 1, 1, 1)

                ln_scales(0)
                for st in range(ST):
                    rotate(0, st, 0)
                    rotate(0, st, 1)
                ln_scales(1)
                turn(0, 2)
                with pool.Fori(1, B - 2) as b:
                    turn(b, 2)
                turn(B - 2, 1)
                turn(B - 1, 0)

            @block.scalar
            def _(act):
                def weight_first(n):
                    act.wait_ge(w_loaded[n % 2], 16 * (n // 2 + 1))
                    if n < NW - 1:
                        act.wait_ge(rnw_loaded, 16)
                        for k in range(KC):
                            last = act.activation(whl[:, 0, n, k, :], wraw[n % 2][:, k, :], ACT.Copy,
                                                  scale=rnw[:, k:k + 1])
                    else:
                        last = act.activation(whl[:, 0, n, :, :], wraw[n % 2], ACT.Copy)
                    last.then_inc(w_hi, 1)

                def hT_halves(b, st):
                    act.wait_ge(hT_up, ST * b + st + 1)
                    act.activation(hT[:, 0, st, :, :], pps[:, 2 + st, :].rearrange("p (k t) -> p k t", k=KC),
                                   ACT.Copy).then_inc(hT_hi, 1)

                def values_out(b, st):
                    u = 4 * (ST * b + st)
                    act.wait_ge(proj_up, u + 3)
                    act.wait_ge(o_up, ST * b)
                    act.activation(v[:, st, :, 0:DH], pps[:, 2, :].rearrange("p (h d) -> p h d", h=H),
                                   ACT.Copy).then_inc(v_copied, 1)

                def gate_out(b, st):
                    act.wait_ge(proj_up, 4 * (ST * b + st) + 4)
                    act.wait_ge(on_gated, b)
                    act.activation(gate[:, st, :], pps[:, 3, :], ACT.Silu).then_inc(g_made, 1)

                def turn(b, more):
                    for u in range(2 * ST):
                        w, st = u // ST, u % ST
                        act.wait_ge(qkT_up, 2 * ST * b + u + 1)
                        if w == 0:
                            last = act.activation(qT[:, :, st * P:(st + 1) * P],
                                                  xps[:, u % 2, :].rearrange("p (k t) -> p k t", k=KC), ACT.Copy)
                        else:
                            for g in range(HG):
                                r = slice(DH * g, DH * (g + 1))
                                last = act.activation(kT[r, g, :, st * P:(st + 1) * P],
                                                      xps[r, u % 2, :].rearrange("p (k t) -> p k t", k=KC),
                                                      ACT.Copy)
                        last.then_inc(qkT_copied, 1)
                    if more:
                        hT_halves(b + 1, 0)
                        hT_halves(b + 1, 1)
                    for half in range(2):
                        act.wait_ge(o_up, 2 * b + half + 1)
                        act.wait_ge(on_gated, b)
                        act.activation(o[:, :, half * HALF:(half + 1) * HALF, :],
                                       yps[:, :, 0:HALF * (DH + 1)].rearrange("p s (h d) -> p s h d", h=HALF),
                                       ACT.Copy).then_inc(o_copied, 1)
                    act.wait_ge(o_copied, 2 * b + 2)
                    act.wait_ge(oT_up, ST * b)
                    act.activation(on[:, :, :].rearrange("p s (h d) -> p (s h) d", h=H),
                                   o[:, :, :, 0:DH].rearrange("p s h d -> p (s h) d"),
                                   ACT.Square).then_inc(o_squared, 1)
                    if more:
                        values_out(b + 1, 0)
                        gate_out(b + 1, 0)
                        values_out(b + 1, 1)
                        gate_out(b + 1, 1)
                    for st in range(ST):
                        act.wait_ge(oT_up, ST * b + st + 1)
                        act.activation(oT[:, 0, st, :, :], pps[:, 2 + st, :].rearrange("p (k t) -> p k t", k=KC),
                                       ACT.Copy).then_inc(oT_hi, 1)

                weight_first(0)
                weight_first(1)
                hT_halves(0, 0)
                hT_halves(0, 1)
                weight_first(2)
                weight_first(3)
                act.wait_ge(ones_set, 1)
                values_out(0, 0)
                gate_out(0, 0)
                weight_first(4)
                values_out(0, 1)
                gate_out(0, 1)
                act.wait_ge(zeros_set, 1)
                turn(0, True)
                with act.Fori(1, B - 1) as b:
                    turn(b, True)
                turn(B - 1, False)

            @block.vector
            def _(dve):
                def ln_stats(b):
                    dve.wait_ge(x_loaded, 16 * (b + 1))
                    for st in range(ST):
                        dve.bn_stats(st6[:, st, :], xin[:, st, :]).then_inc(bn_made, 1)
                    dve.wait_ge(bn_made, ST * b + ST).then_inc(bn_passed, 1)
                    for st in range(ST):
                        dve.bn_aggr(mv[:, st, :], st6[:, st, :]).then_inc(stats_made, 1)

                def ln_rows(b):
                    dve.wait_ge(ln_step, LN * (b + 1))
                    dve.wait_ge(hT_up, ST * b)
                    for st in range(ST):
                        dve.tensor_scalar(acc[:, bass.ds(ST * b + st, 1), :].rearrange("p a d -> p (a d)"),
                                          xin[:, st, :], mv[:, st, 0:1], lnc[:, 1, st:st + 1],
                                          ALU.subtract, ALU.mult)
                        last = dve.tensor_scalar(h[:, st, :], xin[:, st, :], mv[:, st, 0:1],
                                                 lnc[:, 3, st:st + 1], ALU.subtract, ALU.mult)
                    last.then_inc(h_made, 1)

                def hT_rest(b, st):
                    dve.wait_ge(hT_hi, ST * b + st + 1)
                    dve.tensor_tensor(hT[:, 1, st, :, :], pps[:, 2 + st, :].rearrange("p (k t) -> p k t", k=KC),
                                      hT[:, 0, st, :, :].bitcast(F32), ALU.subtract).then_inc(hT_lo, 1)

                def rotate(b, st, w):
                    n = 2 * ST * b + 2 * st + w
                    dve.wait_ge(proj_up, 4 * (ST * b + st) + w + 1)
                    if not (isinstance(n, int) and n == 0):
                        dve.wait_ge(qk_rotated, n)
                    src = pps[:, w, :].rearrange("p (h d) -> p h d", h=H)
                    dve.tensor_tensor(tcos[:, :].rearrange("p (h d) -> p h d", h=H), src,
                                      bcast(cos[:, st:st + 1, :], [P, H, DH]), ALU.mult)
                    pair = pps[:, w, :].rearrange("p (h d t) -> p h d t", h=H, t=2)
                    swap = tsin[:, :].rearrange("p (h d t) -> p h d t", h=H, t=2)
                    sign = sin[:, st:st + 1, :].rearrange("p s (d t) -> p s d t", t=2)
                    for t in range(2):
                        last = dve.tensor_tensor(swap[:, :, :, t], pair[:, :, :, 1 - t],
                                                 bcast(sign[:, :, :, t], [P, H, DH // 2]), ALU.mult)
                    last.then_inc(rot_read, 1)

                def masks(b, half, first=0, end=HALF):
                    for j in range(first, end):
                        hh = half * HALF + j
                        dve.wait_ge(scores_up, H * b + hh + 1)
                        if j == 0:
                            dve.wait_ge(o_up, 2 * b + half)
                        x = hh % 2
                        dve.tensor_tensor(scm[:, j, 0:2 * P], xps[:, x, 0:2 * P],
                                          mask[:, hh, :, :].rearrange("p a t -> p (a t)"), ALU.mult)
                        dve.tensor_tensor(scm[:, j, 2 * P:3 * P], xps[:, x, 2 * P:3 * P],
                                          mask[:, hh, 0, :], ALU.mult).then_inc(scores_masked, 1)

                def norm(b):
                    den, aa, ms, t, u = (sm[:, k, :, :] for k in range(5))
                    n = NV * b
                    dve.wait_ge(o_copied, 2 * b + 2)
                    dve.tensor_tensor(den, o[:, :, :, DH], invn[:, :, :], ALU.mult).then_inc(nv, 1)
                    dve.wait_ge(nv, n + 1)
                    dve.scalar_tensor_tensor(out=t, in0=den, scalar=-1.0, in1=den,
                                             op0=ALU.mult, op1=ALU.max).then_inc(nv, 1)
                    dve.wait_ge(nv, n + 2)
                    dve.tensor_scalar(t, t, 1.0, None, ALU.max).then_inc(nv, 1)
                    dve.wait_ge(nv, n + 3)
                    dve.reciprocal(den, t).then_inc(nv, 1)
                    dve.wait_ge(nv, n + 4)
                    dve.tensor_tensor(aa, den, invn[:, :, :], ALU.mult).then_inc(nv, 1)
                    dve.wait_ge(o_squared, b + 1)
                    dve.wait_ge(nv, n + 5)
                    dve.tensor_reduce(ms, on[:, :, :].rearrange("p s (h d) -> p s h d", h=H), AX_X, ALU.add)\
                        .then_inc(nv, 1)
                    dve.tensor_tensor(u, aa, aa, ALU.mult).then_inc(nv, 1)
                    dve.wait_ge(nv, n + 7)
                    dve.tensor_tensor(t, u, ms, ALU.mult).then_inc(nv, 1)
                    dve.wait_ge(nv, n + 8)
                    dve.tensor_scalar(u, t, 1.0 / DH, EPS, ALU.mult, ALU.add).then_inc(nv, 1)

                def normed(b):
                    n = NV * b
                    dve.wait_ge(ng, b + 1)
                    dve.tensor_tensor(sm[:, 5, :, :], sm[:, 3, :, :], sm[:, 1, :, :], ALU.mult).then_inc(nv, 1)
                    dve.wait_ge(nv, n + 10)
                    dve.tensor_tensor(on[:, :, :].rearrange("p s (h d) -> p (s h) d", h=H),
                                      o[:, :, :, 0:DH].rearrange("p s h d -> p (s h) d"),
                                      bcast(sm[:, 5, :, :].rearrange("p s (h o) -> p (s h) o", o=1),
                                            [P, ST * H, DH]), ALU.mult).then_inc(nv, 1)

                def oT_rest(b):
                    for st in range(ST):
                        dve.wait_ge(oT_hi, ST * b + st + 1)
                        dve.tensor_tensor(oT[:, 1, st, :, :], pps[:, 2 + st, :].rearrange("p (k t) -> p k t", k=KC),
                                          oT[:, 0, st, :, :].bitcast(F32), ALU.subtract).then_inc(oT_lo, 1)

                def out_rows(b):
                    for st in range(ST):
                        row = acc[:, bass.ds(ST * b + st, 1), :].rearrange("p a d -> p (a d)")
                        dve.wait_ge(out_up, ST * b + st + 1)
                        dve.wait_ge(h_made, b + 1)
                        dve.tensor_tensor(row, yps[:, st, :], row, ALU.add).then_inc(r_added, 1)

                def turn(b, after):
                    more = after > 0
                    if more:
                        ln_rows(b + 1)
                    if not (isinstance(b, int) and b == 0):
                        out_rows(b - 1)
                    masks(b, 0, 0, HALF // 2)
                    if more:
                        hT_rest(b + 1, 0)
                    masks(b, 0, HALF // 2)
                    if more:
                        hT_rest(b + 1, 1)
                        rotate(b + 1, 0, 0)
                    masks(b, 1)
                    if more:
                        rotate(b + 1, 0, 1)
                    norm(b)
                    normed(b)
                    if after > 1:
                        ln_stats(b + 2)
                    if more:
                        rotate(b + 1, 1, 0)
                        rotate(b + 1, 1, 1)
                    oT_rest(b)

                def weight_rest(n):
                    dve.wait_ge(w_hi, n + 1)
                    if n < NW - 1:
                        for k in range(KC):
                            last = dve.scalar_tensor_tensor(out=whl[:, 1, n, k, :], in0=wraw[n % 2][:, k, :],
                                                            scalar=rnw[:, k:k + 1],
                                                            in1=whl[:, 0, n, k, :].bitcast(F32),
                                                            op0=ALU.mult, op1=ALU.subtract)
                    else:
                        last = dve.tensor_tensor(whl[:, 1, n, :, :], wraw[n % 2],
                                                 whl[:, 0, n, :, :].bitcast(F32), ALU.subtract)
                    last.then_inc(w_lo, 1)

                ln_stats(0)
                dve.wait_ge(w_loaded[0], 16)
                dve.wait_ge(rnw_loaded, 16)
                weight_rest(0)
                ln_rows(0)
                dve.wait_ge(w_loaded[1], 16)
                weight_rest(1)
                hT_rest(0, 0)
                hT_rest(0, 1)
                weight_rest(2)
                weight_rest(3)
                for loaded in (*rot_loaded, invn_loaded):
                    dve.wait_ge(loaded, 16)
                rotate(0, 0, 0)
                rotate(0, 0, 1)
                weight_rest(4)
                dve.wait_ge(mask_loaded, 16)
                rotate(0, 1, 0)
                rotate(0, 1, 1)
                ln_stats(1)
                turn(0, 2)
                with dve.Fori(1, B - 2) as b:
                    turn(b, 2)
                turn(B - 2, 1)
                turn(B - 1, 0)
                out_rows(B - 1)

            @block.tensor
            def _(pe):
                def hT_turn(b, st):
                    pe.wait_ge(h_made, b + 1)
                    pe.wait_ge((v_copied, g_made)[st], ST * b)
                    for k in range(KC):
                        last = pe.transpose(pps[:, 2 + st, k * P:(k + 1) * P], h[:, st, k * P:(k + 1) * P],
                                            ident[:, :])
                    last.then_inc(hT_up, 1)

                def project(b, st, w):
                    if w == 0:
                        pe.wait_ge(hT_lo, ST * b + st + 1)
                    if w < 2:
                        n = 2 * ST * b + 2 * st + w
                        if not (isinstance(n, int) and n < 2):
                            pe.wait_ge(rot_read, n - 1)
                    else:
                        pe.wait_ge(v_copied if w == 2 else g_made, ST * b + st)
                        pe.wait_ge(hT_lo, ST * b + w - 1)
                    for n, (i, j) in enumerate(PASSES):
                        for k in range(KC):
                            last = pe.matmul(pps[:, w, :], hT[:, i, st, k, :], whl[:, j, w, k, :],
                                             start=(n == 0 and k == 0), stop=(n == 2 and k == KC - 1))
                    last.then_inc(proj_up, 1)

                def qkT_turn(b, u):
                    w, st = u // ST, u % ST
                    pe.wait_ge(qk_rotated, 2 * ST * b + 2 * st + w + 1)
                    if u >= 2:
                        pe.wait_ge(qkT_copied, 2 * ST * b + u - 1)
                    for k in range(KC):
                        last = pe.transpose(xps[:, u % 2, k * P:(k + 1) * P], qk[:, w, st, k * P:(k + 1) * P],
                                            ident[:, :])
                    last.then_inc(qkT_up, 1)

                def scores(b, half):
                    for hh in range(half * HALF, (half + 1) * HALF):
                        if hh < 2:
                            pe.wait_ge(qkT_copied, 2 * ST * b + 2 * ST)
                        else:
                            pe.wait_ge(scores_masked, H * b + hh - 1)
                        g, k = hh % HG, hh // HG
                        pe.matmul(xps[:, hh % 2, 0:S], kT[:, g, k, 0:P], qT[:, k, :],
                                  start=True, stop=True)
                        pe.matmul(xps[:, hh % 2, S:S + P], kT[:, g, k, P:S], qT[:, k, P:S],
                                  start=True, stop=True).then_inc(scores_up, 1)

                def values(b, half):
                    pe.wait_ge(scores_masked, H * b + (half + 1) * HALF)
                    pe.wait_ge(v_copied, ST * b + ST)
                    if half == 0:
                        pe.wait_ge(r_added, ST * b)
                    else:
                        pe.wait_ge(o_copied, 2 * b + 1)
                    n = DH + 1
                    for j in range(HALF):
                        hh = half * HALF + j
                        pe.matmul(yps[:, 0, j * n:(j + 1) * n], scm[:, j, 0:P], v[:, 0, hh, :],
                                  start=True, stop=True)
                        pe.matmul(yps[:, 1, j * n:(j + 1) * n], scm[:, j, P:2 * P], v[:, 0, hh, :],
                                  start=True, stop=False)
                        last = pe.matmul(yps[:, 1, j * n:(j + 1) * n], scm[:, j, 2 * P:3 * P], v[:, 1, hh, :],
                                         start=False, stop=True)
                    last.then_inc(o_up, 1)

                def oT_turn(b, more):
                    pe.wait_ge(on_gated, b + 1)
                    for st in range(ST):
                        pe.wait_ge((v_copied, g_made)[st], ST * (b + 1 + more))
                        for k in range(KC):
                            last = pe.transpose(pps[:, 2 + st, k * P:(k + 1) * P], on[:, st, k * P:(k + 1) * P],
                                                ident[:, :])
                        last.then_inc(oT_up, 1)

                def out_proj(b):
                    pe.wait_ge(o_copied, 2 * b + 2)
                    for st in range(ST):
                        pe.wait_ge(oT_lo, ST * b + st + 1)
                        for n, (i, j) in enumerate(PASSES):
                            for k in range(KC):
                                last = pe.matmul(yps[:, st, :], oT[:, i, st, k, :], whl[:, j, 4, k, :],
                                                 start=(n == 0 and k == 0), stop=(n == 2 and k == KC - 1))
                        last.then_inc(out_up, 1)

                def turn(b, more):
                    for u in range(2 * ST):
                        qkT_turn(b, u)
                    if not (isinstance(b, int) and b == 0):
                        out_proj(b - 1)
                    if more:
                        hT_turn(b + 1, 0)
                        hT_turn(b + 1, 1)
                    scores(b, 0)
                    if more:
                        project(b + 1, 0, 0)
                    values(b, 0)
                    scores(b, 1)
                    if more:
                        project(b + 1, 0, 1)
                    values(b, 1)
                    if more:
                        project(b + 1, 0, 2)
                        project(b + 1, 0, 3)
                        for w in range(4):
                            project(b + 1, 1, w)
                    oT_turn(b, more)

                pe.wait_ge(ident_loaded, 16)
                for st in range(ST):
                    hT_turn(0, st)
                for st in range(ST):
                    for w in range(4):
                        pe.wait_ge(w_lo, w + 1)
                        project(0, st, w)
                pe.wait_ge(w_lo, NW)
                turn(0, True)
                with pe.Fori(1, B - 1) as b:
                    turn(b, True)
                turn(B - 1, False)
                out_proj(B - 1)


def ffn_wkv_phase(nc, a, acc, ident, cols, cw, mask, xn):
    FS = F // I
    BB = TB // S
    QS = FS // BB
    LAG = BB
    CB = TB // (2 * P)
    CP = NT // 2
    NQ = NB * BB
    W1 = KC * I
    W2 = IC * D
    BR = 32

    with ExitStack() as ctx:
        def sb(name, shape, dt=F32):
            return ctx.enter_context(nc.sbuf_tensor(f"k_{name}_sb", shape, dt))

        def sem(name):
            return ctx.enter_context(nc.semaphore(f"k_{name}"))

        raw1 = sb("w1_raw", [P, W1])
        raw2 = sb("w2_raw", [P, W2])
        w1h = sb("w1_halves", [P, 2, 2, W1], F32R)
        w2h = sb("w2_halves", [P, 2, 2, W2], F32R)
        hid = sb("hidden", [P, IC, TB])
        hh = sb("hidden_halves", [P, 2, 2, IC, TB], F32R)
        b1 = sb("fc1_b", [P, F // P])
        b2h = sb("fc2_b_halves", [BR + 1, D], F32R)
        oneh = sb("one_rows_r", [BR + 1, P], F32R)
        xin = sb("x", [P, ST, D])
        kT = sb("kT", [P, KC, S])
        vT = sb("vT", [P, KC, S])
        pp = sb("pp", [P, KC, S + 1])
        av = sb("aa", [P, KC, S + 1])
        bv = sb("bb", [P, KC, S + 1])
        e1b = sb("e1b", [P, KC, S])
        e2b = sb("e2b", [P, KC, S])
        e1 = sb("e1", [P, KC, S])
        e2 = sb("e2", [P, KC, S])
        t1 = sb("t1", [P, KC, S])
        kr = [t[:, :, :].rearrange("p k s -> p (k s)").rearrange("p (s d) -> p s d", s=ST) for t in (e2, e1)]
        xT = t1[:, :, :].rearrange("p k s -> p (k s)").rearrange("p (s k t) -> p s k t", s=ST, k=KC)
        b2 = e1b[0:BR + 1, 0:D // S, :].rearrange("p k s -> p (k s)")
        one = e2[0:BR + 1, 0, 0:P]
        c_squares, c_rows = (t[:, :, :].rearrange("p k s -> p (k s)").rearrange("p (n d) -> p n d", n=2)
                             for t in (kT, t1))
        c_weight = e2b[:, :, :].rearrange("p k s -> p (k s)")[:, 0:D]
        decay = sb("decay", [P, KC])
        dexp = sb("decay_exp", [P, KC])
        u = sb("first", [P, KC])
        st6 = sb("bn6", [P, 2, ST, 6])
        mv = sb("mean_var", [P, 2, ST, 2])
        rstd = sb("rstd", [P, 2, 2, ST])
        consts = sb("consts", [P, 2, ST])
        gw = sb("gate_w", [P, KC, NE])
        ebias = sb("expert_bias", [P, NE])
        ones = sb("ones", [P, NE])
        score = sb("score", [P, ST, NE])
        biased = sb("biased", [P, ST, NE])
        top8 = sb("top8", [P, ST, 8])
        over = sb("over", [P, ST, NE])
        ties = sb("ties", [P, ST, NE])
        rank = sb("rank", [P, ST, NE])
        chosen = sb("chosen", [P, ST, NE])
        c_sums = score[:, 0, 0:2]
        c_scale = [biased[:, 0, 2 * n:2 * n + 2] for n in range(3)]
        inv_d = over[:, 0, 0:2]
        nover = sb("nover", [P, ST])
        total = sb("total", [P, ST])

        gps = ctx.enter_context(nc.psum_tensor("k_g_ps", [P, IC, TB], F32))
        dps = ctx.enter_context(nc.psum_tensor("k_d_ps", [P, BT, D], F32))
        xps = ctx.enter_context(nc.psum_tensor("k_x_ps", [P, ST, 512], F32))

        c_w_loaded = sem("c_w_loaded")
        c_squared = sem("c_squared")
        c_scale_step = sem("c_scale_step")
        c_rows_made = sem("c_rows_made")
        c_rows_up = sem("c_rows_up")
        c_hi = sem("c_hi")
        c_lo = sem("c_lo")
        const_loaded = sem("const_loaded")
        const_set = sem("const_set")
        act_passed = sem("act_passed")
        passed = sem("passed")
        w1_loaded = sem("w1_loaded")
        w1_hi = sem("w1_hi")
        w1_lo = sem("w1_lo")
        w2_loaded = sem("w2_loaded")
        w2_hi = sem("w2_hi")
        w2_lo = sem("w2_lo")
        b2_hi = sem("b2_hi")
        b2_lo = sem("b2_lo")
        first_up = sem("first_up")
        hid_made = sem("hid_made")
        hid_hi = sem("hid_hi")
        hid_lo = sem("hid_lo")
        down_up = sem("down_up")
        added = sem("added")
        x_loaded = sem("x_loaded")
        v_loaded = sem("v_loaded")
        x_added = sem("x_added")
        ln1_stats = sem("ln1_stats")
        ln1_step = sem("ln1_step")
        ln2_stats = sem("ln2_stats")
        ln2_step = sem("ln2_step")
        rows_made = sem("rows_made")
        rows_up = sem("rows_up")
        kT_copied = sem("kT_copied")
        decay_exp = sem("decay_exp")
        pp_made = sem("pp_made")
        d1_made = sem("d1_made")
        d2_made = sem("d2_made")
        q_made = sem("q_made")
        d3_made = sem("d3_made")
        d4_made = sem("d4_made")
        exps = sem("exps")
        bv_made = sem("bv_made")
        bb_made = sem("bb_made")
        aa_made = sem("aa_made")
        n2_made = sem("n2_made")
        n_made = sem("n_made")
        y_step = sem("y_step")
        y_made = sem("y_made")
        y_up = sem("y_up")
        y_added = sem("y_added")
        rows2_made = sem("rows2_made")
        cols_up = sem("cols_up")
        xT_copied = sem("xT_copied")
        xn_stored = sem("xn_stored")
        logits_up = sem("logits_up")
        logits_exp = sem("logits_exp")
        route = sem("route")

        xd = a["x"].rearrange("(b s p) d -> b p s d", p=P, s=ST)
        RS = 2 + 10 * ST
        def known(v):
            return isinstance(v, int)

        def beside(n):
            return CB + n if known(n) and CB + n < CP else None

        def rows(b, st):
            return acc[:, bass.ds(ST * b + st, 1), :].rearrange("p a d -> p (a d)")

        xn_rows = xn.rearrange("(b s p) d -> b p s d", p=P, s=ST)

        with nc.Block() as block:
            @block.sync
            def _(sp):
                def load_w(n, e1_, e2_):
                    if e1_ is not None:
                        sp.wait_ge(w1_lo, n + 2)
                        sp.dma_start(raw1[:, :], a["ffn_w"][e1_, :, 0:W1]).then_inc(w1_loaded, 16)
                    if e2_ is not None:
                        sp.wait_ge(w2_lo, n + 1)
                        sp.dma_start(raw2[:, :], a["ffn_w"][e2_, :, W1:W1 + W2]).then_inc(w2_loaded, 16)

                def load_x(b):
                    if not (known(b) and b == 0):
                        sp.wait_ge(x_added, ST * b)
                    sp.dma_start(xin[:, :, :], xd[b]).then_inc(x_loaded, 16)

                def load_v(b):
                    if not (known(b) and b == 0):
                        sp.wait_ge(n2_made, b)
                    sp.dma_start(vT[:, :, :], a["ctx"][b]).then_inc(v_loaded, 16)

                def store_xn(b):
                    sp.wait_ge(rows2_made, ST * (b + 1))
                    sp.dma_start(xn_rows[b], kr[1]).then_inc(xn_stored, 16)

                def quarter(m, hb):
                    for s in range(QS):
                        e = QS * hb + s
                        load_w(QS * m + s, (e + 2) % FS, (e + 1) % FS)
                        if s == 1 and not (known(m) and m == LAG):
                            store_xn(m - LAG - 1)
                        if s == 1:
                            load_x(m - LAG + 1)
                        if s == 3:
                            load_v(m - LAG + 1)

                sp.dma_start(c_weight, a["final_w"].partition_broadcast(P)).then_inc(c_w_loaded, 16)
                sp.dma_start(raw1[:, :], a["ffn_w"][0, :, 0:W1]).then_inc(w1_loaded, 16)
                sp.dma_start(raw2[:, :], a["ffn_w"][0, :, W1:W1 + W2]).then_inc(w2_loaded, 16)
                loads = ((b1[:, :], a["fc1_b"]), (b2[0:1, :], a["fc2_b"]),
                         (b2[BR:BR + 1, :], a["fc2_b"]), (decay[:, :], a["time_decay"]),
                         (u[:, :], a["time_first"]), (gw[:, :, :], a["gate_w"]),
                         (ebias[:, :], a["expert_bias"].partition_broadcast(P)))
                for dst, src in loads:
                    sp.dma_start(dst, src).then_inc(const_loaded, 16)
                sp.wait_ge(w1_lo, 1)
                sp.dma_start(raw1[:, :], a["ffn_w"][1, :, 0:W1]).then_inc(w1_loaded, 16)
                with sp.Fori(0, QS * LAG - 2) as e:
                    load_w(e, e + 2, e + 1)
                load_x(0)
                load_v(0)
                load_w(FS - 2, 0, FS - 1)
                load_w(FS - 1, 1, 0)
                for hb in range(BB):
                    quarter(LAG + hb, hb)
                with sp.Fori(2, NB - 1) as j:
                    for hb in range(BB):
                        quarter(BB * j + hb, hb)
                for s in range(QS):
                    load_w(QS * (NQ - 2) + s, s + 2, s + 1)
                    if s == 1:
                        store_xn(NQ - LAG - 3)
                    if s == 1:
                        load_x(NQ - LAG - 1)
                    if s == 3:
                        load_v(NQ - LAG - 1)
                for s in range(QS):
                    e = QS + s
                    load_w(QS * (NQ - 1) + s, e + 2 if e + 2 < FS else None, e + 1 if e + 1 < FS else None)
                    if s == 1:
                        store_xn(NQ - LAG - 2)
                    if s == 1:
                        load_x(NQ - LAG)
                    if s == 3:
                        load_v(NQ - LAG)
                store_xn(B - LAG - 1)
                for b in range(B - LAG + 1, B):
                    load_x(b)
                    load_v(b)
                    store_xn(b - 1)
                store_xn(B - 1)
                sp.wait_ge(xn_stored, 16 * B)

            @block.gpsimd
            def _(pool):
                for dst, value in ((consts[:, 0, :], EPS), (consts[:, 1, :], -0.5), (ones[:, :], 1.0),
                                   (pp[:, :, 0:1], NEG), (av[:, :, 0:1], 0.0), (bv[:, :, 0:1], 0.0),
                                   (one[:, :], 1.0), (b2h[:, :].bitcast(F32), 0.0), (inv_d, 1.0 / D)):
                    pool.memset(dst, value).then_inc(const_set, 1)
                pool.wait_ge(const_set, 9)

                def c_scales(q):
                    pool.wait_ge(c_squared, 2 * q + 2)
                    pool.wait_ge(c_rows_made, 2 * q)
                    pool.tensor_tensor(c_scale[0], c_sums, inv_d, ALU.mult).then_inc(c_scale_step, 1)
                    pool.wait_ge(c_scale_step, 3 * q + 1)
                    pool.tensor_tensor(c_scale[1], c_scale[0], consts[:, 0, :], ALU.add).then_inc(c_scale_step, 1)
                    pool.wait_ge(c_scale_step, 3 * q + 2)
                    pool.tensor_tensor(c_scale[2], c_scale[1], consts[:, 1, :], ALU.pow).then_inc(c_scale_step, 1)

                def w1_rest(n, par):
                    pool.wait_ge(w1_hi, n + 1)
                    pool.tensor_tensor(w1h[:, par, 1, :], raw1[:, :], w1h[:, par, 0, :].bitcast(F32),
                                       ALU.subtract).then_inc(w1_lo, 1)

                def w2_rest(n, par):
                    pool.wait_ge(w2_hi, n + 1)
                    pool.tensor_tensor(w2h[:, par, 1, :], raw2[:, :], w2h[:, par, 0, :].bitcast(F32),
                                       ALU.subtract).then_inc(w2_lo, 1)

                def hidden_rest(n, par):
                    for c in range(IC):
                        pool.wait_ge(hid_hi, IC * n + c + 1)
                        pool.tensor_tensor(hh[:, par, 1, c, :], hid[:, c, :], hh[:, par, 0, c, :].bitcast(F32),
                                           ALU.subtract).then_inc(hid_lo, 1)

                def scales(b, ln, stats, step):
                    pool.wait_ge(stats, 2 * ST * (b + 1))
                    pool.tensor_tensor(rstd[:, ln, 0, :], mv[:, ln, :, 1], consts[:, 0, :], ALU.add).then_inc(step, 1)
                    pool.wait_ge(step, 2 * b + 1)
                    pool.tensor_tensor(rstd[:, ln, 1, :], rstd[:, ln, 0, :], consts[:, 1, :], ALU.pow).then_inc(step, 1)

                def differences(b):
                    pool.wait_ge(pp_made, b + 1)
                    pool.tensor_tensor(e2b[:, :, :], kT[:, :, :], pp[:, :, 1:S + 1], ALU.subtract).then_inc(d2_made, 1)

                def differences_out(b):
                    pool.wait_ge(d4_made, b + 1)
                    pool.tensor_tensor(e1[:, :, :], pp[:, :, 0:S], e1[:, :, :], ALU.subtract).then_inc(d3_made, 1)

                def values(b):
                    pool.wait_ge(v_loaded, 16 * (b + 1))
                    pool.wait_ge(exps, 4 * b + 2)
                    pool.tensor_tensor(kT[:, :, :], e2b[:, :, :], vT[:, :, :], ALU.mult).then_inc(bv_made, 1)

                def values_out(b):
                    if not (known(b) and b == 0):
                        pool.wait_ge(logits_up, b)
                    pool.wait_ge(exps, 4 * b + 3)
                    pool.tensor_tensor(t1[:, :, :], e2[:, :, :], vT[:, :, :], ALU.mult).then_inc(n2_made, 1)

                def numerator(b):
                    pool.wait_ge(aa_made, b + 1)
                    pool.wait_ge(exps, 4 * b + 4)
                    pool.tensor_tensor(kT[:, :, :], e1[:, :, :], av[:, :, 0:S], ALU.mult).then_inc(n_made, 1)
                    pool.wait_ge(n_made, 2 * b + 1)
                    pool.wait_ge(n2_made, b + 1)
                    pool.tensor_tensor(kT[:, :, :], kT[:, :, :], t1[:, :, :], ALU.add).then_inc(n_made, 1)

                def slot(m, s, left=None):
                    n = QS * m + s
                    w = not (known(m) and m < LAG)
                    b = m - LAG
                    if w and s == 2:
                        values(b)
                    if w and s == 3:
                        numerator(b)
                    if beside(n):
                        c_scales(beside(n))
                    if left is None or left > 2:
                        w1_rest(n + 2, s % 2)
                    if left is None or left > 1:
                        w2_rest(n + 1, (s + 1) % 2)
                    if w and s == 0:
                        scales(b, 0, ln1_stats, ln1_step)
                    if w and s == 1:
                        differences(b)
                    if left is None or left > 1:
                        hidden_rest(n + 1, (s + 1) % 2)
                    if w and s == 0 and not (known(b) and b == 0):
                        scales(b - 1, 1, ln2_stats, ln2_step)
                    if w and s == 1:
                        differences_out(b)
                    if w and s == 2:
                        values_out(b)

                for q in range(CB):
                    c_scales(q)
                w1_rest(0, 0)
                w2_rest(0, 0)
                w1_rest(1, 1)
                hidden_rest(0, 0)
                for m in range(LAG + 1):
                    for s in range(QS):
                        slot(m, s)
                with pool.Fori(LAG + 1, NQ - 1) as m:
                    for s in range(QS):
                        slot(m, s)
                for s in range(QS):
                    slot(NQ - 1, s, QS - s)
                for b in range(B - LAG, B):
                    scales(b, 0, ln1_stats, ln1_step)
                    scales(b - 1, 1, ln2_stats, ln2_step)
                    differences(b)
                    differences_out(b)
                    values(b)
                    values_out(b)
                    numerator(b)
                scales(B - 1, 1, ln2_stats, ln2_step)

            @block.scalar
            def _(act):
                def w1_first(n, par):
                    act.wait_ge(w1_loaded, 16 * (n + 1))
                    if not (known(n) and n < 2):
                        act.wait_ge(first_up, IC * (n - 1))
                    act.activation(w1h[:, par, 0, :], raw1[:, :], ACT.Copy).then_inc(w1_hi, 1)

                def w2_first(n, par):
                    act.wait_ge(w2_loaded, 16 * (n + 1))
                    if not (known(n) and n < 2):
                        act.wait_ge(down_up, BT * (n - 1))
                    act.activation(w2h[:, par, 0, :], raw2[:, :], ACT.Copy).then_inc(w2_hi, 1)

                def hidden(n, s, hb):
                    for c in range(IC):
                        act.wait_ge(first_up, IC * n + c + 1)
                        if not (known(n) and n == 0):
                            act.wait_ge(hid_lo, IC * (n - 1) + c + 1)
                        act.wait_ge(const_loaded, 112).then_inc(act_passed, 1)
                        act.activation(hid[:, c, :], gps[:, c, :], ACT.Gelu_apprx_tanh,
                                       bias=b1[:, bass.ds(IC * QS * hb + IC * s + c, 1)]).then_inc(hid_made, 1)
                    for c in range(IC):
                        act.wait_ge(hid_made, IC * n + c + 1)
                        if not (known(n) and n < 2):
                            act.wait_ge(down_up, BT * (n - 1))
                        act.activation(hh[:, s % 2, 0, c, :], hid[:, c, :], ACT.Copy).then_inc(hid_hi, 1)

                def c_square(q):
                    if q:
                        act.wait_ge(c_squared, 2 * q)
                        act.wait_ge(c_scale_step, 3 * q - 2)
                    for n in range(2):
                        act.activation(c_squares[:, n, :], acc[:, 2 * q + n, :], ACT.Square,
                                       accum_out=c_sums[:, n:n + 1]).then_inc(c_squared, 1)

                def c_first(q):
                    for n in range(2):
                        t = 2 * q + n
                        act.wait_ge(c_rows_up, t + 1)
                        act.activation(cols[:, 0, :, P * t:P * t + P],
                                       xps[:, n, :].rearrange("p (k t) -> p k t", k=KC), ACT.Copy).then_inc(c_hi, 1)

                def k_columns(b):
                    if not (known(b) and b == 0):
                        act.wait_ge(y_made, b)
                    for st in range(ST):
                        act.wait_ge(rows_up, ST * b + st + 1)
                        act.activation(kT[:, :, st * P:(st + 1) * P],
                                       xps[:, st, :].rearrange("p (k t) -> p k t", k=KC), ACT.Copy)\
                           .then_inc(kT_copied, 1)

                def x_columns(b):
                    act.wait_ge(y_made, b + 1)
                    for st in range(ST):
                        act.wait_ge(cols_up, ST * b + st + 1)
                        act.activation(xT[:, st, :, :], xps[:, st, :].rearrange("p (k t) -> p k t", k=KC),
                                       ACT.Copy).then_inc(xT_copied, 1)

                def logit_exps(b):
                    act.wait_ge(logits_up, b + 1)
                    act.activation(score[:, :, :], xps[:, 0, 0:ST * NE].rearrange("p (s e) -> p s e", s=ST),
                                   ACT.Exp, scale=-1.0).then_inc(logits_exp, 1)

                def wkv_exps(b):
                    for ready, buf in ((d1_made, e1b), (d2_made, e2b), (d4_made, e2), (d3_made, e1)):
                        act.wait_ge(ready, b + 1)
                        act.activation(buf[:, :, :], buf[:, :, :], ACT.Exp).then_inc(exps, 1)

                def slot(m, s, hb, left=None):
                    n = QS * m + s
                    w = not (known(m) and m < LAG)
                    b = m - LAG
                    if beside(n):
                        c_square(beside(n))
                    if left is None or left > 2:
                        w1_first(n + 2, s % 2)
                    if left is None or left > 1:
                        w2_first(n + 1, (s + 1) % 2)
                        hidden(n + 1, (s + 1) % QS, hb if s < QS - 1 else (hb + 1) % BB)
                        if beside(n):
                            c_first(beside(n))
                    if w and s == 0:
                        k_columns(b)
                    if w and s == 1:
                        if not (known(b) and b == 0):
                            x_columns(b - 1)
                        wkv_exps(b)
                        if not (known(b) and b == 0):
                            logit_exps(b - 1)

                for q in range(CB):
                    c_square(q)
                w1_first(0, 0)
                c_first(0)
                w2_first(0, 0)
                for q in range(1, CB):
                    c_first(q)
                w1_first(1, 1)
                act.wait_ge(const_loaded, 112)
                act.activation(dexp[:, :], decay[:, :], ACT.Exp).then_inc(decay_exp, 1)
                act.wait_ge(const_set, 9)
                for row in (0, BR):
                    act.activation(b2h[row:row + 1, :], b2[row:row + 1, :], ACT.Copy).then_inc(b2_hi, 1)
                act.activation(oneh[:, :], one[:, :], ACT.Copy).then_inc(b2_hi, 1)
                hidden(0, 0, 0)
                for m in range(LAG + BB):
                    for s in range(QS):
                        slot(m, s, m % BB)
                with act.Fori(2, NB - 1) as j:
                    for hb in range(BB):
                        for s in range(QS):
                            slot(BB * j + hb, s, hb)
                for hb in range(BB):
                    for s in range(QS):
                        slot(NQ - BB + hb, s, hb, FS - QS * hb - s)
                for b in range(B - LAG, B):
                    k_columns(b)
                    x_columns(b - 1)
                    wkv_exps(b)
                    logit_exps(b - 1)
                x_columns(B - 1)
                act.wait_ge(route, RS * (B - 1))
                logit_exps(B - 1)

            @block.vector
            def _(dve):
                def stats(b, ln, sem_):
                    for st in range(ST):
                        dve.bn_stats(st6[:, ln, st, :], rows(b, st)).then_inc(sem_, 1)
                    dve.wait_ge(sem_, 2 * ST * b + ST).then_inc(passed, 1)
                    for st in range(ST):
                        dve.bn_aggr(mv[:, ln, st, :], st6[:, ln, st, :]).then_inc(sem_, 1)

                def ln_rows(b, ln, step, made):
                    dve.wait_ge(step, 2 * b + 2)
                    for st in range(ST):
                        dve.tensor_scalar(kr[ln][:, st, :], rows(b, st), mv[:, ln, st, 0:1],
                                          rstd[:, ln, 1, st:st + 1], ALU.subtract, ALU.mult).then_inc(made, 1)

                def x1(b):
                    dve.wait_ge(x_loaded, 16 * (b + 1))
                    for st in range(ST):
                        dve.tensor_tensor(rows(b, st), rows(b, st), xin[:, st, :], ALU.add).then_inc(x_added, 1)
                    dve.wait_ge(x_added, ST * b + ST).then_inc(passed, 1)
                    stats(b, 0, ln1_stats)

                def y_rows(b):
                    for st in range(ST):
                        dve.wait_ge(y_up, ST * b + st + 1)
                        dve.tensor_tensor(rows(b, st), xps[:, st, :], rows(b, st), ALU.add).then_inc(y_added, 1)
                    dve.wait_ge(y_added, ST * b + ST).then_inc(passed, 1)
                    stats(b, 1, ln2_stats)

                def maxima(b):
                    dve.wait_ge(kT_copied, ST * b + ST)
                    for c in range(KC):
                        last = dve.tensor_tensor_scan(pp[:, c, 1:S + 1], bcast(dexp[:, c:c + 1], [P, S]),
                                                      kT[:, c, :], NEG, ALU.add, ALU.max)
                    last.then_inc(pp_made, 1)
                    dve.wait_ge(pp_made, b + 1).then_inc(passed, 1)
                    if not (known(b) and b == 0):
                        dve.wait_ge(cols_up, ST * b)
                        dve.wait_ge(xn_stored, 16 * b)
                    for c in range(KC):
                        last = dve.scalar_tensor_tensor(out=e1[:, c, :], in0=kT[:, c, :], scalar=u[:, c:c + 1],
                                                        in1=pp[:, c, 0:S], op0=ALU.add, op1=ALU.max)
                    last.then_inc(q_made, 1)
                    for c in range(KC):
                        last = dve.scalar_tensor_tensor(out=e1b[:, c, :], in0=pp[:, c, 0:S],
                                                        scalar=dexp[:, c:c + 1], in1=pp[:, c, 1:S + 1],
                                                        op0=ALU.add, op1=ALU.subtract)
                    last.then_inc(d1_made, 1)
                    dve.wait_ge(q_made, b + 1)
                    for c in range(KC):
                        last = dve.scalar_tensor_tensor(out=e2[:, c, :], in0=kT[:, c, :], scalar=u[:, c:c + 1],
                                                        in1=e1[:, c, :], op0=ALU.add, op1=ALU.subtract)
                    last.then_inc(d4_made, 1)

                def bb_scan(b):
                    dve.wait_ge(exps, 4 * b + 2)
                    for c in range(KC):
                        last = dve.tensor_tensor_scan(bv[:, c, 1:S + 1], e1b[:, c, :], e2b[:, c, :], 0.0,
                                                      ALU.mult, ALU.add)
                    last.then_inc(bb_made, 1)

                def aa_scan(b):
                    dve.wait_ge(bv_made, b + 1)
                    for c in range(KC):
                        last = dve.tensor_tensor_scan(av[:, c, 1:S + 1], e1b[:, c, :], kT[:, c, :], 0.0,
                                                      ALU.mult, ALU.add)
                    last.then_inc(aa_made, 1)

                def quotient(b):
                    dve.wait_ge(aa_made, b + 1)
                    dve.wait_ge(bb_made, b + 1)
                    dve.wait_ge(exps, 4 * b + 4)
                    dve.tensor_tensor(e1b[:, :, :], e1[:, :, :], bv[:, :, 0:S], ALU.mult).then_inc(y_step, 1)
                    dve.wait_ge(y_step, 3 * b + 1)
                    dve.tensor_tensor(e1b[:, :, :], e1b[:, :, :], e2[:, :, :], ALU.add).then_inc(y_step, 1)
                    dve.wait_ge(y_step, 3 * b + 2)
                    dve.reciprocal(e1b[:, :, :], e1b[:, :, :]).then_inc(y_step, 1)
                    dve.wait_ge(y_step, 3 * b + 3)
                    dve.wait_ge(n_made, 2 * b + 2)
                    dve.tensor_tensor(e1[:, :, :], kT[:, :, :], e1b[:, :, :], ALU.mult).then_inc(y_made, 1)

                def routed(b):
                    n = RS * b
                    dve.wait_ge(logits_exp, b + 1)
                    dve.tensor_scalar(score[:, :, :], score[:, :, :], 1.0, None, ALU.add).then_inc(route, 1)
                    dve.wait_ge(route, n + 1)
                    dve.reciprocal(score[:, :, :], score[:, :, :]).then_inc(route, 1)
                    n += 2

                    def stage(k, op):
                        dve.wait_ge(route, n + ST * k).then_inc(passed, 1)
                        for st in range(ST):
                            op(st).then_inc(route, 1)

                    stage(0, lambda st: dve.tensor_tensor(biased[:, st, :], score[:, st, :], ebias[:, :], ALU.add))
                    stage(1, lambda st: dve.max(top8[:, st, :], biased[:, st, :]))
                    stage(2, lambda st: dve.tensor_scalar(over[:, st, :], biased[:, st, :],
                                                          top8[:, st, TOPK - 1:TOPK], 0.0, ALU.is_gt, ALU.add,
                                                          accum_out=nover[:, st:st + 1]))
                    stage(3, lambda st: dve.tensor_scalar(ties[:, st, :], biased[:, st, :],
                                                          top8[:, st, TOPK - 1:TOPK], None, ALU.is_equal))
                    stage(4, lambda st: dve.tensor_tensor_scan(rank[:, st, :], ones[:, :], ties[:, st, :],
                                                               nover[:, st:st + 1], ALU.mult, ALU.add))
                    stage(5, lambda st: dve.scalar_tensor_tensor(out=chosen[:, st, :], in0=rank[:, st, :],
                                                                 scalar=float(TOPK), in1=ties[:, st, :],
                                                                 op0=ALU.is_le, op1=ALU.mult))
                    def kept(st):
                        return mask[:, :, bass.ds(ST * b + st, 1)].rearrange("p e o -> p (e o)")

                    stage(6, lambda st: dve.tensor_tensor(kept(st), over[:, st, :], chosen[:, st, :], ALU.add))
                    stage(7, lambda st: dve.scalar_tensor_tensor(out=chosen[:, st, :], in0=kept(st), scalar=1.0,
                                                                 in1=score[:, st, :], op0=ALU.mult, op1=ALU.mult,
                                                                 accum_out=total[:, st:st + 1]))
                    stage(8, lambda st: dve.reciprocal(total[:, st:st + 1], total[:, st:st + 1]))
                    stage(9, lambda st: dve.tensor_scalar(
                        cw[:, :, bass.ds(ST * b + st, 1)].rearrange("p e o -> p (e o)"),
                        chosen[:, st, :], total[:, st:st + 1], None, ALU.mult))

                def c_scaled(q):
                    dve.wait_ge(c_scale_step, 3 * q + 3)
                    dve.wait_ge(c_rows_up, 2 * q)
                    for n in range(2):
                        dve.scalar_tensor_tensor(out=c_rows[:, n, :], in0=acc[:, 2 * q + n, :],
                                                 scalar=c_scale[2][:, n:n + 1], in1=c_weight,
                                                 op0=ALU.mult, op1=ALU.mult).then_inc(c_rows_made, 1)

                def c_rest(q):
                    for n in range(2):
                        t = 2 * q + n
                        dve.wait_ge(c_hi, t + 1)
                        dve.tensor_tensor(cols[:, 1, :, P * t:P * t + P],
                                          xps[:, n, :].rearrange("p (k t) -> p k t", k=KC),
                                          cols[:, 0, :, P * t:P * t + P].bitcast(F32), ALU.subtract)\
                           .then_inc(c_lo, 1)

                def add(n, j):
                    if not (known(n) and n < 1):
                        dve.wait_ge(added, BT * n)
                    for t in range(BT):
                        dve.wait_ge(down_up, BT * n + t + 1)
                        row = acc[:, bass.ds(BT * j + t, 1), :].rearrange("p a d -> p (a d)")
                        dve.tensor_tensor(row, dps[:, t, :], row, ALU.add).then_inc(added, 1)

                def slot(m, s, j, hb):
                    n = QS * m + s
                    if beside(n):
                        c_scaled(beside(n))
                    if not (known(n) and n == 0):
                        add(n - 1, j if (s or hb) else j - 1)
                    if beside(n):
                        c_rest(beside(n))
                    if known(m) and m < LAG:
                        return
                    b = m - LAG
                    before = not (known(b) and b == 0)
                    if s == 0:
                        dve.wait_ge(added, BT * n)
                        x1(b)
                        if before:
                            y_rows(b - 1)
                        ln_rows(b, 0, ln1_step, rows_made)
                        if before:
                            ln_rows(b - 1, 1, ln2_step, rows2_made)
                    elif s == 1:
                        maxima(b)
                    elif s == 2:
                        bb_scan(b)
                        if before:
                            routed(b - 1)
                        aa_scan(b)
                    else:
                        quotient(b)

                dve.wait_ge(c_w_loaded, 16)
                for q in range(CB):
                    c_scaled(q)
                for q in range(CB):
                    c_rest(q)
                dve.wait_ge(decay_exp, 1)
                dve.wait_ge(const_loaded, 112)
                dve.wait_ge(const_set, 9)
                dve.tensor_scalar(dexp[:, :], dexp[:, :], -1.0, None, ALU.mult).then_inc(passed, 1)
                dve.wait_ge(b2_hi, 3)
                dve.tensor_tensor(b2h[BR:BR + 1, :], b2[BR:BR + 1, :], b2h[BR:BR + 1, :].bitcast(F32),
                                  ALU.subtract).then_inc(b2_lo, 1)
                dve.wait_ge(passed, 1)
                for m in range(2 * LAG):
                    for s in range(QS):
                        slot(m, s, m // BB, m % BB)
                with dve.Fori(2, NB) as j:
                    for hb in range(BB):
                        for s in range(QS):
                            slot(BB * j + hb, s, j, hb)
                add(QS * NQ - 1, NB - 1)
                dve.wait_ge(added, BT * QS * NQ)
                x1(B - LAG)
                for b in range(B - LAG, B):
                    y_rows(b - 1)
                    ln_rows(b, 0, ln1_step, rows_made)
                    ln_rows(b - 1, 1, ln2_step, rows2_made)
                    maxima(b)
                    if b + 1 < B:
                        x1(b + 1)
                    bb_scan(b)
                    if b + 1 < B:
                        routed(b - 1)
                    aa_scan(b)
                    quotient(b)
                y_rows(B - 1)
                ln_rows(B - 1, 1, ln2_step, rows2_made)
                routed(B - 2)
                routed(B - 1)

            @block.tensor
            def _(pe):
                def w1(par, half, k, c):
                    return w1h[:, par, half, k * I + c * P:k * I + (c + 1) * P]

                def w2(par, half, c):
                    return w2h[:, par, half, c * D:(c + 1) * D]

                def c_turn(q):
                    for n in range(2):
                        t = 2 * q + n
                        pe.wait_ge(c_rows_made, t + 1)
                        if q:
                            pe.wait_ge(c_lo, t - 1)
                        turned(n, lambda k: c_rows[:, n, k * P:(k + 1) * P]).then_inc(c_rows_up, 1)

                def first(n, par, j):
                    if known(n) and n in (0, FS):
                        pe.wait_ge(c_lo, BT if n == 0 else NT)
                    pe.wait_ge(w1_lo, n + 1)
                    for c in range(IC):
                        if not (known(n) and n == 0):
                            pe.wait_ge(hid_made, IC * (n - 1) + c + 1)
                        for m, (x, y) in enumerate(PASSES):
                            for k in range(KC):
                                last = pe.matmul(gps[:, c, :], w1(par, x, k, c), cols[:, y, k, bass.ds(j * TB, TB)],
                                                 start=(m == 0 and k == 0), stop=(m == 2 and k == KC - 1))
                        last.then_inc(first_up, 1)

                def down(n, par, biased_):
                    pe.wait_ge(hid_lo, IC * (n + 1))
                    pe.wait_ge(w2_lo, n + 1)
                    for t in range(BT):
                        if not (known(n) and n == 0):
                            pe.wait_ge(added, BT * (n - 1) + t + 1)
                        for m, (x, y) in enumerate(PASSES):
                            for c in range(IC):
                                last = pe.matmul(dps[:, t, :], hh[:, par, x, c, t * P:(t + 1) * P], w2(par, y, c),
                                                 start=(m == 0 and c == 0),
                                                 stop=(m == 2 and c == IC - 1 and not biased_))
                        if biased_:
                            last = pe.matmul(dps[:, t, :], oneh[:, :], b2h[:, :], start=False, stop=True)
                        last.then_inc(down_up, 1)

                def turned(st, src):
                    for k in range(KC):
                        last = pe.transpose(xps[:, st, k * P:(k + 1) * P], src(k), ident[:, :])
                    return last

                def k_turn(b):
                    for st in range(ST):
                        pe.wait_ge(rows_made, ST * b + st + 1)
                        if not (known(b) and b == 0):
                            pe.wait_ge(y_added, ST * b)
                        turned(st, lambda k: kr[0][:, st, k * P:(k + 1) * P]).then_inc(rows_up, 1)

                def logits(b):
                    pe.wait_ge(xT_copied, ST * b + ST)
                    for st in range(ST):
                        for k in range(KC):
                            last = pe.matmul(xps[:, 0, st * NE:(st + 1) * NE], xT[:, st, k, :], gw[:, k, :],
                                             start=(k == 0), stop=(k == KC - 1))
                    last.then_inc(logits_up, 1)

                def y_turn(b):
                    pe.wait_ge(y_made, b + 1)
                    if not (known(b) and b == 0):
                        pe.wait_ge(logits_exp, b)
                    for st in range(ST):
                        turned(st, lambda k: e1[:, k, st * P:(st + 1) * P]).then_inc(y_up, 1)

                def x_turn(b, b_next):
                    for st in range(ST):
                        pe.wait_ge(rows2_made, ST * b + st + 1)
                        if b_next is not None:
                            pe.wait_ge(kT_copied, ST * b_next + ST)
                        turned(st, lambda k: kr[1][:, st, k * P:(k + 1) * P]).then_inc(cols_up, 1)

                def slot(m, s, j, hb, last=False):
                    n = QS * m + s
                    w = not (known(m) and m < LAG)
                    b = m - LAG
                    before = w and not (known(b) and b == 0)
                    if not last:
                        first(n + 1, (s + 1) % 2, j + 1 if hb == BB - 1 and s == QS - 1 else j)
                    if beside(n):
                        c_turn(beside(n))
                    if s == 0 and before:
                        y_turn(b - 1)
                    if s == 1 and before:
                        x_turn(b - 1, b)
                    down(n, s % 2, s == 0 and hb == 0)
                    if s == 0 and w:
                        k_turn(b)
                    if s == 1 and before:
                        logits(b - 1)

                for q in range(CB):
                    c_turn(q)
                first(0, 0, 0)
                pe.wait_ge(b2_lo, 1)
                for m in range(LAG + BB):
                    for s in range(QS):
                        slot(m, s, m // BB, m % BB)
                with pe.Fori(2, NB - 1) as j:
                    for hb in range(BB):
                        for s in range(QS):
                            slot(BB * j + hb, s, j, hb)
                for hb in range(BB):
                    for s in range(QS):
                        slot(NQ - BB + hb, s, NB - 1, hb, hb == BB - 1 and s == QS - 1)
                for b in range(B - LAG, B):
                    y_turn(b - 1)
                    k_turn(b)
                    x_turn(b - 1, b)
                    logits(b - 1)
                y_turn(B - 1)
                x_turn(B - 1, None)
                logits(B - 1)


def moe_phase(nc, a, acc, ident, cw, mask, xn, listed, yr, out):
    W1 = 2 * KC * I
    W2 = IC * D
    UN = SU + RU
    YW = 4
    PLACED = 19

    with ExitStack() as ctx:
        def sb(name, shape, dt=F32):
            return ctx.enter_context(nc.sbuf_tensor(f"m_{name}_sb", shape, dt))

        def sem(name):
            return ctx.enter_context(nc.semaphore(f"m_{name}"))

        raw1 = sb("w1_raw", [P, 2, W1])
        raw2 = sb("w2_raw", [P, 2, W2])
        w1h = sb("w1_halves", [P, 2, 2, W1], F32R)
        w2h = sb("w2_halves", [P, 2, 2, W2], F32R)
        xr = sb("x_rows", [P, 2, UR, D])
        xh = sb("xT_halves", [P, 2, 2, KC, UT], F32R)
        gate = sb("gate", [P, IC, UT])
        hid = sb("hidden", [P, IC, UT])
        hh = sb("hidden_halves", [P, 2, 2, IC, UT], F32R)
        y = sb("y_rows", [P, 2, UR, D])
        yg = sb("y_of_tile", [P, YW, TOPK, D])
        consts = sb("routing_consts", [P, P + NE * NT + SU + RU + 1])
        at = np.cumsum([0, P, NE * NT, SU, RU, 1])
        before, same, starts, unit_no, expert_row = (consts[:, at[n]:at[n + 1]] for n in range(5))
        ones = sb("ones", [P, P])
        ids = sb("choice_ids", [P, NT, TOPK], I32)
        unused = sb("unused_places", [LR, P], I32)
        tot = sb("tile_counts", [P, NE, NT])
        incl = sb("counts_incl", [P, NE, NT])
        rank = sb("rank", [P, NE, NT])
        over = sb("units_over", [P, NE, SU])
        units = sb("units", [P, NE])
        ends = sb("unit_ends", [P, NE])
        first = sb("first_place", [P, NE])
        turned = sb("mask_turned", [P, NT, NE])
        nth = sb("nth_chosen", [P, NT, NE])
        pick = sb("picked", [P, TOPK, NT, NE])
        place = sb("places", [P, TOPK, NT])
        placei = sb("places_int", [P, TOPK, NT], I32)
        wk = sb("place_weights", [P, TOPK, NT])
        past = sb("experts_past", [P, RU, NE - 1])
        unit_e = sb("unit_expert", [P, RU])
        w_rows = sb("weight_rows", [P, RU])
        list_i = sb("list_int", [LR, P], I32)
        token_i = sb("list_tokens_int", [LR, P], I32)
        list_f = sb("list", [LR, 2, P])
        listT = sb("list_turned", [P, 2, LR])
        w_at = sb("w_at", [P, 2, 1], I32)
        x_at = sb("x_at", [P, 2, UR], I32)
        y_at = sb("y_at", [P, 2, UR], I32)

        xps = ctx.enter_context(nc.psum_tensor("m_x_ps", [P, UR, 512], F32))
        gps = ctx.enter_context(nc.psum_tensor("m_g_ps", [P, 2, 2, IC, UT], F32))
        dps = ctx.enter_context(nc.psum_tensor("m_d_ps", [P, UR, D], F32))

        const_loaded = sem("const_loaded")
        ids_loaded = sem("ids_loaded")
        const_set = sem("const_set")
        pool_passed = sem("pool_passed")
        emptied = sem("list_emptied")
        unused_loaded = sem("unused_loaded")
        ranks_up = sem("ranks_up")
        rt = sem("routing_step")
        scattered = sem("scattered")
        list_loaded = sem("list_loaded")
        list_made = sem("list_made")
        list_up = sem("list_up")
        at_set = sem("at_set")
        w1_got = [sem("w1_got_even"), sem("w1_got_odd")]
        w2_got = [sem("w2_got_even"), sem("w2_got_odd")]
        x_got = [[sem(f"x_got_{n}_{h}") for h in range(UR)] for n in ("even", "odd")]
        s1_got = [sem("s1_got_even"), sem("s1_got_odd")]
        s2_got = [sem("s2_got_even"), sem("s2_got_odd")]
        sx_got = [sem("sx_got_even"), sem("sx_got_odd")]
        w1_hi = sem("w1_hi")
        w1_lo = sem("w1_lo")
        w2_hi = sem("w2_hi")
        w2_lo = sem("w2_lo")
        x_up = sem("x_up")
        x_hi = sem("x_hi")
        x_lo = sem("x_lo")
        first_up = sem("first_up")
        gate_made = sem("gate_made")
        hid_made = sem("hid_made")
        hid_hi = sem("hid_hi")
        hid_lo = sem("hid_lo")
        down_up = sem("down_up")
        added = sem("added")
        y_made = sem("y_made")
        y_at_set = sem("y_at_set")
        y_stored = [sem("y_stored_even"), sem("y_stored_odd")]
        y_got = [sem(f"y_got_{r}") for r in range(YW)]
        summed = sem("summed")
        out_stored = sem("out_stored")

        class Unit:

            def __init__(self, i, c):
                self.i, self.c = i, c
                self.known = isinstance(i, int)
                self.n = 2 * i + c
                self.par = c % 2
                self.routed = not self.known or c >= SU
                self.exists = not self.known or c < UN
                self.u = 2 * i + (c - SU)
                self.turn = i + (c - SU) // 2
                self.splits = self.exists and (self.routed or c < 2)
                self.split = 2 * i + (c - (SU - 2) if self.routed else c)

                self.lists = self.known and c == SU - 2

            def __add__(self, k):
                return Unit(self.i, self.c + k)

            def first(self, n):
                return self.known and self.c < n

        HEAD, TAIL = SU + 2, 5

        def slots(eng, slot, start=0, end=UN - TAIL):
            for c in range(start, HEAD):
                slot(Unit(0, c))
            turns = (end - HEAD) // 2
            with eng.Fori(0, turns) as i:
                slot(Unit(i, HEAD))
                slot(Unit(i, HEAD + 1))
            for c in range(HEAD + 2 * turns, UN):
                slot(Unit(0, c))

        yd = yr[0:TOPK * B * S, :].rearrange("(k t p) d -> t p k d", k=TOPK, p=P)
        xd = xn.rearrange("(u h p) d -> u p h d", p=P, h=UR)
        out_rows = out.rearrange("(t p) d -> t p d", p=P)
        w1_rows = a["moe_w1"].rearrange("e p c -> (e p) c")
        w2_rows = a["moe_w2"].rearrange("e p c -> (e p) c")

        with nc.Block() as block:
            @block.sync
            def _(sp):
                def x_shared(g):
                    if g > 1:
                        sp.wait_ge(x_up, UR * (g - 1))
                    sp.dma_start(xr[:, g % 2, :, :], xd[g]).then_inc(sx_got[g % 2], 16)

                sp.dma_start(consts[:, :], a["routing"]).then_inc(const_loaded, 16)
                sp.dma_start(unused[:, :], a["unused_places"]).then_inc(unused_loaded, 16)
                x_shared(0)
                x_shared(1)
                sp.dma_start(raw1[:, 0, :], a["moe_w1"][0]).then_inc(s1_got[0], 16)
                sp.dma_start(ids[:, :, :], a["choice_ids"]).then_inc(ids_loaded, 16)
                sp.dma_start(raw2[:, 0, :], a["moe_w2"][0]).then_inc(s2_got[0], 16)
                sp.dma_start(raw1[:, 1, :], a["moe_w1"][0]).then_inc(s1_got[1], 16)
                sp.dma_start(raw2[:, 1, :], a["moe_w2"][0]).then_inc(s2_got[1], 16)
                for g in range(2, SU):
                    x_shared(g)
                sp.wait_ge(scattered, 16 * NT * TOPK)
                sp.dma_start(list_i[:, :], listed.rearrange("(r p) o -> r (p o)", p=P)).then_inc(list_loaded, 16)
                for par in range(2):
                    sp.wait_ge(y_stored[par], 16 * UR * len(range(SU + par, UN, 2)))

                def collect(i, n):
                    t = YW * i + n
                    if not isinstance(i, int):
                        sp.wait_ge(summed, TOPK * (t + (1 - YW)))
                    sp.dma_start(yg[:, n, :, :], yd[t]).then_inc(y_got[n], 16)

                def store(t):
                    sp.wait_ge(summed, TOPK * t + TOPK)
                    sp.dma_start(out_rows[t], acc[:, bass.ds(t, 1), :].rearrange("p a d -> p (a d)"))\
                      .then_inc(out_stored, 16)

                for n in range(YW):
                    collect(0, n)
                with sp.Fori(1, NT // YW) as i:
                    for n in range(YW):
                        collect(i, n)
                        store(YW * i + (n - YW))
                for n in range(YW):
                    store(NT - YW + n)
                sp.wait_ge(out_stored, 16 * NT)

            @block.gpsimd
            def _(pool):
                def gather_w(buf, src, par, got):
                    pool.indirect_dma_start(buf[:, par, :], None, src,
                                            bass.IndirectOffsetOnAxis(w_at[:, par, :], 0)).then_inc(got[par], 16)

                def fetch(g):
                    pool.wait_ge(at_set, 2 * (g.u + 1)).then_inc(pool_passed, 1)
                    pool.wait_ge(x_up, UR * (g.n - 1)).then_inc(pool_passed, 1)
                    for h in range(UR):
                        pool.indirect_dma_start(xr[:, g.par, h, :], None, xn,
                                                bass.IndirectOffsetOnAxis(x_at[:, g.par, h:h + 1], 0))\
                            .then_inc(x_got[g.par][h], 16)
                    pool.wait_ge(w1_lo, g.split - 1).then_inc(pool_passed, 1)
                    gather_w(raw1, w1_rows, g.par, w1_got)
                    pool.wait_ge(w2_lo, g.split - 1).then_inc(pool_passed, 1)
                    gather_w(raw2, w2_rows, g.par, w2_got)

                pool.memset(ones[:, :], 1.0).then_inc(const_set, 1)
                pool.wait_ge(unused_loaded, 16)
                pool.dma_start(listed.rearrange("(r p) o -> r (p o)", p=P), unused[:, :]).then_inc(emptied, 16)
                pool.wait_ge(emptied, 16)
                pool.wait_ge(ids_loaded, 16)
                pool.wait_ge(rt, PLACED)
                for t in range(NT):
                    for k in range(TOPK):
                        pool.indirect_dma_start(listed, bass.IndirectOffsetOnAxis(placei[:, k, t:t + 1], 0),
                                                ids[:, t, k:k + 1], None).then_inc(scattered, 16)

                def slot(g):
                    if (g + 3).exists:
                        fetch(g + 3)
                    pool.wait_ge(y_at_set, g.u + 1).then_inc(pool_passed, 1)
                    for h in range(UR):
                        pool.wait_ge(y_made, UR * g.u + (h + 1)).then_inc(pool_passed, 1)
                        pool.indirect_dma_start(yr, bass.IndirectOffsetOnAxis(y_at[:, g.par, h:h + 1], 0),
                                                y[:, g.par, h, :], None).then_inc(y_stored[g.par], 16)

                for n in range(3):
                    fetch(Unit(0, SU + n))
                slots(pool, slot, SU)

            @block.scalar
            def _(act):
                def w1_first(g):
                    if g.routed:
                        act.wait_ge(w1_got[g.par], 16 * (g.turn + 1))
                        act.wait_ge(first_up, 2 * IC * (g.n - 1))
                    else:
                        act.wait_ge(s1_got[g.par], 16)
                    act.activation(w1h[:, g.par, 0, :], raw1[:, g.par, :], ACT.Copy).then_inc(w1_hi, 1)

                def w2_first(g):
                    if g.routed:
                        act.wait_ge(w2_got[g.par], 16 * (g.turn + 1))
                        act.wait_ge(down_up, UR * (g.n - 1))
                    else:
                        act.wait_ge(s2_got[g.par], 16)
                    act.activation(w2h[:, g.par, 0, :], raw2[:, g.par, :], ACT.Copy).then_inc(w2_hi, 1)

                def x_first(g):
                    if not g.first(2):
                        act.wait_ge(first_up, 2 * IC * (g.n - 1))
                    for h in range(UR):
                        act.wait_ge(x_up, UR * g.n + (h + 1))
                        act.activation(xh[:, g.par, 0, :, h * P:(h + 1) * P],
                                       xps[:, h, :].rearrange("p (k t) -> p k t", k=KC), ACT.Copy).then_inc(x_hi, 1)

                def gated(g):
                    act.wait_ge(first_up, 2 * IC * g.n + IC)
                    if not g.first(1):
                        act.wait_ge(hid_made, g.n)
                    act.activation(gate[:, :, :], gps[:, g.par, 0, :, :], ACT.Silu).then_inc(gate_made, 1)

                def hidden_first(g):
                    act.wait_ge(hid_made, g.n + 1)
                    if not g.first(2):
                        act.wait_ge(down_up, UR * (g.n - 1))
                    act.activation(hh[:, g.par, 0, :, :], hid[:, :, :], ACT.Copy).then_inc(hid_hi, 1)

                def results(g):
                    if not g.first(SU + 2):
                        act.wait_ge(y_stored[g.par], 16 * UR * g.turn)
                    for h in range(UR):
                        act.wait_ge(down_up, UR * g.n + (h + 1))
                        act.activation(y[:, g.par, h, :], dps[:, h, :], ACT.Copy).then_inc(y_made, 1)

                def slot(g):
                    if (g + 1).splits:
                        w2_first(g + 1)
                    if (g + 2).exists and not g.lists:
                        x_first(g + 2)
                        if (g + 2).splits:
                            w1_first(g + 2)
                    if (g + 1).exists:
                        gated(g + 1)
                        hidden_first(g + 1)
                    if g.lists:
                        x_first(g + 2)
                        w1_first(g + 2)
                    if g.routed:
                        results(g)

                x_first(Unit(0, 0))
                w1_first(Unit(0, 0))
                w2_first(Unit(0, 0))
                w1_first(Unit(0, 1))
                x_first(Unit(0, 1))
                gated(Unit(0, 0))
                hidden_first(Unit(0, 0))
                slots(act, slot)

            @block.vector
            def _(dve):
                def w1_rest(g):
                    dve.wait_ge(w1_hi, g.split + 1)
                    dve.tensor_tensor(w1h[:, g.par, 1, :], raw1[:, g.par, :], w1h[:, g.par, 0, :].bitcast(F32),
                                      ALU.subtract).then_inc(w1_lo, 1)

                def w2_rest(g):
                    dve.wait_ge(w2_hi, g.split + 1)
                    dve.tensor_tensor(w2h[:, g.par, 1, :], raw2[:, g.par, :], w2h[:, g.par, 0, :].bitcast(F32),
                                      ALU.subtract).then_inc(w2_lo, 1)

                def x_rest(g):
                    for h in range(UR):
                        part = slice(h * P, (h + 1) * P)
                        dve.wait_ge(x_hi, UR * g.n + (h + 1))
                        dve.tensor_tensor(xh[:, g.par, 1, :, part],
                                          xps[:, h, :].rearrange("p (k t) -> p k t", k=KC),
                                          xh[:, g.par, 0, :, part].bitcast(F32), ALU.subtract).then_inc(x_lo, 1)

                def hidden(g):
                    dve.wait_ge(gate_made, g.n + 1)
                    dve.wait_ge(first_up, 2 * IC * (g.n + 1))
                    if not g.first(1):
                        dve.wait_ge(hid_lo, g.n)
                    dve.tensor_tensor(hid[:, :, :], gate[:, :, :], gps[:, g.par, 1, :, :], ALU.mult)\
                       .then_inc(hid_made, 1)

                def hidden_rest(g):
                    dve.wait_ge(hid_hi, g.n + 1)
                    dve.tensor_tensor(hh[:, g.par, 1, :, :], hid[:, :, :], hh[:, g.par, 0, :, :].bitcast(F32),
                                      ALU.subtract).then_inc(hid_lo, 1)

                def add(g):
                    for h in range(UR):
                        dve.wait_ge(down_up, UR * g.n + h + 1)
                        dve.tensor_tensor(acc[:, UR * g.n + h, :], dps[:, h, :], acc[:, UR * g.n + h, :], ALU.add)\
                           .then_inc(added, 1)

                def set_at(g):
                    if not g.first(SU + 2):
                        for got in (w1_got[g.par], w2_got[g.par], *x_got[g.par]):
                            dve.wait_ge(got, 16 * g.turn)
                    dve.tensor_scalar(w_at[:, g.par, :], w_rows[:, bass.ds(g.u, 1)], 1.0, None, ALU.mult)\
                       .then_inc(at_set, 1)
                    dve.tensor_scalar(x_at[:, g.par, :], listT[:, 0, bass.ds(UR * g.u, UR)], 1.0, None,
                                      ALU.mult).then_inc(at_set, 1)

                def set_y_at(g):
                    if not g.first(SU + 2):
                        dve.wait_ge(y_stored[g.par], 16 * UR * g.turn)
                    dve.tensor_scalar(y_at[:, g.par, :], listT[:, 1, bass.ds(UR * g.u, UR)], 1.0, None,
                                      ALU.mult).then_inc(y_at_set, 1)

                def turned_list():
                    dve.wait_ge(list_loaded, 16)
                    dve.tensor_scalar(token_i[:, :], list_i[:, :], B * S - 1, None, ALU.bitwise_and)\
                       .then_inc(list_made, 1)
                    dve.tensor_scalar(list_f[:, 1, :], list_i[:, :], 1.0, None, ALU.mult).then_inc(list_made, 1)
                    dve.wait_ge(list_made, 2)
                    dve.tensor_scalar(list_f[:, 0, :], token_i[:, :], 1.0, None, ALU.mult).then_inc(list_made, 1)
                    dve.wait_ge(list_up, 1)
                    dve.tensor_scalar(listT[:, :, :], xps[:, :, 0:LR], 1.0, None, ALU.mult).then_inc(list_made, 1)
                    dve.wait_ge(list_made, 4)

                steps = [0]

                def step(op):
                    if steps[0]:
                        dve.wait_ge(rt, steps[0])
                    op().then_inc(rt, 1)
                    steps[0] += 1

                def flat(t):
                    return t[:, :, :].rearrange("p a b -> p (a b)")

                def places():
                    dve.wait_ge(const_loaded, 16)
                    dve.wait_ge(ranks_up, 1)
                    step(lambda: dve.tensor_scalar(flat(tot), xps[:, 1, 0:NE * NT], 1.0, None, ALU.mult))
                    step(lambda: dve.tensor_tensor_scan(flat(incl), same, flat(tot), 0.0, ALU.mult, ALU.add))
                    step(lambda: dve.tensor_tensor(flat(tot), flat(incl), flat(tot), ALU.subtract))
                    step(lambda: dve.tensor_tensor(flat(rank), xps[:, 0, 0:NE * NT], flat(tot), ALU.add))
                    step(lambda: dve.tensor_tensor(over[:, :, :], bcast(incl[:, :, NT - 1:NT], [P, NE, SU]),
                                                   bcast(starts[:, :].rearrange("p (o s) -> p o s", o=1),
                                                         [P, NE, SU]), ALU.is_gt))
                    step(lambda: dve.tensor_reduce(units[:, :], over[:, :, :], AX_X, ALU.add))
                    step(lambda: dve.tensor_tensor_scan(ends[:, :], ones[:, 0:NE], units[:, :], 0.0,
                                                        ALU.mult, ALU.add))
                    step(lambda: dve.tensor_tensor(first[:, :], ends[:, :], units[:, :], ALU.subtract))
                    step(lambda: dve.tensor_scalar(first[:, :], first[:, :], float(UT), None, ALU.mult))
                    step(lambda: dve.tensor_tensor(rank[:, :, :], rank[:, :, :],
                                                   bcast(first[:, :].rearrange("p (e o) -> p e o", o=1),
                                                         [P, NE, NT]), ALU.add))
                    step(lambda: dve.tensor_scalar(turned[:, :, :], mask[:, :, :].rearrange("p e t -> p t e"),
                                                   1.0, None, ALU.mult))
                    step(lambda: dve.tensor_tensor_scan(flat(nth), same, flat(turned), 0.0,
                                                        ALU.mult, ALU.add))
                    step(lambda: dve.tensor_tensor(flat(nth), flat(nth), flat(turned), ALU.mult))
                    for src, dst in ((rank, place), (cw, wk)):
                        for k in range(TOPK):
                            step(lambda: dve.scalar_tensor_tensor(
                                out=pick[:, k, :, :], in0=nth[:, :, :], scalar=float(k + 1),
                                in1=src[:, :, :].rearrange("p e t -> p t e"), op0=ALU.is_equal, op1=ALU.mult))
                        step(lambda: dve.tensor_reduce(dst[:, :, :], pick[:, :, :, :], AX_X, ALU.add))
                        if dst is place:
                            step(lambda: dve.tensor_scalar(placei[:, :, :], place[:, :, :], 1.0, None, ALU.mult))
                            assert steps[0] == PLACED
                    step(lambda: dve.tensor_tensor(past[:, :, :],
                                                   bcast(unit_no[:, :].rearrange("p (u o) -> p u o", o=1),
                                                         [P, RU, NE - 1]),
                                                   bcast(ends[:, 0:NE - 1].rearrange("p (o e) -> p o e", o=1),
                                                         [P, RU, NE - 1]), ALU.is_ge))
                    step(lambda: dve.tensor_reduce(unit_e[:, :], past[:, :, :], AX_X, ALU.add))
                    step(lambda: dve.tensor_scalar(w_rows[:, :], unit_e[:, :], float(P), expert_row[:, 0:1],
                                                   ALU.mult, ALU.add))
                    dve.wait_ge(rt, steps[0])

                def slot(g):
                    if (g + 1).splits:
                        w2_rest(g + 1)
                    if (g + 2).exists and not g.lists:
                        x_rest(g + 2)
                        if (g + 2).splits:
                            w1_rest(g + 2)
                    if (g + 4).exists and not (g + 4).first(SU + 3):
                        set_at(g + 4)
                    if (g + 1).exists:
                        hidden(g + 1)
                        hidden_rest(g + 1)
                    if g.routed and (g + 1).exists:
                        set_y_at(g + 1)
                    if g.lists:
                        turned_list()
                        set_at(g + 2)
                        set_at(g + 3)
                    if not g.routed:
                        add(g)
                    if g.lists:
                        x_rest(g + 2)
                        w1_rest(g + 2)
                        set_at(g + 4)
                        set_y_at(g + 2)

                def total(i, n, first=False):
                    t = YW * i + n
                    row = acc[:, bass.ds(t, 1), :].rearrange("p a d -> p (a d)")
                    dve.wait_ge(y_got[n], 16 * (i + 1))
                    for k in range(TOPK):
                        if not (first and n == 0 and k == 0):
                            dve.wait_ge(summed, TOPK * t + k)
                        dve.scalar_tensor_tensor(out=row, in0=yg[:, n, k, :], scalar=wk[:, k, bass.ds(t, 1)],
                                                 in1=row, op0=ALU.mult, op1=ALU.add).then_inc(summed, 1)

                dve.wait_ge(const_set, 1)
                places()
                x_rest(Unit(0, 0))
                w1_rest(Unit(0, 0))
                w2_rest(Unit(0, 0))
                w1_rest(Unit(0, 1))
                x_rest(Unit(0, 1))
                hidden(Unit(0, 0))
                hidden_rest(Unit(0, 0))
                slots(dve, slot)
                dve.wait_ge(added, UR * SU)
                for n in range(YW):
                    total(0, n, first=True)
                with dve.Fori(1, NT // YW) as i:
                    for n in range(YW):
                        total(i, n)

            @block.tensor
            def _(pe):
                def turn(g):
                    for h in range(UR):
                        if g.routed:
                            pe.wait_ge(x_got[g.par][h], 16 * (g.turn + 1))
                        else:
                            pe.wait_ge(sx_got[g.par], 16 * (g.c // 2 + 1))
                        if not g.first(1):
                            pe.wait_ge(x_lo, UR * (g.n - 1) + (h + 1))
                        for k in range(KC):
                            last = pe.transpose(xps[:, h, k * P:(k + 1) * P], xr[:, g.par, h, k * P:(k + 1) * P],
                                                ident[:, :])
                        last.then_inc(x_up, 1)

                def first_layer(g):
                    pe.wait_ge(x_lo, UR * (g.n + 1))
                    if g.splits:
                        pe.wait_ge(w1_lo, g.split + 1)
                    if not g.first(2):
                        pe.wait_ge(hid_made, g.n - 1)
                    for part in range(2):
                        for c in range(IC):
                            for m, (i, j) in enumerate(PASSES):
                                for k in range(KC):
                                    w = (part * KC + k) * I + c * P
                                    last = pe.matmul(gps[:, g.par, part, c, :], w1h[:, g.par, i, w:w + P],
                                                     xh[:, g.par, j, k, :],
                                                     start=(m == 0 and k == 0), stop=(m == 2 and k == KC - 1))
                            last.then_inc(first_up, 1)

                def down(g):
                    pe.wait_ge(hid_lo, g.n + 1)
                    if g.splits:
                        pe.wait_ge(w2_lo, g.split + 1)
                    for h in range(UR):
                        if (g + -1).routed:
                            pe.wait_ge(y_made, UR * (g + -1).u + (h + 1))
                        elif not g.first(1):
                            pe.wait_ge(added, UR * (g.n - 1) + (h + 1))
                        for m, (i, j) in enumerate(PASSES):
                            for c in range(IC):
                                last = pe.matmul(dps[:, h, :], hh[:, g.par, i, c, h * P:(h + 1) * P],
                                                 w2h[:, g.par, j, c * D:(c + 1) * D],
                                                 start=(m == 0 and c == 0), stop=(m == 2 and c == IC - 1))
                        last.then_inc(down_up, 1)

                def slot(g):
                    if (g + 2).exists and not g.lists:
                        turn(g + 2)
                    if (g + 1).exists:
                        first_layer(g + 1)
                    if g.lists:
                        pe.wait_ge(list_made, 3)
                        pe.wait_ge(x_lo, UR * SU)
                        for n in range(2):
                            last = pe.transpose(xps[:, n, 0:LR], list_f[:, n, :], ident[0:LR, 0:LR])
                        last.then_inc(list_up, 1)
                    down(g)
                    if g.lists:
                        pe.wait_ge(list_made, 4)
                        turn(g + 2)

                pe.wait_ge(const_loaded, 16)
                pe.wait_ge(const_set, 1)
                for b, m in enumerate((before, ones[:, :])):
                    last = pe.matmul(xps[:, b, 0:NE * NT], m, mask[:, :, :].rearrange("p e t -> p (e t)"),
                                     start=True, stop=True)
                last.then_inc(ranks_up, 1)
                pe.wait_ge(rt, 4)
                turn(Unit(0, 0))
                turn(Unit(0, 1))
                first_layer(Unit(0, 0))
                slots(pe, slot)


def build(nc, a, out):
    def dram(name, shape, dt=F32):
        return nc.dram_tensor(name, shape, dt, kind="Internal").ap()

    xn = dram("xn_rows", (B * S, D))
    listed = dram("listed_tokens", (RU * UT, 1), I32)
    yr = dram("expert_rows", (TOPK * B * S + RU * UT, D))
    with ExitStack() as ctx:
        acc = ctx.enter_context(nc.sbuf_tensor("acc", [P, NT, D], F32))
        ident = ctx.enter_context(nc.sbuf_tensor("identity", [P, P], F32))
        attention_phase(nc, a, acc, ident)
        cw = ctx.enter_context(nc.sbuf_tensor("expert_weights", [P, NE, NT], F32))
        mask = ctx.enter_context(nc.sbuf_tensor("expert_mask", [P, NE, NT], F32))
        with ExitStack() as inner:
            cols = inner.enter_context(nc.sbuf_tensor("cols_halves", [P, 2, KC, B * S], F32R))
            ffn_wkv_phase(nc, a, acc, ident, cols, cw, mask, xn)
        moe_phase(nc, a, acc, ident, cw, mask, xn, listed, yr, out)


def attention_constants():
    angle = (1.0 / 10000.0 ** np.linspace(0.0, 1.0, DH // 2, dtype=np.float32)).astype(np.float32)
    phase = np.arange(S, dtype=np.float32)[:, None] * np.repeat(angle, 2)[None, :]
    sign = np.where(np.arange(DH) % 2 == 0, -1.0, 1.0).astype(np.float32)
    rows = lambda t: np.ascontiguousarray(t.reshape(ST, P, -1).transpose(1, 0, 2).astype(np.float32))
    decay = np.log(1.0 - 2.0 ** (-5.0 - np.arange(H)))
    i, t = np.arange(S)[:, None], np.arange(S)[None, :]
    m = np.where(i >= t, np.exp(np.where(i >= t, i - t, 0)[None] * decay[:, None, None]), 0.0)
    inv = 1.0 / np.sqrt(m.sum(-1))
    mt = m.transpose(2, 0, 1)[:P].reshape(P, H, 2, P) * DH ** -0.5
    return {"cos": rows(np.cos(phase)), "sin": rows(np.sin(phase) * sign),
            "inv_norm": rows(inv.T), "mask": np.ascontiguousarray(mt.astype(np.float32)),
            "ident": np.eye(P, dtype=np.float32)}


def routing_constants():
    rows = lambda v: np.broadcast_to(np.asarray(v, dtype=np.float32).reshape(1, -1), (P, np.size(v)))
    same = np.arange(NE * NT) % NT != 0
    assert NE == NT
    before = np.triu(np.ones((P, P), np.float32), 1)
    row = P + np.arange(P, dtype=np.float32).reshape(P, 1)
    return {"routing": np.concatenate([before, rows(same), rows(UT * np.arange(SU)), rows(np.arange(RU)), row], 1),
            "choice_ids": (P * np.arange(NT)[None, :, None] + np.arange(P)[:, None, None]
                           + B * S * np.arange(TOPK)[None, None, :]).astype(np.int32),
            "unused_places": (TOPK * B * S + np.arange(RU * UT)).astype(np.int32).reshape(LR, P)}


def kernel(**inputs):
    from concourse import bacc
    from concourse.bass_utils import run_bass_kernel_spmd

    x = {n: np.asarray(v) for n, v in inputs.items()}
    arrays = layouts(x)
    nc = bacc.Bacc("TRN2", target_bir_lowering=False, num_devices=1)
    aps = {n: nc.dram_tensor(n, v.shape, mybir.dt.from_np(v.dtype), kind="ExternalInput").ap()
           for n, v in arrays.items()}
    out = nc.dram_tensor("out", (B * S, D), F32, kind="ExternalOutput").ap()
    build(nc, aps, out)
    r = run_bass_kernel_spmd(nc, [arrays], core_ids=[0])
    return r.results[0]["out"].reshape(B, S, D)


def layouts(x):
    def chunks(w):
        return w.reshape(-1, P, w.shape[-1]).transpose(1, 0, 2)

    arrays = dict(attention_constants())
    arrays["x"] = x["x"].reshape(B * S, D)
    arrays["attn_w"] = np.stack([chunks(x[f"L0_attn_{n}_w"]) for n in ("q", "k", "v", "g", "out")])
    arrays["retn_w"] = x["L0_attn_retn_norm_w"].reshape(KC, P).T
    arrays["final_w"] = x["L0_attn_final_norm_w"].reshape(1, D)

    def joined(*parts):
        return np.concatenate([p.reshape(p.shape[0], P, -1) for p in parts], axis=2)

    def slice_chunks(w):
        return w.reshape(w.shape[0], -1, P, w.shape[-1]).transpose(0, 2, 1, 3)

    fc1 = x["L0_attn_fc1_w"].reshape(D, F // I, I).transpose(1, 0, 2)
    fc2 = x["L0_attn_fc2_w"].reshape(F // I, I, D)
    arrays["ffn_w"] = joined(slice_chunks(fc1), slice_chunks(fc2))
    arrays["fc1_b"] = x["L0_attn_fc1_b"].reshape(F // P, P).T
    arrays["fc2_b"] = x["L0_attn_fc2_b"].reshape(1, D)
    experts = [np.concatenate([x[f"L0_ffn_sw_{n}"][None], x[f"L0_ffn_w_{n}"]]) for n in ("gate", "up", "down")]
    gate, up, down = (slice_chunks(w.transpose(0, 2, 1)) for w in experts)
    arrays["moe_w1"] = joined(gate, up)
    arrays["moe_w2"] = joined(down)
    arrays.update(routing_constants())
    arrays["ctx"] = x["ctx_2048"].reshape(B, S, KC, P).transpose(0, 3, 2, 1)
    arrays["time_decay"] = x["L0_xattn_time_decay"].reshape(KC, P).T
    arrays["time_first"] = x["L0_xattn_time_first"].reshape(KC, P).T
    arrays["gate_w"] = chunks(x["L0_ffn_gate_w"].T)
    arrays["expert_bias"] = x["L0_ffn_expert_bias"].reshape(1, NE)
    return {n: np.ascontiguousarray(v) for n, v in arrays.items()}
```
